# Optimizing a Trainium2 kernel written in Bass

```python
import numpy as np
import jax
import jax.numpy as jnp

def _softmax(x, axis=-1):
    return jax.nn.softmax(x, axis=axis)

def _gelu(x):
    return jax.nn.gelu(x, approximate=True)

def _silu(x):
    return jax.nn.silu(x)

def _sigmoid(x):
    return jax.nn.sigmoid(x)

def _layernorm(x, axis=-1, eps=1e-05):
    m = jnp.mean(x, axis=axis, keepdims=True)
    v = jnp.var(x, axis=axis, keepdims=True)
    return (x - m) / jnp.sqrt(v + eps)

def _scatter_add(tgt, idx, src, axis=0):
    return tgt.at[idx].add(src)

def _segment_sum(src, seg, n):
    return jax.ops.segment_sum(src, seg, n)
kernel_name = 'mk_gnn_preln_d4_gnn_r8_87a4b0'

def setup_inputs(seed: int=0):
    np.random.seed(seed)
    _w = jnp.asarray

    def _rec_inputs():
        import jax
        import jax.numpy as jnp
        _gk = jax.random.key(seed)
        x = -0.000202 + 1 * jax.random.normal(jax.random.fold_in(_gk, 1), (12500, 64), jnp.float32)
        _s = jax.random.randint(jax.random.fold_in(_gk, 2), (100000,), 0, 12500, jnp.int32)
        _d = jax.random.randint(jax.random.fold_in(_gk, 3), (100000,), 0, 12500, jnp.int32)
        _loop = jnp.arange(12500, dtype=jnp.int32)
        src = jnp.concatenate([_s, _d, _loop])
        dst = jnp.concatenate([_d, _s, _loop])
        _o = jnp.argsort(dst, stable=True)
        src = src[_o]
        dst = dst[_o]
        edge_attr_32 = -5.16925e-05 + 1.00005 * jax.random.normal(jax.random.fold_in(_gk, 12), (212500, 32), jnp.float32)
        edge_weight = jax.random.uniform(jax.random.fold_in(_gk, 14), (212500,), jnp.float32, 0.0, 0.999999)
        node_vec1 = 0.0014194 + 1.00024 * jax.random.normal(jax.random.fold_in(_gk, 15), (12500, 1), jnp.float32)
        return (x, src, dst, edge_attr_32, edge_weight, node_vec1)
    x, src, dst, edge_attr_32, edge_weight, node_vec1 = _rec_inputs()

    def _L0_gnn_setup():
        import jax, jax.numpy as jnp
        import numpy as np
        N_NODES = 12500
        N_EDGES = 200000
        IN_CH = 64
        OUT_CH = 64
        key = jax.random.key(seed)
        ks = jax.random.split(key, 8)
        x = jax.random.normal(ks[0], (N_NODES, IN_CH), dtype=jnp.float32)
        edge_index = jax.random.randint(ks[1], (2, N_EDGES), 0, N_NODES, dtype=jnp.int64)
        edge_weight = jax.random.uniform(ks[2], (N_EDGES,), dtype=jnp.float32)
        s1 = 1.0 / np.sqrt(IN_CH)
        s2 = 1.0 / np.sqrt(2 * IN_CH)
        pool_w = jax.random.uniform(ks[3], (IN_CH, IN_CH), minval=-s1, maxval=s1, dtype=jnp.float32)
        pool_b = jax.random.uniform(ks[4], (IN_CH,), minval=-s1, maxval=s1, dtype=jnp.float32)
        final_w = jax.random.uniform(ks[5], (OUT_CH, 2 * IN_CH), minval=-s2, maxval=s2, dtype=jnp.float32)
        final_b = jax.random.uniform(ks[6], (OUT_CH,), minval=-s2, maxval=s2, dtype=jnp.float32)
        coef = jnp.float32(0.5)
        return {'x': x, 'edge_index': edge_index, 'edge_weight': edge_weight, 'pool_w': pool_w, 'pool_b': pool_b, 'final_w': final_w, 'final_b': final_b, 'coef': coef}
    _L0_gnn_all = _L0_gnn_setup()
    _L0_gnn_in = {k: v for k, v in _L0_gnn_all.items() if k in ('pool_w', 'pool_b', 'final_w', 'final_b', 'coef')}
    del _L0_gnn_all

    def _L1_gnn_setup():
        import jax, jax.numpy as jnp
        import numpy as np
        N = 12500
        E = 200000
        D = 64
        L = 4
        EPS = 1e-05
        key = jax.random.key(seed)
        k = jax.random.split(key, 4)
        x = jax.random.normal(k[0], (N, D), dtype=jnp.float32)
        edge_index = jax.random.randint(k[1], (2, E), 0, N, dtype=jnp.int32)
        Ws = jax.random.normal(k[2], (L, D, D), dtype=jnp.float32) * (1.0 / np.sqrt(D))
        bs = jnp.zeros((L, D), dtype=jnp.float32)
        ln_w = jnp.ones((L, D), dtype=jnp.float32)
        ln_b = jnp.zeros((L, D), dtype=jnp.float32)
        return {'x': x, 'edge_index': edge_index, 'Ws': Ws, 'bs': bs, 'ln_w': ln_w, 'ln_b': ln_b}
    _L1_gnn_all = _L1_gnn_setup()
    _L1_gnn_in = {k: v for k, v in _L1_gnn_all.items() if k in ('Ws', 'bs', 'ln_w', 'ln_b')}
    del _L1_gnn_all

    def _L2_gnn_setup():
        import jax, jax.numpy as jnp
        import numpy as np
        N = 6250
        E = 200000
        IN_DIM = 64
        OUT_DIM = 64
        key = jax.random.key(seed)
        ks = jax.random.split(key, 8)
        mu = jax.random.normal(ks[0], (N, IN_DIM), dtype=jnp.float32)
        x = jax.random.normal(ks[1], (N, 1), dtype=jnp.float32)
        edge_index = jax.random.randint(ks[2], (2, E), 0, N, dtype=jnp.int64)
        edge_w = jax.random.uniform(ks[3], (E,), dtype=jnp.float32)
        W1 = jax.random.normal(ks[4], (OUT_DIM, 1), dtype=jnp.float32) * (1.0 / 1.0)
        W2 = jax.random.normal(ks[5], (OUT_DIM, 1), dtype=jnp.float32) * (1.0 / 1.0)
        W3 = jax.random.normal(ks[6], (OUT_DIM, IN_DIM), dtype=jnp.float32) * (1.0 / np.sqrt(IN_DIM))
        W4 = jax.random.normal(ks[7], (OUT_DIM, 3 * OUT_DIM), dtype=jnp.float32) * (1.0 / np.sqrt(3 * OUT_DIM))
        return {'mu': mu, 'x': x, 'edge_index': edge_index, 'edge_w': edge_w, 'W1': W1, 'W2': W2, 'W3': W3, 'W4': W4}
    _L2_gnn_all = _L2_gnn_setup()
    _L2_gnn_in = {k: v for k, v in _L2_gnn_all.items() if k in ('W1', 'W2', 'W3', 'W4')}
    del _L2_gnn_all

    def _L3_gnn_setup():
        import jax, jax.numpy as jnp
        import numpy as np
        N_NODES = 12500
        N_EDGES = 400000
        EDGE_OUT = 32
        HID = 128
        NODE_OUT = 64
        N_GRAPHS = 16
        key = jax.random.key(seed)
        ks = jax.random.split(key, 9)
        x = jax.random.normal(ks[0], (N_NODES, 64), dtype=jnp.float32)
        edge_index = jax.random.randint(ks[1], (2, N_EDGES), 0, N_NODES, dtype=jnp.int64)
        edge_attr = jax.random.normal(ks[2], (N_EDGES, EDGE_OUT), dtype=jnp.float32)
        u = jax.random.normal(ks[3], (N_GRAPHS, 1), dtype=jnp.float32)
        batch = jnp.sort(jax.random.randint(ks[4], (N_NODES,), 0, N_GRAPHS, dtype=jnp.int64))
        d_in = 3 * EDGE_OUT + 1
        W1 = jax.random.normal(ks[5], (d_in, HID), dtype=jnp.float32) / np.sqrt(d_in)
        b1 = jnp.zeros((HID,), dtype=jnp.float32)
        W2 = jax.random.normal(ks[6], (HID, NODE_OUT), dtype=jnp.float32) / np.sqrt(HID)
        b2 = jnp.zeros((NODE_OUT,), dtype=jnp.float32)
        return {'x': x, 'edge_index': edge_index, 'edge_attr': edge_attr, 'u': u, 'batch': batch, 'W1': W1, 'b1': b1, 'W2': W2, 'b2': b2}
    _L3_gnn_all = _L3_gnn_setup()
    _L3_gnn_in = {k: v for k, v in _L3_gnn_all.items() if k in ('u', 'W1', 'b1', 'W2', 'b2')}
    del _L3_gnn_all
    return {'x': x, 'src': src, 'dst': dst, 'edge_attr_32': edge_attr_32, 'edge_weight': edge_weight, 'node_vec1': node_vec1, 'L0_gnn_pool_w': _L0_gnn_in['pool_w'], 'L0_gnn_pool_b': _L0_gnn_in['pool_b'], 'L0_gnn_final_w': _L0_gnn_in['final_w'], 'L0_gnn_final_b': _L0_gnn_in['final_b'], 'L0_gnn_coef': _L0_gnn_in['coef'], 'L1_gnn_Ws': _L1_gnn_in['Ws'], 'L1_gnn_bs': _L1_gnn_in['bs'], 'L1_gnn_ln_w': _L1_gnn_in['ln_w'], 'L1_gnn_ln_b': _L1_gnn_in['ln_b'], 'L2_gnn_W1': _L2_gnn_in['W1'], 'L2_gnn_W2': _L2_gnn_in['W2'], 'L2_gnn_W3': _L2_gnn_in['W3'], 'L2_gnn_W4': _L2_gnn_in['W4'], 'L3_gnn_u': _L3_gnn_in['u'], 'L3_gnn_W1': _L3_gnn_in['W1'], 'L3_gnn_b1': _L3_gnn_in['b1'], 'L3_gnn_W2': _L3_gnn_in['W2'], 'L3_gnn_b2': _L3_gnn_in['b2']}

def reference(x, src, dst, edge_attr_32, edge_weight, node_vec1, L0_gnn_pool_w, L0_gnn_pool_b, L0_gnn_final_w, L0_gnn_final_b, L0_gnn_coef, L1_gnn_Ws, L1_gnn_bs, L1_gnn_ln_w, L1_gnn_ln_b, L2_gnn_W1, L2_gnn_W2, L2_gnn_W3, L2_gnn_W4, L3_gnn_u, L3_gnn_W1, L3_gnn_b1, L3_gnn_W2, L3_gnn_b2):
    import jax
    import jax.numpy as jnp

    def _L0_gnn_ref(x, edge_index, edge_weight, pool_w, pool_b, final_w, final_b, coef):
        import jax, jax.numpy as jnp
        import numpy as np
        N_NODES = 12500
        N_EDGES = 200000
        IN_CH = 64
        OUT_CH = 64
        src, dst = (edge_index[0], edge_index[1])
        all_src = jnp.concatenate([src, dst], axis=0)
        all_dst = jnp.concatenate([dst, src], axis=0)
        mask = all_src != all_dst
        neighbors = jnp.concatenate([x[src], x[dst]], axis=0)
        ew = jnp.concatenate([edge_weight, edge_weight], axis=0)
        edge_features = neighbors * (1.0 + coef * ew[:, None])
        pooled = jax.nn.relu(edge_features @ pool_w.T + pool_b)
        pooled = jnp.where(mask[:, None], pooled, -jnp.inf)
        agg = jax.ops.segment_max(pooled, all_dst, num_segments=x.shape[0])
        agg = jnp.maximum(agg, 0.0)
        h = jnp.concatenate([x, agg], axis=-1)
        return jax.nn.relu(h @ final_w.T + final_b)

    def _L1_gnn_ref(x, edge_index, Ws, bs, ln_w, ln_b):
        import jax, jax.numpy as jnp
        import numpy as np
        N = 12500
        E = 200000
        D = 64
        L = 4
        EPS = 1e-05
        src, dst = (edge_index[0], edge_index[1])
        n = x.shape[0]
        deg = jnp.zeros((n,), x.dtype).at[dst].add(1.0) + 1.0
        dinv = jax.lax.rsqrt(deg)
        enorm = (dinv[src] * dinv[dst])[:, None]
        self_norm = (dinv * dinv)[:, None]
        h = x
        for l in range(Ws.shape[0]):
            hw = h @ Ws[l]
            agg = jnp.zeros_like(hw).at[dst].add(enorm * hw[src])
            agg = agg + self_norm * hw + bs[l]
            mean = jnp.mean(agg)
            var = jnp.mean(jnp.square(agg - mean))
            hn = ln_w[l] * (agg - mean) * jax.lax.rsqrt(var + EPS) + ln_b[l]
            h = jax.nn.relu(hn)
        return h

    def _L2_gnn_ref(mu, x, edge_index, edge_w, W1, W2, W3, W4):
        import jax, jax.numpy as jnp
        import numpy as np
        N = 6250
        E = 200000
        IN_DIM = 64
        OUT_DIM = 64
        relu = jax.nn.relu
        n_nodes = mu.shape[0]
        h_x = relu(x @ W1.T)
        h_e = relu(edge_w[:, None] @ W2.T)
        h_mu = relu(mu @ W3.T)
        dst = edge_index[1]
        src = edge_index[0]
        cat_feat = jnp.concatenate([h_x[dst], h_e, h_mu[dst]], axis=1)
        agg = jax.ops.segment_sum(cat_feat, src, num_segments=n_nodes)
        agg = relu(agg @ W4.T)
        return relu(h_x + h_mu + agg)

    def _L3_gnn_ref(x, edge_index, edge_attr, u, batch, W1, b1, W2, b2):
        import jax, jax.numpy as jnp
        import numpy as np
        N_NODES = 12500
        N_EDGES = 400000
        EDGE_OUT = 32
        HID = 128
        NODE_OUT = 64
        N_GRAPHS = 16
        N = x.shape[0]
        row = edge_index[0]
        seg_sum = jax.ops.segment_sum(edge_attr, row, num_segments=N)
        seg_max = jax.ops.segment_max(edge_attr, row, num_segments=N)
        cnt = jax.ops.segment_sum(jnp.ones((edge_attr.shape[0], 1), edge_attr.dtype), row, num_segments=N)
        seg_mean = seg_sum / jnp.maximum(cnt, 1.0)
        seg_max = jnp.where(cnt > 0, seg_max, 0.0)
        h = jnp.concatenate([seg_sum, seg_max, seg_mean, u[batch]], axis=1)
        h = jax.nn.relu(h @ W1 + b1)
        return h @ W2 + b2
    edge_index = jnp.stack([src, dst])
    batch0 = jnp.zeros((12500,), jnp.int32)
    h = jnp.maximum(_layernorm(x, axis=-1), 0.0)
    x = x + _L0_gnn_ref(h, edge_index, edge_weight, L0_gnn_pool_w, L0_gnn_pool_b, L0_gnn_final_w, L0_gnn_final_b, L0_gnn_coef)
    h = jnp.maximum(_layernorm(x, axis=-1), 0.0)
    x = x + _L1_gnn_ref(h, edge_index, L1_gnn_Ws, L1_gnn_bs, L1_gnn_ln_w, L1_gnn_ln_b)
    h = jnp.maximum(_layernorm(x, axis=-1), 0.0)
    x = x + _L2_gnn_ref(h, node_vec1, edge_index, edge_weight, L2_gnn_W1, L2_gnn_W2, L2_gnn_W3, L2_gnn_W4)
    h = jnp.maximum(_layernorm(x, axis=-1), 0.0)
    x = x + _L3_gnn_ref(h, edge_index, edge_attr_32, L3_gnn_u, batch0, L3_gnn_W1, L3_gnn_b1, L3_gnn_W2, L3_gnn_b2)
    return x

_drawn_inputs = setup_inputs


def setup_inputs(seed=0):
    import zlib

    import numpy as np

    out = dict(_drawn_inputs(seed))
    spreads = {'L1_gnn_bs': (0.0, 0.1),
     'L1_gnn_ln_w': (1.0, 0.2),
     'L1_gnn_ln_b': (0.0, 0.1),
     'L3_gnn_b1': (0.0, 0.746),
     'L3_gnn_b2': (0.0, 0.542)}
    factors = {'L0_gnn_pool_b': 5.498, 'L0_gnn_final_b': 2.762, 'L3_gnn_u': 7.386}
    for name, (base, spread) in spreads.items():
        noise = np.random.default_rng([zlib.crc32(name.encode()), seed]).standard_normal(out[name].shape)
        drawn = base * np.exp(spread * noise) if base else spread * noise
        out[name] = jnp.asarray(drawn.astype(out[name].dtype))
    for name, factor in factors.items():
        out[name] = (out[name] * factor).astype(out[name].dtype)
    return out
```

```python
import concourse.bass as bass
from concourse import mybir
from contextlib import ExitStack

F32 = mybir.dt.float32
BF16 = mybir.dt.bfloat16
I32 = mybir.dt.int32
ALU = mybir.AluOpType
ACT = mybir.ActivationFunctionType
AX = mybir.AxisListType
D = 64
AD = 32
P = 128
GT = 7
KC = 4
CE = KC * P
RW = D + AD + 4
C_DST, C_WP, C_WN, C_SRC = 96, 97, 98, 99
D0 = RW - D
BIG = 3.4028234e38
SELF = 1e33
EPS = 1e-5
LAYERS = 4


def sizes(n_nodes, n_edges):
    nj = -(-n_nodes // (P * GT * 2)) * GT * 2
    tiles = -(-n_edges // (P * KC * 8)) * KC * 8
    return nj, tiles


def positive(value):
    return not isinstance(value, int) or value > 0


def gnn_kernel(nc, n_nodes, n_edges, a, out):
    NJ, TILES = sizes(n_nodes, n_edges)
    NP = NJ * P
    EP = TILES * P
    H = EP // 2
    NCH = TILES // (2 * KC)
    NIT = NCH // 4
    NG = NJ // GT
    GW = GT * D
    assert NP > n_nodes or EP == n_edges
    assert NJ <= P and NIT >= 2

    def dram(name, shape, dt):
        return nc.dram_tensor(name, shape, dt, kind="Internal").ap()

    table = dram("node_table", (NP, D), F32)
    fill = dram("fill_rows", (H, 2 * D), F32)
    rec = dram("records", (EP, RW), F32)
    runs = dram("runs", (H, 2 * D), F32)
    runs_l0 = dram("runs_l0", (H, 2 * D), F32)
    runs_e = dram("runs_e", (H, 4 * D), F32)
    same_dst = dram("same_dst", (2, H), BF16)
    same_src = dram("same_src", (2, H), BF16)
    dst_by_src = dram("dst_by_src", (P, TILES), I32)
    counts = dram("counts", (2, NP), F32)
    starts = dram("starts", (2, NP), F32)

    ctx = ExitStack()
    with ctx:
        def sb(name, shape, dt=F32):
            return ctx.enter_context(nc.sbuf_tensor(name, shape, dt))

        sems = {}

        def sem(name):
            if name not in sems:
                sems[name] = ctx.enter_context(nc.semaphore(name))
            return sems[name]

        X = sb("X", [P, NJ * D])
        Hn = sb("Hn", [P, NJ * D])
        T = sb("T", [P, NJ * D])
        AGB = sb("AG", [P, max(NJ * D, 3 * GT * P + 768, 3 * TILES + 8)])
        AG = AGB[:, 0:NJ * D]
        EA = sb("EA", [P, max(4 * TILES, NJ * D, 13 * CE + 8)])

        def v3(t, j0=0, n=NJ):
            return t[:, j0 * D:(j0 + n) * D].rearrange("p (j d) -> p j d", d=D)

        def group(t, g):
            return t[:, bass.ds(g * GW, GW)].rearrange("p (j d) -> p j d", d=D)

        s_q = EA[:, 0:TILES]
        pen_q = EA[:, TILES:2 * TILES]
        w_q = EA[:, 2 * TILES:3 * TILES]
        srcf_q = EA[:, 3 * TILES:4 * TILES]
        KEYS = AGB[:, 0:2 * (TILES + KC)].bitcast(BF16).rearrange("p (i t) -> p i t", i=4)
        dstf_q = AGB[:, 2 * (TILES + KC):2 * (TILES + KC) + TILES]
        SI = T[:, 0:TILES].bitcast(I32)
        DI = T[:, TILES:2 * TILES].bitcast(I32)
        tmp_i = dstf_q.bitcast(I32)

        G = sb("G", [P, 4, KC * P])
        M = sb("M", [P, 2, 2 * CE], BF16)
        L = sb("L", [P, 2, CE])
        S = sb("S", [P, 2, CE])
        R = sb("R", [P, 4, CE])
        RT = sb("RT", [P, 4, 8, RW])
        RTf = RT[:, :, :, :].rearrange("p s q r -> p (s q r)")
        Gs = RTf[:, 0:2 * CE].rearrange("p (s e) -> p s e", s=2)
        RD = RT[:, :, :, :].rearrange("p s q r -> p s (q r)")[:, :, 0:CE]
        IDX = sb("IDX", [P, 4, 8], I32)
        OH = sb("OH", [P, 2, 4, KC, P], BF16)
        OHTs = R[:, 0:2, :]
        Cs = R[:, 2, 0:2 * P].rearrange("p (s l) -> p s l", s=2)
        Lf = L[:, :, :].rearrange("p s e -> p (s e)")
        junk_rank = Lf.rearrange("p (x k e) -> p x k e", x=2, k=KC)
        Gf = G[:, :, :].rearrange("p s e -> p (s e)")
        Rf = R[:, :, :].rearrange("p s e -> p (s e)")
        DX = Gf[:, 0:TILES + 1].bitcast(I32)
        MD = Rf[:, 0:TILES // 2].bitcast(BF16)
        assert TILES < 4 * CE
        inr = sb("inr", [P, 2, 2, KC])
        lku = sb("lku", [P, 2, KC])
        off = [0]

        def ea(cols):
            o = off[0]
            off[0] += cols
            return EA[:, o:o + cols]
        KS = [ea(CE + 4) for _ in range(2)]
        MK = [ea(CE // 2).bitcast(BF16) for _ in range(2)]
        MP = [ea(CE) for _ in range(2)]
        S2 = [ea(CE) for _ in range(2)]
        S3 = [ea(CE) for _ in range(2)]
        R2 = [ea(2 * CE) for _ in range(2)]
        L3O = EA[:, 0:NJ * D]
        Z = sb("Z", [P, 2, GT * P])
        junk_look = Z[:, :, :].rearrange("p a b -> p (a b)")[:, 0:8 * P].rearrange("p (x k e) -> p x k e", x=2, k=KC)
        ZTs = Gf[:, 0:GT * P]
        DG = [AGB[:, i * GT * P:(i + 1) * GT * P] for i in range(2)]
        HS = AGB[:, 2 * GT * P:3 * GT * P]
        t1 = AGB[:, 3 * GT * P:3 * GT * P + GT * 36]
        t2 = AGB[:, 3 * GT * P + 256:3 * GT * P + 256 + GT * 36]
        t3 = AGB[:, 3 * GT * P + 512:3 * GT * P + 512 + GT * 32]
        CARG = L[:, 0, 0:GW]
        CR = sb("CR", [P, 2 * D])
        CR2 = sb("CR2", [P, D])

        def node(name, dt=F32):
            return sb(name, [P, NJ], dt)

        cnt = [node("cnt_dst"), node("cnt_src")]
        beg = [node("beg_dst"), node("beg_src")]
        has = [node("has_dst"), node("has_src")]
        span = [node("span_dst"), node("span_src")]
        endrow = [node("endrow_dst", I32), node("endrow_src", I32)]
        begrow = node("begrow", I32)
        dinv = node("dinv")
        rcnt = node("rcnt")
        pen2 = node("pen2")
        valid = node("valid")
        vpos = node("vpos")
        vneg = node("vneg")
        vin = node("vin")
        wsum = sb("wsum", [P, NJ, 2])
        na = node("na")
        nb = node("nb")
        nd = node("nd")
        gsum = sb("gsum", [P, NG])
        st = sb("st", [P, 8])
        iota_i = sb("iota_i", [P, P], I32)
        pidx_i = sb("pidx_i", [P, 1], I32)
        iota_f = sb("iota_f", [P, P])
        iota_b = sb("iota_b", [P, P], BF16)
        pidx = sb("pidx", [P, 1])
        ident = sb("ident", [P, P])
        ident_b = sb("ident_b", [P, P], BF16)
        earlier = sb("earlier", [P, P])
        below = sb("below", [P, P])
        ones = sb("ones", [P, P])
        zero_rows = Z[:, :, :].rearrange("p a b -> p (a b)")
        HC = sb("HC", [P, 4, P])
        hoff = sb("hoff", [P, 2])
        dh = sb("dh", [1, 1], I32)
        poolw = sb("poolw", [D, D])
        finalw = sb("finalw", [2 * D, D])
        w3 = sb("w3", [D, D])
        w4 = sb("w4", [D, 3, D])
        w4c = sb("w4c", [D + 2, D])
        l3w1 = sb("l3w1", [3 * AD + 1, P])
        l3w2 = sb("l3w2", [P, D])
        l3b1 = sb("l3b1", [P, 1])
        wl = sb("wl", [D, D])
        lrows = sb("lrows", [P, 3, D])
        lnwr = sb("lnwr", [P, D])
        poolb = sb("poolb", [P, 1])
        fb = sb("fb", [P, D])
        b2 = sb("b2", [P, D])
        w1row = sb("w1row", [P, D])
        w12c = sb("w12c", [D, 2])
        w12r = sb("w12r", [D, 4])
        rcd = sb("rcd", [P, 2, D])
        coef = sb("coef", [P, 1])
        ucol = sb("ucol", [P, 1])

        PS = ctx.enter_context(nc.psum_tensor("PS", [P, 8 * 512], F32))

        def bank(i, n=1):
            return PS[:, i * 512:(i + n) * 512]

        def bc(ap, shape):
            while len(ap.shape) < len(shape):
                ap = ap.unsqueeze(len(ap.shape))
            return ap.broadcast_to(shape)

        def rowbc(row, mid):
            return row.unsqueeze(1).broadcast_to([P, mid, row.shape[1]])

        def dbc(ap, n):
            return bass.AP(tensor=ap.tensor, offset=ap.offset, ap=[[0, n], [1, ap.shape[-1]]])

        runs64 = runs.rearrange("r (h d) -> (r h) d", d=D)
        runs_l064 = runs_l0.rearrange("r (h d) -> (r h) d", d=D)
        runs_e128 = runs_e.rearrange("r (h d) -> (r h) d", d=2 * D)
        fill64 = fill.rearrange("r (h d) -> (r h) d", d=D)

        block = ctx.enter_context(nc.Block())
        W = {"params": 0}
        N1, N2, N3, N4, N8 = 0, NCH, 2 * NCH, 3 * NCH, 7 * NCH
        QA, QB, QC, QD, QE = 0, NG, 2 * NG, 6 * NG, 7 * NG
        ZF = 2 * GT * P
        FW = H * 2 * D // P
        NZ = -(-FW // ZF)

        @block.sync
        def _(sp):
            def load(dst, src):
                sp.dma_start(dst, src).then_inc(sem("params"), 16)
                W["params"] += 16

            load(X[:, :], a["x"].rearrange("(p j) d -> p (j d)", p=P))
            load(SI, a["src_q"])
            load(DI, a["dst_q"])
            load(DX, bass.AP(tensor=a["dst_ext"].tensor, offset=0, ap=[[TILES, P], [1, TILES + 1]]))
            load(w_q, a["ew_q"])
            load(poolw[:, :], a["poolw_t"])
            load(finalw[:, :], a["finalw_t"])
            load(w3[:, :], a["w3_t"])
            for i in range(3):
                load(w4[:, i, :], a["w4_t"][i * D:(i + 1) * D, :])
            load(w4c[2:D + 2, :], a["w4_t"][2 * D:3 * D, :])
            load(l3w1[:, :], a["l3w1"])
            load(l3w2[:, :], a["l3w2"])
            load(l3b1[:, :], a["l3b1"])
            load(poolb[0:D, :], a["pool_b"])
            load(poolb[D:P, :], a["pool_b"])
            load(fb[:, :], dbc(a["final_b"], P))
            load(b2[:, :], dbc(a["l3b2"], P))
            load(w1row[:, :], dbc(a["w1"].rearrange("d o -> o d"), P))
            load(w12c[:, 0:1], a["w1"])
            load(w12c[:, 1:2], a["w2"])
            load(coef[:, :], dbc(a["coef"], P))
            load(ucol[:, :], dbc(a["u"], P))
            load(vin[:, :], a["v"].rearrange("(p j) o -> p (j o)", p=P))

            def table_out(n):
                sp.wait_ge(sem("t_ready"), n)
                sp.sem_inc(sem("sp_turns"), 1)
                sp.dma_start(table.rearrange("(p j) d -> p (j d)", p=P), T[:, :]).then_inc(sem("table_out"), 16)

            sp.wait_ge(sem("md_ready"), 1)
            sp.dma_start(same_dst.rearrange("h (q t) -> (h q) t", t=TILES), MD).then_inc(sem("same_dst"), 16)
            table_out(1)
            def masks_in(masks, c, slot, lo):
                if positive(lo):
                    sp.wait_ge(sem("scanned"), lo)
                sp.sem_inc(sem("sp_turns"), 1)
                for h in range(2):
                    src = masks[h:h + 1, bass.ds(c * CE, 2 * CE)]
                    sp.dma_start(M[h * D:(h + 1) * D, slot, :],
                                 src.broadcast_to([D, 2 * CE])).then_inc(sem(f"masks_in{slot}"), 16)

            def runs_out(dst, c, i, n):
                sp.wait_ge(sem("r_ready"), n + 1)
                sp.sem_inc(sem("sp_turns"), 1)
                rows = dst[bass.ds(c * CE, CE), :].rearrange("(k p) d -> p k d", p=P)
                sp.dma_start(rows, R[:, i, :].rearrange("p (k d) -> p k d", k=KC)).then_inc(sem(f"runs_out{i}"), 16)

            def gather_pass(masks, idx, dst, n0, g0, first_of_sem):
                r0 = n0 if isinstance(n0, int) and n0 == 0 else n0 - NCH
                """Indices and masks in, running rows out, of a pass that gathers."""
                def step(it, i, lead):
                    c = it * 4 + i
                    if lead != "last":
                        if lead != "first":
                            sp.wait_ge(sem(f"{g0}{i}"), (it + first_of_sem) * 128)
                            sp.sem_inc(sem("sp_turns"), 1)
                        sp.dma_start(IDX[:, i, :], idx[:, bass.ds(c * 8, 8)]).then_inc(sem(f"idx_in{i}"), 16)
                        if i % 2 == 0:
                            masks_in(masks, c, i // 2, c + n0 - 2)
                    if lead != "first":
                        runs_out(dst, c - 4, i, c - 4 + r0)
                for i in range(4):
                    step(0, i, "first")
                with sp.Fori(1, NIT) as it:
                    for i in range(4):
                        step(it, i, "mid")
                for i in range(4):
                    step(NIT, i, "last")

            gather_pass(same_dst, a["src_q"], runs_l0, N1, "gath_a", 0)

            for i in range(2):
                sp.wait_ge(sem("starts_ready"), i + 1)
                sp.dma_start(counts[i:i + 1, :].rearrange("o (h l) -> (o h) l", l=P), HC[0:NJ, i, :]).then_inc(sem("starts_out"), 16)
                sp.dma_start(starts[i:i + 1, :].rearrange("o (h l) -> (o h) l", l=P), HC[0:NJ, 2 + i, :]).then_inc(sem("starts_out"), 16)
            sp.wait_ge(sem("starts_out"), 64)
            for i in range(2):
                sp.dma_start(cnt[i][:, :], counts[i:i + 1, :].rearrange("o (p j) -> (o p) j", p=P)).then_inc(sem("starts_in"), 16)
                sp.dma_start(beg[i][:, :], starts[i:i + 1, :].rearrange("o (p j) -> (o p) j", p=P)).then_inc(sem("starts_in"), 16)
            sp.dma_start(dh[0:1, 0:1], a["dst_ext"][:, H + 1:H + 2]).then_inc(sem("dh_in"), 16)
            sp.wait_ge(sem("dh_in"), 16)
            node_h = sp.value_load(dh[0:1, 0:1], min_val=0, max_val=NP - 1)
            sp.wait_ge(sem("filled"), 16 * NJ)
            sp.dma_start(fill64[1:2, :], table[bass.ds(node_h, 1), :]).then_inc(sem("fill_b"), 16)
            sp.wait_ge(sem("fill_b"), 16)

            def step2(it, i, first):
                c = it * 4 + i
                sp.wait_ge(sem("fwd"), c + N2 - 3)
                sp.sem_inc(sem("sp_turns"), 1)
                rows = fill[bass.ds(c * CE, CE), :].rearrange("(k p) d -> p k d", p=P)
                sp.dma_start(G[:, i, :].rearrange("p (k d) -> p k d", k=KC), rows).then_inc(sem(f"fill_in{i}"), 16)
                if i % 2 == 0:
                    masks_in(same_dst, c, i // 2, c + N2 - 2)
                if not first:
                    sp.wait_ge(sem(f"scattered{i}"), it * 128)
                    sp.sem_inc(sem("sp_turns"), 1)
                rt = RT[:, i, :, :].rearrange("p (k h) r -> p k h r", h=2)
                for h in range(2):
                    rows = a["attr"][bass.ds(c * CE + h * H, CE), :].rearrange("(k p) d -> p k d", p=P)
                    sp.dma_start(rt[:, :, h, D:D + AD], rows).then_inc(sem(f"attr_in{i}"), 16)
            for i in range(4):
                step2(0, i, True)
            with sp.Fori(1, NIT) as it:
                for i in range(4):
                    step2(it, i, False)

            for i in range(4):
                sp.wait_ge(sem(f"scattered{i}"), NIT * 128)

            def out3(c, i):
                runs_out(runs, c, i, c + N3 - NCH)
                sp.wait_ge(sem("r2_ready"), c + 1)
                sp.sem_inc(sem("sp_turns"), 1)
                rows = runs_e[bass.ds(c * CE, CE), :].rearrange("(k p) d -> p k d", p=P)
                sp.dma_start(rows, R2[i % 2].rearrange("p (k d) -> p k d", k=KC)).then_inc(sem(f"runs_e_out{i % 2}"), 16)
                sp.wait_ge(sem("mk_ready"), c + 1)
                sp.sem_inc(sem("sp_turns"), 1)
                for h in range(2):
                    sp.dma_start(same_src[h:h + 1, bass.ds(c * CE, CE)], MK[i % 2][h * D:h * D + 1, :]).then_inc(sem(f"same_src{i % 2}"), 16)
                sp.wait_ge(sem("dst_ready"), c + 1)
                sp.sem_inc(sem("sp_turns"), 1)
                sp.dma_start(dst_by_src[:, bass.ds(c * 8, 8)], IDX[:, i % 2, :]).then_inc(sem(f"dst_out{i % 2}"), 16)

            def step3(it, i, lead):
                c = it * 4 + i
                if lead != "last":
                    if lead != "first":
                        sp.wait_ge(sem("rec_used"), c - 3)
                        sp.sem_inc(sem("sp_turns"), 1)
                        sp.wait_ge(sem("dst_ready"), c - 3)
                        sp.sem_inc(sem("sp_turns"), 1)
                    for h in range(2):
                        rows = rec[bass.ds(c * CE + h * H, CE), :].rearrange("(k p) d -> p k d", p=P)
                        for t, c0 in ((G[:, i, :], 0), (RD[:, i, :], D0)):
                            sp.dma_start(t.rearrange("p (k h d) -> p k h d", k=KC, h=2)[:, :, h, :],
                                         rows[:, :, c0:c0 + D]).then_inc(sem(f"rec_in{i}"), 16)
                if lead != "first" or i >= 2:
                    if lead != "last" or i < 2:
                        out3(c - 2, (i + 2) % 4)
            for i in range(4):
                step3(0, i, "first")
            with sp.Fori(1, NIT) as it:
                for i in range(4):
                    step3(it, i, "mid")
            for i in range(2):
                step3(NIT, i, "last")

            def carry_in(dst, src, n):
                sp.dma_start(dst, src).then_inc(sem("carry"), 16)

            for i in range(4):
                sp.wait_ge(sem(f"runs_out{i}"), 16 * NIT * 2)
            for i in range(2):
                sp.wait_ge(sem(f"runs_e_out{i}"), 16 * NCH // 2)
            carry_in(CR[:, :], dbc(runs_e[H - 1:H, 0:2 * D], P), 0)
            sp.wait_ge(sem("carry_used"), 1)
            carry_in(CR[:, 0:D], dbc(runs_l0[H - 1:H, 0:D], P), 0)
            carry_in(CR2[:, :], dbc(runs[H - 1:H, 0:D], P), 0)

            with sp.Fori(0, LAYERS) as l:
                sp.wait_ge(sem("h_ready"), l + 1)
                sp.sem_inc(sem("sp_turns"), 1)
                sp.dma_start(wl[:, :], a["ws"][bass.ds(l * D, D), :]).then_inc(sem("layer_in"), 16)
                for i, nm in enumerate(("bs", "lnw", "lnb")):
                    sp.dma_start(lrows[:, i, :], a[nm][bass.ds(l, 1), :].broadcast_to([P, D])).then_inc(sem("layer_in"), 16)
                table_out(l + 2)
                gather_pass(same_dst, a["src_q"], runs, N4 + l * NCH, "gath_b", l * NIT)
                for i in range(4):
                    sp.wait_ge(sem(f"runs_out{i}"), 16 * NIT * (l + 3))
                    sp.sem_inc(sem("sp_turns"), 1)
                sp.wait_ge(sem("carry_used"), l + 2)
                sp.sem_inc(sem("sp_turns"), 1)
                carry_in(CR[:, 0:D], dbc(runs[H - 1:H, 0:D], P), 0)

            table_out(LAYERS + 2)
            for i in range(2):
                sp.wait_ge(sem(f"same_src{i}"), 16 * NCH)
                sp.wait_ge(sem(f"dst_out{i}"), 8 * NCH)
            gather_pass(same_src, dst_by_src, runs, N8, "gath_c", 0)
            for i in range(4):
                sp.wait_ge(sem(f"runs_out{i}"), 16 * NIT * 7)
            sp.wait_ge(sem("carry_used"), LAYERS + 2)
            carry_in(CR[:, 0:D], dbc(runs[H - 1:H, 0:D], P), 0)

            sp.wait_ge(sem("x_ready"), 1)
            sp.dma_start(out.rearrange("(p j) d -> p (j d)", p=P), X[:, :]).then_inc(sem("out"), 16)
            sp.wait_ge(sem("out"), 16)

        @block.gpsimd
        def _(pool):
            pool.iota(iota_i[:, :], [[1, P]], base=0, channel_multiplier=0).then_inc(sem("iota"), 1)
            pool.iota(pidx_i[:, :], [[0, 1]], base=0, channel_multiplier=1).then_inc(sem("iota"), 1)
            pool.iota(na[:, :].bitcast(I32), [[1, NJ]], base=0, channel_multiplier=NJ).then_inc(sem("iota"), 1)

            def gather_pass(used, n0, name, done, tables):
                pool.wait_ge(sem("table_out"), tables)
                pool.sem_inc(sem("pool_turns"), 1)

                def step(it, i):
                    c = it * 4 + i
                    pool.wait_ge(sem(f"idx_in{i}"), (it + done) * 16 + 16)
                    pool.sem_inc(sem("pool_turns"), 1)
                    if positive(c + n0 - 3):
                        pool.wait_ge(sem(used), c + n0 - 3)
                    pool.sem_inc(sem("pool_turns"), 1)
                    for q in range(8):
                        pool.indirect_dma_start(
                            G[:, i, q * D:(q + 1) * D], None, table,
                            bass.IndirectOffsetOnAxis(ap=IDX[:, i, q:q + 1], axis=0)).then_inc(sem(f"{name}{i}"), 16)
                for i in range(4):
                    step(0, i)
                with pool.Fori(1, NIT) as it:
                    for i in range(4):
                        step(it, i)

            gather_pass("g_used", 0, "gath_a", 0, 16)

            pool.wait_ge(sem("fill_zero"), 16 * NZ)
            pool.wait_ge(sem("rows_ready"), 1)
            for j in range(NJ):
                pool.indirect_dma_start(
                    fill64, bass.IndirectOffsetOnAxis(ap=begrow[:, j:j + 1], axis=0),
                    T[:, j * D:(j + 1) * D], None, bounds_check=EP - 1, oob_is_err=False).then_inc(sem("filled"), 16)

            def scatter(it, i):
                pool.wait_ge(sem(f"attr_in{i}"), it * 32 + 32)
                pool.sem_inc(sem("pool_turns"), 1)
                pool.wait_ge(sem("pay_ready"), it * 4 + i + 1)
                pool.sem_inc(sem("pool_turns"), 1)
                pool.wait_ge(sem("msg_ready"), it * 4 + i + 1)
                pool.sem_inc(sem("pool_turns"), 1)
                pool.wait_ge(sem("pos_ready"), it * 4 + i + 1)
                pool.sem_inc(sem("pool_turns"), 1)
                for q in range(8):
                    pool.indirect_dma_start(
                        rec, bass.IndirectOffsetOnAxis(ap=IDX[:, i, q:q + 1], axis=0),
                        RT[:, i, q, :], None).then_inc(sem(f"scattered{i}"), 16)
            with pool.Fori(0, NIT) as it:
                for i in range(4):
                    scatter(it, i)

            def ends(dst, rows, idx, n):
                for g in range(NG):
                    s = g % 2
                    done = (n + g) // 2 * 16 * GT
                    if positive(done):
                        pool.wait_ge(sem(f"ends{s}"), done)
                    pool.sem_inc(sem("pool_turns"), 1)
                    for k in range(GT):
                        j = g * GT + k
                        pool.indirect_dma_start(dst[:, j * D:(j + 1) * D], None, rows,
                                                bass.IndirectOffsetOnAxis(ap=idx[:, j:j + 1], axis=0)).then_inc(sem(f"ends{s}"), 16)

            def runs_done(n):
                for i in range(4):
                    pool.wait_ge(sem(f"runs_out{i}"), 16 * NIT * n)
                    pool.sem_inc(sem("pool_turns"), 1)

            runs_done(1)
            for i in range(4):
                pool.wait_ge(sem(f"scattered{i}"), NIT * 128)
                pool.sem_inc(sem("pool_turns"), 1)
            ends(T, runs_l064, endrow[0], 0)

            for i in range(2):
                pool.wait_ge(sem(f"runs_e_out{i}"), 16 * NCH // 2)
            runs_done(2)
            for g in range(NG):
                s = g % 2
                if positive(g - 1):
                    pool.wait_ge(sem("d_used"), g - 1)
                pool.sem_inc(sem("pool_turns"), 1)
                for k in range(GT):
                    j = g * GT + k
                    pool.indirect_dma_start(DG[s][:, k * P:(k + 1) * P], None, runs_e128,
                                            bass.IndirectOffsetOnAxis(ap=endrow[1][:, j:j + 1], axis=0)).then_inc(sem(f"dends{s}"), 16)
            pool.wait_ge(sem("l3_done"), NG)
            ends(AG, runs64, endrow[1], NG)

            with pool.Fori(0, LAYERS) as l:
                gather_pass("fwd", N4 - NCH + l * NCH, "gath_b", (l + 1) * NIT, l * 16 + 32)
                runs_done(l + 3)
                pool.wait_ge(sem("h_ready"), l + 1)
                pool.sem_inc(sem("pool_turns"), 1)
                ends_layer(pool, l, sem, AG, runs64, endrow[0], NG, GT)
            gather_pass("fwd", N8 - NCH, "gath_c", 5 * NIT, 16 * (LAYERS + 2))
            runs_done(7)
            pool.wait_ge(sem("he_ready"), 1)
            ends(AG, runs64, endrow[1], 6 * NG)

        @block.tensor
        def _(pe):
            def fwd(i, src, n, arrived, value):
                pe.wait_ge(arrived, value)
                if positive(n - 1):
                    pe.wait_ge(sem("pt_free"), n - 1)
                for k in range(KC):
                    t = pe.transpose(bank(i % 2)[:, k * P:(k + 1) * P], src[:, k * P:(k + 1) * P], ident[:, :])
                return t.then_inc(sem("fwd"), 1)

            def back(i, n, r):
                pe.wait_ge(sem("scanned"), n + 1)
                if positive(r - 1):
                    pe.wait_ge(sem("r_ready"), r - 1)
                for k in range(KC):
                    t = pe.transpose(bank(2 + i % 2)[:, k * P:(k + 1) * P], S[:, i % 2, k * P:(k + 1) * P], ident[:, :])
                t.then_inc(sem("back"), 1)

            def project(K, rhs, n0):
                def step(n, s):
                    pe.wait_ge(sem("z_ready"), n + 1)
                    if positive(n):
                        pe.wait_ge(sem("zts_ready"), n)
                    pe.sem_inc(sem("pe_turns"), 1)
                    for k in range(GT):
                        t = pe.transpose(PS[0:K, k * P:(k + 1) * P], Z[:, s, k * K:(k + 1) * K], ident[:, :])
                    t.then_inc(sem("zt"), 1)
                    pe.wait_ge(sem("zts_ready"), n + 1)
                    if positive(n):
                        pe.wait_ge(sem("zo_used"), n)
                    for k in range(GT):
                        t = pe.matmul(bank(2)[:, k * D:(k + 1) * D], ZTs[0:K, k * P:(k + 1) * P], rhs, start=True, stop=True)
                    t.then_inc(sem("zo"), 1)
                if isinstance(n0, int) and n0 == 0:
                    step(0, 0)
                    step(1, 1)
                    with pe.Fori(1, NG // 2) as g:
                        step(g * 2, 0)
                        step(g * 2 + 1, 1)
                else:
                    with pe.Fori(0, NG // 2) as g:
                        step(g * 2 + n0, 0)
                        step(g * 2 + n0 + 1, 1)

            def gather_pass(n0, name, done):
                def step(it, i, first):
                    c = it * 4 + i
                    fwd(i, G[:, i, :], c + n0 - NCH, sem(f"{name}{i}"), (it + done) * 128 + 128)
                    if not (first and i == 0):
                        back((i - 1) % 4, c + n0 - 1, c + n0 - 1 - NCH)
                for i in range(4):
                    step(0, i, True)
                with pe.Fori(1, NIT) as it:
                    for i in range(4):
                        step(it, i, False)
                back(3, n0 + (NCH - 1), n0 - 1)

            pe.wait_ge(sem("consts"), 1)
            pe.wait_ge(sem("params"), W["params"])
            pe.wait_ge(sem("w12_ready"), 1)
            pe.matmul(bank(4)[0:2, 0:D], w12r[:, 0:2], w4[:, 0, :], start=True, stop=True).then_inc(sem("w4_small"), 1)
            for i in range(2):
                pe.matmul(bank(5 + i)[:, 0:D], w12r[:, 2 + i:3 + i].broadcast_to([D, P]), w4[:, 1, :],
                          start=True, stop=True).then_inc(sem("w4_small"), 1)
            pe.wait_ge(sem("w4_copied"), 1)
            project(D, poolw[:, :], QA)

            pe.wait_ge(sem("hist_zero"), 1)
            for b in range(2):
                pe.matmul(bank(4 + b)[0:NJ, 0:P], ident[:, 0:NJ], HC[:, 0, :], start=True, stop=False, skip_group_check=True)

            def hist(n, s):
                pe.wait_ge(sem("oh_ready"), n + 1)
                for b in range(2):
                    for k in range(KC):
                        t = pe.matmul(bank(4 + b)[0:NJ, 0:P], OH[:, s, 2 * b, k, 0:NJ], OH[:, s, 2 * b + 1, k, :],
                                      start=False, stop=False, skip_group_check=True)
                t.then_inc(sem("hist_done"), 1)

            def step1(it, i, first):
                c = it * 4 + i
                fwd(i, Gs[:, i % 2, :], c, sem("gs_ready"), c + 1)
                hist(c * 2, 0)
                if not (first and i == 0):
                    back((i - 1) % 4, c - 1, c - 1)
                hist(c * 2 + 1, 1)
            for i in range(4):
                step1(0, i, True)
            with pe.Fori(1, NIT) as it:
                for i in range(4):
                    step1(it, i, False)
            back(3, NCH - 1, NCH - 1)
            for b in range(2):
                pe.matmul(bank(4 + b)[0:NJ, 0:P], ident[:, 0:NJ], HC[:, 0, :], start=False, stop=True,
                          skip_group_check=True).then_inc(sem("hist_sum"), 1)

            pe.wait_ge(sem("row_sums"), 1)
            pe.matmul(bank(6)[0:NJ, 0:2], below[0:NJ, 0:NJ], hoff[0:NJ, :], start=True, stop=True).then_inc(sem("row_offs"), 1)

            pe.wait_ge(sem("starts_ready"), 2)
            pe.wait_ge(sem("r_ready"), NCH)
            pe.matmul(bank(3)[0:NJ, 0:P], ident[0:NJ, 0:NJ], HC[0:NJ, 3, :], start=True, stop=False,
                      skip_group_check=True).then_inc(sem("counted"), 1)
            HB = 2 * NCH

            def digit(h, s, d, k):
                return OH[:, s // 2, 2 * (s % 2) + d, k, :]

            def key_col(i, q):
                return RT[:, i, q, C_SRC:C_SRC + 1].broadcast_to([P, P])

            def turn(h, s):
                pe.wait_ge(sem("oh_ready"), h + HB + 1)
                if positive(h):
                    pe.wait_ge(sem("oht_copied"), h)
                ohb = bank(5).bitcast(BF16)
                for k in range(KC):
                    t = pe.transpose(ohb[0:NJ, k * P:(k + 1) * P], digit(h, s, 0, k)[:, 0:NJ], ident_b[:, :])
                t.then_inc(sem("oht"), 1)

            def src_row(h, s, k):
                t = pe.matmul(bank(4 - 2 * (s % 2))[:, k * P:(k + 1) * P], key_col(s // 2, s % 2 * KC + k), ident[:, :],
                              start=True, stop=True)
                if k == KC - 1:
                    t.then_inc(sem("src_rows"), 1)

            def rows_free(h, c):
                pe.wait_ge(sem("pay_ready"), c + 1)
                if positive(h - 1):
                    pe.wait_ge(sem("ranked"), h - 1)

            def chain(c, i, x, last):
                h, s = c * 2 + x, i % 2 * 2 + x
                h_slot, n_slot = (i * 2 + x) % 4, (i * 2 + x + 1) % 4
                if positive(h - 1):
                    pe.wait_ge(sem("looked"), h - 1)
                for k in range(KC):
                    pe.wait_ge(sem("c_copied"), h * KC + k + 1)
                    pe.matmul(bank(3)[0:NJ, 0:P], digit(h, h_slot, 0, k)[:, 0:NJ], digit(h, h_slot, 1, k),
                              start=False, stop=False, skip_group_check=True).then_inc(sem("counted"), 1)
                    if k == 0:
                        pe.wait_ge(sem("oht_copied"), h + 1)
                    t = pe.matmul(bank(6 + x)[:, k * P:(k + 1) * P], OHTs[0:NJ, x, k * P:(k + 1) * P], Cs[0:NJ, k % 2, :],
                                  start=True, stop=True)
                    if k == KC - 1:
                        t.then_inc(sem("lookups"), 1)
                    if not last:
                        if k == 0:
                            turn(h + 1, n_slot)
                            rows_free(h + 1, c + x)
                        n = i * 2 + x + 1
                        src_row(h + 1, n % 8, k)

            def fwd2(it, i):
                pe.wait_ge(sem(f"fill_in{i}"), it * 16 + 16)
                pe.wait_ge(sem("pt_free"), it * 4 + i + N2)
                for k in range(KC):
                    t = pe.transpose(bank(0)[:, k * P:(k + 1) * P], G[:, i, k * P:(k + 1) * P], ident[:, :])
                t.then_inc(sem("fwd"), 1)

            def back2(n, i):
                pe.wait_ge(sem("scanned"), n + N2 + 1)
                if positive(n):
                    pe.wait_ge(sem("msg_ready"), n)
                for k in range(KC):
                    t = pe.transpose(bank(1)[:, k * P:(k + 1) * P], S[:, i % 2, k * P:(k + 1) * P], ident[:, :])
                t.then_inc(sem("back2"), 1)

            def step2(it, i, last):
                c = it * 4 + i
                end = last and i == 3
                chain(c, i, 0, False)
                back2(c, i)
                if not end:
                    fwd2(it + (i + 1) // 4, (i + 1) % 4)
                chain(c, i, 1, end)
            fwd2(0, 0)
            turn(0, 0)
            rows_free(0, 0)
            for k in range(KC):
                src_row(0, 0, k)
            for i in range(4):
                step2(0, i, False)
            with pe.Fori(1, NIT - 1) as it:
                for i in range(4):
                    step2(it, i, False)
            for i in range(4):
                step2(NIT - 1, i, True)

            def fwd3(it, i, first):
                c = it * 4 + i
                pe.wait_ge(sem(f"rec_in{i}"), it * 64 + 64)
                if positive(c):
                    pe.wait_ge(sem("ks_ready"), c)
                for k in range(KC):
                    for h in range(2):
                        q = (k * 2 + h) * D + C_SRC - D0
                        t = pe.matmul(bank(0)[h * D:(h + 1) * D, k * P:(k + 1) * P],
                                      RD[:, i, q:q + 1].broadcast_to([P, D]), ident[:, :], start=True, stop=True)
                t.then_inc(sem("kr"), 1)
                if positive(c - 1):
                    pe.wait_ge(sem("l3r"), c - 1)
                for k in range(KC):
                    t = pe.transpose(bank(1 + 5 * (i % 2))[:, k * P:(k + 1) * P], G[:, i, k * P:(k + 1) * P], ident[:, :])
                t.then_inc(sem("fwd3"), 1)
                if positive(c - 1):
                    pe.wait_ge(sem("scan3"), c - 1)
                for k in range(KC):
                    t = pe.transpose(bank(2 + 5 * (i % 2))[:, k * P:(k + 1) * P], RD[:, i, k * P:(k + 1) * P], ident[:, :])
                t.then_inc(sem("rec_used"), 1)

            def back3(i, c):
                pe.wait_ge(sem("scanned"), c + N3 + 1)
                pe.wait_ge(sem("r_ready"), c + N3 - NCH)
                for k in range(KC):
                    t = pe.transpose(bank(3)[:, k * P:(k + 1) * P], S[:, i % 2, k * P:(k + 1) * P], ident[:, :])
                t.then_inc(sem("back"), 1)
                for m, src in enumerate((S2, S3)):
                    pe.wait_ge(sem("scan2" if m == 0 else "scan3"), c + 1)
                    if positive(2 * c + m - 1):
                        pe.wait_ge(sem("r2_half"), 2 * c + m - 1)
                    for k in range(KC):
                        t = pe.transpose(bank(4 + m)[:, k * P:(k + 1) * P], src[i % 2][:, k * P:(k + 1) * P], ident[:, :])
                    t.then_inc(sem("back3"), 1)

            def step3(it, i, first):
                fwd3(it, i, first)
                if not (first and i == 0):
                    back3((i - 1) % 4, it * 4 + i - 1)
            for i in range(4):
                step3(0, i, True)
            with pe.Fori(1, NIT) as it:
                for i in range(4):
                    step3(it, i, False)
            back3(3, NCH - 1)

            K3 = 3 * AD + 1

            def mlp(g, s):
                pe.wait_ge(sem("z3_ready"), g + 1)
                if positive(g):
                    pe.wait_ge(sem("z3ts_ready"), g)
                for k in range(GT):
                    t = pe.transpose(PS[0:K3, k * P:(k + 1) * P], Z[:, s, k * K3:(k + 1) * K3], ident[:, :])
                t.then_inc(sem("z3t"), 1)
                pe.wait_ge(sem("z3ts_ready"), g + 1)
                if positive(g):
                    pe.wait_ge(sem("hs_ready"), g)
                for m in range(2):
                    t = pe.matmul(bank(4 + m)[:, 0:GW], l3w1[:, :], ZTs[0:K3, m * GW:(m + 1) * GW], start=True, stop=True)
                t.then_inc(sem("h3"), 1)
                pe.wait_ge(sem("hs_ready"), g + 1)
                if positive(g):
                    pe.wait_ge(sem("l3_done"), g)
                for k in range(GT):
                    t = pe.matmul(bank(2)[:, k * D:(k + 1) * D], HS[:, k * P:(k + 1) * P], l3w2[:, :], start=True, stop=True)
                t.then_inc(sem("o3"), 1)
            mlp(0, 0)
            mlp(1, 1)
            with pe.Fori(1, NG // 2) as g:
                mlp(g * 2, 0)
                mlp(g * 2 + 1, 1)

            project(2 * D, finalw[:, :], QB)

            def total(col, n):
                pe.wait_ge(sem("part_sum"), n)
                pe.matmul(bank(4)[:, 0:1], ones[:, :], st[:, col:col + 1], start=True, stop=True).then_inc(sem("total"), 1)
            with pe.Fori(0, LAYERS) as l:
                pe.wait_ge(sem("layer_in"), l * 64 + 64)
                pe.sem_inc(sem("pe_turns"), 1)
                project(D, wl[:, :], QC + l * NG)
                gather_pass(N4 + l * NCH, "gath_b", l * NIT)
                total(0, l * 2 + 1)
                total(1, l * 2 + 2)
            project(D, w3[:, :], QD)
            project(D + 2, w4c[:, :], QE)
            gather_pass(N8, "gath_c", 0)

        @block.scalar
        def _(act):
            def rcopy(it, i, n, outs):
                act.wait_ge(sem("back"), n + 1)
                if positive(outs):
                    act.wait_ge(sem(f"runs_out{i}"), outs)
                act.copy(R[:, i, :], bank(2 + i % 2)).then_inc(sem("r_ready"), 1)

            def project(K, n0):
                def step(n):
                    act.wait_ge(sem("zt"), n + 1)
                    if positive(n):
                        act.wait_ge(sem("zo"), n)
                    act.copy(ZTs[0:K, :], PS[0:K, 0:GT * P]).then_inc(sem("zts_ready"), 1)
                if isinstance(n0, int) and n0 == 0:
                    step(0)
                    with act.Fori(1, NG) as g:
                        step(g)
                else:
                    with act.Fori(0, NG) as g:
                        step(g + n0)

            def gather_pass(n0, outs):
                for i in range(4):
                    rcopy(0, i, n0 + i, outs * 16)
                with act.Fori(1, NIT) as it:
                    for i in range(4):
                        rcopy(it, i, it * 4 + (n0 + i) , (it + outs) * 16)

            def root(n):
                act.wait_ge(sem("root_in"), n)
                act.activation(na[:, :], nb[:, :], ACT.Sqrt).then_inc(sem("root_out"), 1)

            act.wait_ge(sem("w4_small"), 3)
            act.copy(w4c[0:2, :], bank(4)[0:2, 0:D]).then_inc(sem("w4_act"), 1)
            act.copy(rcd[:, 0, :], bank(5)[:, 0:D]).then_inc(sem("w4_act"), 1)
            act.copy(rcd[:, 1, :], bank(6)[:, 0:D]).then_inc(sem("w4_act"), 1)
            act.wait_ge(sem("w4_act"), 3)
            act.sem_inc(sem("w4_copied"), 1)
            root(1)
            project(D, QA)
            act.wait_ge(sem("zeroed"), 1)
            fv = fill.rearrange("(p r) d -> p (r d)", p=P)
            for z0 in range(0, FW, ZF):
                w = min(ZF, FW - z0)
                act.dma_start(fv[:, z0:z0 + w], zero_rows[:, 0:w]).then_inc(sem("fill_zero"), 16)

            def relu1(i, n):
                act.wait_ge(sem("fwd"), n + 1)
                if positive(n - 1):
                    act.wait_ge(sem("scanned"), n - 1)
                act.activation(L[:, i % 2, :], bank(i % 2), ACT.Relu, bias=poolb[:, 0:1]).then_inc(sem("pt_free"), 1)

            def step1(it, i, first):
                relu1(i, it * 4 + i)
                if not (first and i == 0):
                    rcopy(it, (i - 1) % 4, it * 4 + i - 1, (it if i else it - 1) * 16 if not first else 0)
            for i in range(4):
                step1(0, i, True)
            relu1(0, 4)
            rcopy(0, 3, 3, 0)
            for i in range(1, 4):
                step1(1, i, False)
            with act.Fori(2, NIT) as it:
                for i in range(4):
                    step1(it, i, False)
            rcopy(NIT - 1, 3, NCH - 1, (NIT - 1) * 16)
            root(2)

            def payload(it, i, first):
                if not first:
                    act.wait_ge(sem(f"scattered{i}"), it * 128)
                    act.sem_inc(sem("act_turns"), 1)
                q = it * 32 + i * 8
                for k, (col, t) in enumerate(((C_DST, dstf_q[:, bass.ds(q, 8)]), (C_SRC, srcf_q[:, bass.ds(q, 8)]))):
                    act.activation(RT[:, i, :, col], t, ACT.Copy)
                act.activation(RT[:, i, :, C_WP], w_q[:, bass.ds(q, 8)], ACT.Relu)
                act.activation(RT[:, i, :, C_WN], w_q[:, bass.ds(q, 8)], ACT.Relu, scale=-1.0).then_inc(sem("pay_ready"), 1)

            def oht_copy(h, s):
                act.wait_ge(sem("oht"), h + 1)
                if positive(h - 1):
                    act.wait_ge(sem("lookups"), h - 1)
                act.copy(OHTs[0:NJ, s, :], bank(5).bitcast(BF16)[0:NJ, 0:KC * P]).then_inc(sem("oht_copied"), 1)

            def c_copy(h, k):
                n = h * KC + k
                act.wait_ge(sem("counted"), n + 1)
                act.copy(Cs[0:NJ, k % 2, :], bank(3)[0:NJ, 0:P]).then_inc(sem("c_copied"), 1)

            def messages(c, i, q0):
                for q in (q0, q0 + 1):
                    t = act.activation(RT[:, i, q, 0:D], bank(1)[:, q * D:(q + 1) * D], ACT.Identity,
                                       scale=s_q[:, bass.ds(c * 8 + q, 1)], bias=pen_q[:, bass.ds(c * 8 + q, 1)])
                if q0 == 6:
                    t.then_inc(sem("msg_ready"), 1)

            def half(c, i, x, mc, mi, last):
                h = c * 2 + x
                c_copy(h, 0)
                c_copy(h, 1)
                if not last:
                    oht_copy(h + 1, 1 - x)
                c_copy(h, 2)
                if mc is not None:
                    if x == 1:
                        act.wait_ge(sem("back2"), mc + 1)
                        act.sem_inc(sem("act_turns"), 1)
                    messages(mc, mi, 4 - 4 * x)
                c_copy(h, 3)
                if mc is not None:
                    messages(mc, mi, 6 - 4 * x)

            def step2(it, i, first, last):
                c = it * 4 + i
                half(c, i, 0, None if first and i == 0 else c - 1, (i - 1) % 4, False)
                if not (last and i == 3):
                    payload(it + (i + 1) // 4, (i + 1) % 4, first and i < 3)
                half(c, i, 1, c, i, last and i == 3)
            act.wait_ge(sem("starts_ready"), 2)
            for i in range(3):
                act.wait_ge(sem(f"runs_out{i}"), NIT * 16)
            payload(0, 0, True)
            oht_copy(0, 0)
            for i in range(4):
                step2(0, i, True, False)
            with act.Fori(1, NIT - 1) as it:
                for i in range(4):
                    step2(it, i, False, False)
            for i in range(4):
                step2(NIT - 1, i, False, True)
            messages(NCH - 1, 3, 4)
            messages(NCH - 1, 3, 6)

            def step3(it, i, first):
                c = it * 4 + i
                s = i % 2
                act.wait_ge(sem("kr"), c + 1)
                if positive(c - 1):
                    act.wait_ge(sem("mk_ready"), c - 1)
                if positive(c - 1):
                    act.wait_ge(sem("ks_carry"), c - 1)
                act.copy(KS[s][:, 1:CE + 1], bank(0)).then_inc(sem("ks_ready"), 1)
                if not (first and i == 0):
                    act.wait_ge(sem("ks_ready"), c)
                    act.copy(KS[s][:, 0:1], KS[1 - s][:, CE:CE + 1]).then_inc(sem("ks_carry"), 1)
                act.wait_ge(sem("fwd3"), c + 1)
                act.wait_ge(sem("scanned"), c + N3 - 1)
                act.activation(L[:, s, :], bank(1 + 5 * s), ACT.Relu, bias=poolb[:, 0:1]).then_inc(sem("l3r"), 1)
                act.wait_ge(sem("mk_ready"), c + 1)
                if positive(c - 1):
                    act.wait_ge(sem("scan3"), c - 1)
                act.activation(MP[s], MK[s], ACT.Copy, scale=BIG, bias=-BIG).then_inc(sem("mp_ready"), 1)
                if not (first and i == 0):
                    out3(it, (i - 1) % 4, c - 1, first, it if i else it - 1)

            def out3(it, i, c, first, uses):
                s = i % 2
                act.wait_ge(sem("back"), c + N3 - NCH + 1)
                if first:
                    act.wait_ge(sem(f"runs_out{i}"), NIT * 16)
                else:
                    act.wait_ge(sem(f"runs_out{i}"), (uses + NIT) * 16)
                act.copy(R[:, i, :], bank(3)).then_inc(sem("r_ready"), 1)
                r2 = R2[s].rearrange("p (k h m d) -> p k h m d", k=KC, h=2, m=2)
                for m in range(2):
                    act.wait_ge(sem("back3"), c * 2 + m + 1)
                    if not first or i >= 2:
                        act.wait_ge(sem(f"runs_e_out{s}"), (c - i + i // 2 * 2) * 8)
                    t = act.copy(r2[:, :, :, m, :], bank(4 + m).rearrange("p (k h d) -> p k h d", k=KC, h=2))
                    t.then_inc(sem("r2_half"), 1)
                act.wait_ge(sem("r2_half"), c * 2 + 2)
                act.sem_inc(sem("r2_ready"), 1)
            for i in range(4):
                step3(0, i, True)
            with act.Fori(1, NIT) as it:
                for i in range(4):
                    step3(it, i, False)
            out3(NIT - 1, 3, NCH - 1, False, NIT - 1)

            K3 = 3 * AD + 1

            def mlp(g):
                act.wait_ge(sem("z3t"), g + 1)
                if positive(g):
                    act.wait_ge(sem("h3"), g)
                act.copy(ZTs[0:K3, :], PS[0:K3, 0:GT * P]).then_inc(sem("z3ts_ready"), 1)
                act.wait_ge(sem("h3"), g + 1)
                if positive(g):
                    act.wait_ge(sem("o3"), g)
                act.activation(HS[:, 0:GW], bank(4)[:, 0:GW], ACT.Relu, bias=l3b1[:, 0:1])
                act.activation(HS[:, GW:2 * GW], bank(5)[:, 0:GW], ACT.Relu, bias=l3b1[:, 0:1]).then_inc(sem("hs_ready"), 1)
            mlp(0)
            with act.Fori(1, NG) as g:
                mlp(g)

            project(2 * D, QB)
            root(3)
            with act.Fori(0, LAYERS) as l:
                project(D, QC + l * NG)
                gather_pass(N4 + l * NCH - NCH, (l + 2) * NIT)
                act.wait_ge(sem("dev_ready"), l + 1)
                act.activation(AG[:, :], Hn[:, :], ACT.Square, accum_out=st[:, 1:2]).then_inc(sem("sq_done"), 1)
                act.wait_ge(sem("var_ready"), l + 1)
                act.activation(st[:, 4:5], st[:, 3:4], ACT.Sqrt).then_inc(sem("std_ready"), 1)
            root(4)
            project(D, QD)
            project(D + 2, QE)
            gather_pass(N8 - NCH, 6 * NIT)

        @block.vector
        def _(dve):
            order = [0]

            def then(ins):
                order[0] += 1
                ins.then_inc(sem("dve_order"), 1)
                dve.wait_ge(sem("dve_order"), order[0])

            class Steps:
                def __init__(self, name, base):
                    self.sem, self.base, self.k = sem(name), base, 0

                def __call__(self, ins):
                    self.k += 1
                    ins.then_inc(self.sem, 1)
                    dve.wait_ge(self.sem, self.base + self.k)

            def f3(t):
                return t.rearrange("p (j d) -> p j d", d=D)

            dve.wait_ge(sem("iota"), 3)
            then(dve.tensor_copy(iota_f[:, :], iota_i[:, :]))
            then(dve.tensor_copy(iota_b[:, :], iota_f[:, :]))
            then(dve.tensor_copy(pidx[:, :], pidx_i[:, :]))
            then(dve.tensor_copy(nb[:, :], na[:, :].bitcast(I32)))
            then(dve.tensor_scalar(valid[:, :], nb[:, :], float(n_nodes), None, ALU.is_lt))
            dve.tensor_scalar(ident[:, :], iota_f[:, :], pidx[:, 0:1], None, ALU.is_equal)
            dve.tensor_scalar(ident_b[:, :], iota_f[:, :], pidx[:, 0:1], None, ALU.is_equal)
            dve.tensor_scalar(earlier[:, :], iota_f[:, :], pidx[:, 0:1], None, ALU.is_lt)
            dve.tensor_scalar(below[:, :], iota_f[:, :], pidx[:, 0:1], None, ALU.is_gt)
            dve.memset(ones[:, :], 1.0)
            then(dve.memset(HC[:, :, :], 0.0))
            dve.sem_inc(sem("consts"), 1)
            dve.sem_inc(sem("hist_zero"), 1)
            dve.wait_ge(sem("params"), W["params"])
            for i in range(2):
                dve.tensor_scalar(w12r[:, 2 * i:2 * i + 1], w12c[:, i:i + 1], 0.0, None, ALU.max)
                then(dve.tensor_scalar(w12r[:, 2 * i + 1:2 * i + 2], w12c[:, i:i + 1], -1.0, 0.0, ALU.mult, ALU.max))
            dve.sem_inc(sem("w12_ready"), 1)
            dve.tensor_tensor(MD, DX[:, 1:TILES + 1], DX[:, 0:TILES], ALU.is_equal).then_inc(sem("md_ready"), 1)

            def norm(n):
                then(dve.tensor_reduce(nd[:, :], v3(X), AX.X, ALU.add))
                then(dve.tensor_scalar(nd[:, :], nd[:, :], 1.0 / D, None, ALU.mult))
                then(dve.tensor_tensor(v3(Hn), v3(X), bc(nd[:, :], [P, NJ, D]), ALU.subtract))
                then(dve.tensor_tensor(AG[:, :], Hn[:, :], Hn[:, :], ALU.mult))
                then(dve.tensor_reduce(nb[:, :], v3(AG), AX.X, ALU.add))
                dve.tensor_scalar(nb[:, :], nb[:, :], 1.0 / D, EPS, ALU.mult, ALU.add).then_inc(sem("root_in"), 1)
                dve.wait_ge(sem("root_out"), n)
                then(dve.reciprocal(nd[:, :], na[:, :]))
                then(dve.scalar_tensor_tensor(v3(Hn), v3(Hn), 0.0, bc(nd[:, :], [P, NJ, D]), ALU.max, ALU.mult))
            norm(1)
            then(dve.memset(KEYS, 0.0))
            for i, t in enumerate((SI, DI)):
                then(dve.tensor_scalar(tmp_i, t, 7, None, ALU.logical_shift_right))
                then(dve.tensor_copy(KEYS[:, 2 * i, 0:TILES], tmp_i))
                then(dve.tensor_scalar(tmp_i, t, 127, None, ALU.bitwise_and))
                then(dve.tensor_copy(KEYS[:, 2 * i + 1, 0:TILES], tmp_i))
            dve.tensor_copy(srcf_q, SI)
            then(dve.tensor_copy(dstf_q, DI))
            dve.tensor_scalar(s_q, w_q, coef[:, 0:1], 1.0, ALU.mult, ALU.add)
            then(dve.tensor_tensor(pen_q, SI, DI, ALU.is_equal))
            then(dve.tensor_scalar(pen_q, pen_q, -SELF, None, ALU.mult))
            dve.tensor_scalar(vpos[:, :], vin[:, :], 0.0, None, ALU.max)
            then(dve.tensor_scalar(vneg[:, :], vin[:, :], -1.0, 0.0, ALU.mult, ALU.max))
            dve.wait_ge(sem("same_dst"), 16)

            def project(n0, make, post):
                def produce(g, s):
                    n = g + n0
                    if positive(n - 1):
                        dve.wait_ge(sem("zt"), n - 1)
                    make(g, s).then_inc(sem("z_ready"), 1)

                def consume(g):
                    n = g + n0
                    dve.wait_ge(sem("zo"), n + 1)
                    post(g).then_inc(sem("zo_used"), 1)
                produce(0, 0)
                produce(1, 1)
                consume(0)
                produce(2, 0)
                consume(1)
                produce(3, 1)
                with dve.Fori(2, NG // 2) as g:
                    consume(g * 2 - 2)
                    produce(g * 2, 0)
                    consume(g * 2 - 1)
                    produce(g * 2 + 1, 1)
                consume(NG - 2)
                consume(NG - 1)
                dve.wait_ge(sem("zo_used"), n0 + NG)
                dve.sem_inc(sem("dve_turns"), 1)

            def z3(s, K):
                return Z[:, s, 0:GT * K].rearrange("p (j d) -> p j d", d=K)

            zo = f3(bank(2)[:, 0:GW])
            project(QA, lambda g, s: dve.tensor_scalar(z3(s, D), group(Hn, g), 1.0, None, ALU.mult),
                    lambda g: dve.tensor_scalar(group(T, g), zo, 1.0, None, ALU.mult))
            dve.sem_inc(sem("t_ready"), 1)
            dve.memset(Z[:, :, :], 0.0).then_inc(sem("zeroed"), 1)

            def onehots(q, s, h, digits):
                if positive(h - 1):
                    dve.wait_ge(sem("hist_done"), h - 1)
                for d in range(digits):
                    t = dve.tensor_tensor(OH[:, s, d, :, :], rowbc(iota_b[:, :], KC),
                                          bc(KEYS[:, d, bass.ds(q, KC)], [P, KC, P]), ALU.is_equal)
                t.then_inc(sem("oh_ready"), 1)

            def scan(i, n, data, op0, op1, first=False, name="scanned"):
                mask = M[:, i // 2, (i % 2) * CE:(i % 2 + 1) * CE]
                init = 0.0 if first else S[:, 1 - i % 2, CE - 1:CE]
                return dve.tensor_tensor_scan(S[:, i % 2, :], mask, data, init, op0, op1)

            def masks_there(it, i, done):
                if i % 2 == 0:
                    dve.wait_ge(sem(f"masks_in{i // 2}"), (it + done) * 32 + 32)

            def pre1(it, i):
                c = it * 4 + i
                q = c * 8
                dve.wait_ge(sem(f"gath_a{i}"), it * 128 + 128)
                if positive(c - 1):
                    dve.wait_ge(sem("fwd"), c - 1)
                g = G[:, i, :].rearrange("p (q d) -> p q d", d=D)
                o = Gs[:, i % 2, :].rearrange("p (q d) -> p q d", d=D)
                dve.tensor_tensor(o, g, bc(s_q[:, bass.ds(q, 8)], [P, 8, D]), ALU.mult).then_inc(sem("g_used"), 1)
                dve.wait_ge(sem("g_used"), c + 1)
                dve.tensor_tensor(o, o, bc(pen_q[:, bass.ds(q, 8)], [P, 8, D]), ALU.add).then_inc(sem("gs_ready"), 1)

            def scan1(it, i, first):
                n = it * 4 + i
                dve.wait_ge(sem("pt_free"), n + 1)
                masks_there(it, i, 0)
                if positive(n - 1):
                    dve.wait_ge(sem("back"), n - 1)
                if positive(n):
                    dve.wait_ge(sem("scanned"), n)
                scan(i, n, L[:, i % 2, :], ALU.mult, ALU.max, first).then_inc(sem("scanned"), 1)

            def step1(it, i, first):
                c = it * 4 + i
                pre1(it, i)
                onehots(c * 8, 0, c * 2, 4)
                if not (first and i == 0):
                    scan1(it if i else it - 1, (i - 1) % 4, first and i == 1)
                onehots(c * 8 + 4, 1, c * 2 + 1, 4)
            for i in range(4):
                step1(0, i, True)
            with dve.Fori(1, NIT) as it:
                for i in range(4):
                    step1(it, i, False)
            scan1(NIT - 1, 3, False)

            dve.wait_ge(sem("hist_sum"), 2)
            then(dve.tensor_copy(HC[0:NJ, 0, :], bank(5)[0:NJ, 0:P]))
            then(dve.tensor_copy(HC[0:NJ, 1, :], bank(4)[0:NJ, 0:P]))
            for i in range(2):
                then(dve.tensor_tensor_scan(HC[0:NJ, 2 + i, :], ones[0:NJ, :], HC[0:NJ, i, :], 0.0, ALU.mult, ALU.add))
                then(dve.tensor_copy(hoff[0:NJ, i:i + 1], HC[0:NJ, 2 + i, P - 1:P]))
            dve.sem_inc(sem("row_sums"), 1)
            dve.wait_ge(sem("row_offs"), 1)
            then(dve.tensor_copy(hoff[0:NJ, :], bank(6)[0:NJ, 0:2]))
            for i in range(2):
                then(dve.tensor_tensor(HC[0:NJ, 2 + i, :], HC[0:NJ, 2 + i, :], HC[0:NJ, i, :], ALU.subtract))
                dve.tensor_scalar(HC[0:NJ, 2 + i, :], HC[0:NJ, 2 + i, :], hoff[0:NJ, i:i + 1], None, ALU.add)\
                   .then_inc(sem("starts_ready"), 1)
            dve.wait_ge(sem("starts_in"), 64)

            def row_of(dst, e, w):
                then(dve.tensor_scalar(w, e, float(H), float(-(2 * H - 1)), ALU.is_ge, ALU.mult))
                then(dve.scalar_tensor_tensor(w, e, 2.0, w, ALU.mult, ALU.add))
                return w

            for i in range(2):
                then(dve.tensor_scalar(has[i][:, :], cnt[i][:, :], 1.0, None, ALU.min))
                then(dve.tensor_tensor(na[:, :], beg[i][:, :], cnt[i][:, :], ALU.add))
                then(dve.tensor_scalar(nb[:, :], na[:, :], float(H), None, ALU.is_gt))
                then(dve.scalar_tensor_tensor(span[i][:, :], beg[i][:, :], float(H), nb[:, :], ALU.is_lt, ALU.mult))
                then(dve.tensor_scalar(na[:, :], na[:, :], -1.0, 0.0, ALU.add, ALU.max))
                row_of(None, na[:, :], nb[:, :])
                then(dve.tensor_copy(endrow[i][:, :], nb[:, :]))
            row_of(None, beg[0][:, :], nb[:, :])
            then(dve.tensor_scalar(na[:, :], has[0][:, :], float(-(1 << 22)), float(1 << 22), ALU.mult, ALU.add))
            then(dve.tensor_tensor(nb[:, :], nb[:, :], na[:, :], ALU.add))
            then(dve.tensor_copy(begrow[:, :], nb[:, :]))
            dve.sem_inc(sem("rows_ready"), 1)
            then(dve.tensor_scalar(nb[:, :], cnt[1][:, :], 1.0, None, ALU.max))
            then(dve.reciprocal(rcnt[:, :], nb[:, :]))
            then(dve.tensor_scalar(pen2[:, :], span[1][:, :], BIG, -BIG, ALU.mult, ALU.add))
            dve.tensor_scalar(nb[:, :], cnt[0][:, :], 1.0, None, ALU.add).then_inc(sem("root_in"), 1)
            dve.wait_ge(sem("root_out"), 2)
            then(dve.reciprocal(dinv[:, :], na[:, :]))

            def onehots2(h, s):
                if positive(h - 3):
                    dve.wait_ge(sem("lookups"), h - 3)
                    dve.wait_ge(sem("looked"), h - 3)
                for d in range(2):
                    t = dve.tensor_tensor(OH[:, s // 2, 2 * (s % 2) + d, :, :], rowbc(iota_b[:, :], KC),
                                          bc(KEYS[:, d, bass.ds(h * KC, KC)], [P, KC, P]), ALU.is_equal)
                t.then_inc(sem("oh_ready"), 1)

            def ranks(h, c, i, x):
                dve.wait_ge(sem("src_rows"), h + 1)
                if positive(c - 1):
                    dve.wait_ge(sem("pos_ready"), c - 1)
                for k in range(KC):
                    t = dve.scalar_tensor_tensor(junk_rank[:, x, k, :], bank(4 - 2 * x)[:, k * P:(k + 1) * P],
                                                 RT[:, i, x * KC + k, C_SRC:C_SRC + 1], earlier[:, :],
                                                 ALU.is_equal, ALU.mult, accum_out=inr[:, i % 2, x, k:k + 1])
                t.then_inc(sem("ranked"), 1)

            def look(h, c, i, x):
                dve.wait_ge(sem("lookups"), h + 1)
                if positive(c):
                    dve.wait_ge(sem("pos_ready"), c)
                for k in range(KC):
                    t = dve.scalar_tensor_tensor(junk_look[:, x, k, :], bank(6 + x)[:, k * P:(k + 1) * P],
                                                 1.0, OH[:, i % 2, 2 * x + 1, k, :],
                                                 ALU.mult, ALU.mult, accum_out=lku[:, x, k:k + 1])
                t.then_inc(sem("looked"), 1)

            def pos(it, i):
                c = it * 4 + i
                dve.wait_ge(sem("looked"), c * 2 + 2)
                dve.wait_ge(sem("ranked"), c * 2 + 2)
                if positive(it):
                    dve.wait_ge(sem(f"scattered{i}"), it * 128)
                dve.tensor_tensor(IDX[:, i, :], inr[:, i % 2, :, :].rearrange("p x k -> p (x k)"),
                                  lku[:, :, :].rearrange("p x k -> p (x k)"), ALU.add).then_inc(sem("pos_ready"), 1)

            def scan2(it, i, first):
                n = it * 4 + i + N2
                dve.wait_ge(sem("fwd"), n + 1)
                masks_there(it, i, NIT)
                if positive(it * 4 + i - 1):
                    dve.wait_ge(sem("back2"), it * 4 + i - 1)
                dve.wait_ge(sem("scanned"), n)
                scan(i, n, bank(0), ALU.mult, ALU.add, first).then_inc(sem("scanned"), 1)
                dve.wait_ge(sem("scanned"), n + 1)
                dve.sem_inc(sem("pt_free"), 1)

            def step2(it, i, first, last):
                c = it * 4 + i
                h = c * 2
                end = last and i == 3
                scan2(it, i, first and i == 0)
                if not (first and i == 0):
                    look(h - 1, c - 1, (i - 1) % 4, 1)
                    pos(it if i else it - 1, (i - 1) % 4)
                if not end:
                    onehots2(h + 2, (i * 2 + 2) % 4)
                ranks(h + 1, c, i, 1)
                look(h, c, i, 0)
                if not end:
                    onehots2(h + 3, (i * 2 + 3) % 4)
                    ranks(h + 2, c + 1, (i + 1) % 4, 0)
            dve.wait_ge(sem("fill_zero"), 16 * NZ)
            onehots2(0, 0)
            onehots2(1, 1)
            ranks(0, 0, 0, 0)
            for i in range(4):
                step2(0, i, True, False)
            for i in range(4):
                step2(1, i, False, False)
            with dve.Fori(2, NIT - 1) as it:
                for i in range(4):
                    step2(it, i, False, False)
            for i in range(4):
                step2(NIT - 1, i, False, True)
            look(2 * NCH - 1, NCH - 1, 3, 1)
            pos(NIT - 1, 3)

            for i in range(4):
                dve.wait_ge(sem(f"scattered{i}"), NIT * 128)
            then(dve.memset(KS[0][:, 0:1], -1.0))

            def step3(it, i, first):
                c = it * 4 + i
                s = i % 2
                start = first and i == 0
                dve.wait_ge(sem("ks_ready"), c + 1)
                if positive(c):
                    dve.wait_ge(sem("ks_carry"), c)
                if positive(c - 1):
                    dve.wait_ge(sem("mp_ready"), c - 1)
                if not first or i >= 2:
                    dve.wait_ge(sem(f"same_src{s}"), (c - i + i // 2 * 2) * 16)
                dve.wait_ge(sem("scanned"), c + N3 - 1)
                dve.tensor_tensor(MK[s], KS[s][:, 1:CE + 1], KS[s][:, 0:CE], ALU.is_equal).then_inc(sem("mk_ready"), 1)
                dve.wait_ge(sem(f"rec_in{i}"), it * 64 + 64)
                if not first or i >= 2:
                    dve.wait_ge(sem(f"dst_out{s}"), (c - i + i // 2 * 2) * 8)
                dve.tensor_copy(IDX[:, s, :], RD[:, i, :].rearrange("p (q d) -> p q d", d=D)[:, :, C_DST - D0]).then_inc(sem("dst_ready"), 1)
                dve.wait_ge(sem("mk_ready"), c + 1)
                dve.wait_ge(sem("rec_used"), c + 1)
                if positive(2 * c - 2):
                    dve.wait_ge(sem("back3"), 2 * c - 2)
                if positive(c):
                    dve.wait_ge(sem("scan2"), c)
                dve.tensor_tensor_scan(S2[s], MK[s], bank(2 + 5 * s), 0.0 if start else S2[1 - s][:, CE - 1:CE],
                                       ALU.mult, ALU.add).then_inc(sem("scan2"), 1)
                dve.wait_ge(sem("l3r"), c + 1)
                dve.wait_ge(sem("back"), c + N3 - NCH - 1)
                dve.wait_ge(sem("scanned"), c + N3)
                dve.tensor_tensor_scan(S[:, s, :], MK[s], L[:, s, :], 0.0 if start else S[:, 1 - s, CE - 1:CE],
                                       ALU.mult, ALU.max).then_inc(sem("scanned"), 1)
                dve.wait_ge(sem("mp_ready"), c + 1)
                if positive(c):
                    dve.wait_ge(sem("scan3"), c)
                dve.tensor_tensor_scan(S3[s], MP[s], bank(2 + 5 * s), 0.0 if start else S3[1 - s][:, CE - 1:CE],
                                       ALU.add, ALU.max).then_inc(sem("scan3"), 1)
            for i in range(4):
                step3(0, i, True)
            with dve.Fori(1, NIT) as it:
                for i in range(4):
                    step3(it, i, False)

            for i in range(2):
                dve.wait_ge(sem(f"runs_e_out{i}"), 8 * NCH)
                dve.wait_ge(sem(f"same_src{i}"), 16 * NCH)
                dve.wait_ge(sem(f"dst_out{i}"), 8 * NCH)
            dve.wait_ge(sem("carry"), 16)
            K3 = 3 * AD + 1
            A0, W0 = AD - 4, AD + 1
            u36 = t1.rearrange("p (j d) -> p j d", d=36)
            s36 = t2.rearrange("p (j d) -> p j d", d=36)
            m32 = t3.rearrange("p (j d) -> p j d", d=AD)

            def gather3(g, s, per, base):
                j = g * GT
                dg = DG[s].rearrange("p (j d) -> p j d", d=P)
                z = Z[:, s, 0:GT * K3].rearrange("p (j d) -> p j d", d=K3)
                hs = has[1][:, bass.ds(j, GT)]
                sp_ = span[1][:, bass.ds(j, GT)]
                step = Steps("l3_order", base)
                dve.wait_ge(sem(f"dends{s}"), per)
                step(dve.tensor_tensor(u36, rowbc(CR[:, A0:D], GT), bc(sp_, [P, GT, 36]), ALU.mult))
                step(dve.tensor_tensor(s36, dg[:, :, A0:D], bc(hs, [P, GT, 36]), ALU.mult))
                step(dve.tensor_tensor(s36, s36, u36, ALU.add))
                if positive(g - 1):
                    dve.wait_ge(sem("z3t"), g - 1)
                dve.tensor_tensor(wsum[:, bass.ds(j, GT), :], s36[:, :, W0:W0 + 2], bc(hs, [P, GT, 2]), ALU.mult)
                dve.tensor_tensor(z[:, :, 0:AD], s36[:, :, 0:AD], bc(hs, [P, GT, AD]), ALU.mult)
                dve.tensor_tensor(z[:, :, 2 * AD:3 * AD], s36[:, :, 0:AD], bc(rcnt[:, bass.ds(j, GT)], [P, GT, AD]), ALU.mult)
                dve.tensor_scalar(z[:, :, 3 * AD:K3], bc(ucol[:, 0:1], [P, GT, 1]), 1.0, None, ALU.mult)
                step(dve.tensor_tensor(m32, rowbc(CR[:, D + A0:D + A0 + AD], GT), bc(pen2[:, bass.ds(j, GT)], [P, GT, AD]), ALU.add))
                step(dve.tensor_tensor(m32, m32, dg[:, :, D + A0:D + A0 + AD], ALU.max))
                step(dve.tensor_tensor(z[:, :, AD:2 * AD], m32, bc(hs, [P, GT, AD]), ALU.mult))
                assert step.k == 6
                dve.sem_inc(sem("z3_ready"), 1)
                dve.sem_inc(sem("d_used"), 1)

            def store3(g):
                dve.wait_ge(sem("o3"), g + 1)
                dve.tensor_tensor(group(L3O, g), zo, rowbc(b2[:, :], GT), ALU.add).then_inc(sem("l3_done"), 1)
            gather3(0, 0, 16 * GT, 0)
            gather3(1, 1, 16 * GT, 6)
            store3(0)
            with dve.Fori(1, NG // 2) as g:
                gather3(g * 2, 0, g * (16 * GT) + 16 * GT, g * 12)
                store3(g * 2 - 1)
                gather3(g * 2 + 1, 1, g * (16 * GT) + 16 * GT, g * 12 + 6)
                store3(g * 2)
            store3(NG - 1)
            dve.wait_ge(sem("l3_done"), NG)
            dve.sem_inc(sem("carry_used"), 1)

            def make_b(g, s):
                j = g * GT
                ga, gb = group(AG, g), group(T, g)
                step = Steps("l0_order", g * 6)
                cc = f3(CARG)
                dve.wait_ge(sem("zo_used"), g + (QB - 1))
                for t, i, row in ((gb, 0, CR[:, 0:D]), (ga, 1, CR2[:, :])):
                    step(dve.tensor_tensor(cc, rowbc(row, GT), bc(span[i][:, bass.ds(j, GT)], [P, GT, D]), ALU.mult))
                    step(dve.tensor_tensor(t, t, bc(has[i][:, bass.ds(j, GT)], [P, GT, D]), ALU.mult))
                    step(dve.tensor_tensor(t, t, cc, ALU.max))
                z = z3(s, 2 * D)
                dve.tensor_scalar(z[:, :, 0:D], group(Hn, g), 1.0, None, ALU.mult)
                return dve.tensor_tensor(z[:, :, D:2 * D], ga, gb, ALU.max)

            dve.wait_ge(sem("carry"), 48)
            for s in range(2):
                dve.wait_ge(sem(f"ends{s}"), 16 * GT * NG)

            def post_b(g):
                cc = f3(CARG)
                step = Steps("l0_post", g * 2)
                step(dve.tensor_tensor(cc, zo, rowbc(fb[:, :], GT), ALU.add))
                step(dve.tensor_scalar(cc, cc, 0.0, None, ALU.max))
                return dve.tensor_tensor(group(X, g), group(X, g), cc, ALU.add)
            project(QB, make_b, post_b)
            dve.sem_inc(sem("carry_used"), 1)
            norm(3)
            dve.sem_inc(sem("h_ready"), 1)

            def gather_pass(n0, done):
                def step(it, i, first):
                    n = it * 4 + i + n0
                    dve.wait_ge(sem("fwd"), n + 1 - NCH)
                    masks_there(it, i, done)
                    dve.wait_ge(sem("back"), n - 1 - NCH)
                    dve.wait_ge(sem("scanned"), n)
                    scan(i, n, bank(i % 2), ALU.mult, ALU.add, first and i == 0).then_inc(sem("scanned"), 1)
                    dve.wait_ge(sem("scanned"), n + 1)
                    dve.sem_inc(sem("pt_free"), 1)
                for i in range(4):
                    step(0, i, True)
                with dve.Fori(1, NIT) as it:
                    for i in range(4):
                        step(it, i, False)

            def ends_sum(g, s, per, i, base, rest):
                j = g * GT
                ga, cc = group(AG, g), f3(CARG)
                step = Steps("ends_order", base)
                dve.wait_ge(sem(f"ends{s}"), per)
                step(dve.tensor_tensor(cc, rowbc(CR[:, 0:D], GT), bc(span[i][:, bass.ds(j, GT)], [P, GT, D]), ALU.mult))
                step(dve.tensor_tensor(ga, ga, bc(has[i][:, bass.ds(j, GT)], [P, GT, D]), ALU.mult))
                step(dve.tensor_tensor(ga, ga, cc, ALU.add))
                rest(g, ga, step)
                return step.k

            with dve.Fori(0, LAYERS) as l:
                dve.wait_ge(sem("layer_in"), l * 64 + 64)
                dve.sem_inc(sem("dve_turns"), 1)
                project(QC + l * NG,
                        lambda g, s: dve.tensor_scalar(z3(s, D), group(Hn, g), 1.0, None, ALU.mult),
                        lambda g: dve.tensor_tensor(group(T, g), zo, bc(dinv[:, bass.ds(g * GT, GT)], [P, GT, D]), ALU.mult))
                dve.sem_inc(sem("t_ready"), 1)
                gather_pass(N4 + l * NCH, (l + 2) * NIT)
                dve.wait_ge(sem("carry"), l * 16 + 64)
                dve.sem_inc(sem("dve_turns"), 1)

                def rest(g, ga, step):
                    j = g * GT
                    step(dve.tensor_tensor(ga, ga, group(T, g), ALU.add))
                    step(dve.tensor_tensor(ga, ga, bc(dinv[:, bass.ds(j, GT)], [P, GT, D]), ALU.mult))
                    step(dve.tensor_tensor(ga, ga, rowbc(lrows[:, 0, :], GT), ALU.add))
                    step(dve.tensor_tensor(ga, ga, bc(valid[:, bass.ds(j, GT)], [P, GT, D]), ALU.mult))
                    step(dve.tensor_reduce(gsum[:, bass.ds(g, 1)], ga, AX.XY, ALU.add))
                with dve.Fori(0, NG // 2) as g:
                    per = (g + l * (NG // 2)) * (16 * GT) + 16 * GT * (NG + 1)
                    k = ends_sum(g * 2, 0, per, 0, (g + l * (NG // 2)) * 16, rest)
                    k = ends_sum(g * 2 + 1, 1, per, 0, (g + l * (NG // 2)) * 16 + 8, rest)
                    assert k == 8
                dve.sem_inc(sem("carry_used"), 1)
                step = Steps("layer_order", l * 6)
                scale = 1.0 / (n_nodes * D)
                dve.tensor_reduce(st[:, 0:1], gsum[:, :], AX.X, ALU.add).then_inc(sem("part_sum"), 1)
                dve.wait_ge(sem("total"), l * 2 + 1)
                step(dve.tensor_scalar(st[:, 2:3], bank(4)[:, 0:1], scale, None, ALU.mult))
                dve.scalar_tensor_tensor(v3(Hn), v3(AG), st[:, 2:3], bc(valid[:, :], [P, NJ, D]),
                                         ALU.subtract, ALU.mult).then_inc(sem("dev_ready"), 1)
                dve.wait_ge(sem("sq_done"), l + 1)
                dve.sem_inc(sem("part_sum"), 1)
                dve.wait_ge(sem("total"), l * 2 + 2)
                dve.tensor_scalar(st[:, 3:4], bank(4)[:, 0:1], scale, EPS, ALU.mult, ALU.add).then_inc(sem("var_ready"), 1)
                dve.wait_ge(sem("std_ready"), l + 1)
                step(dve.reciprocal(st[:, 5:6], st[:, 4:5]))
                step(dve.tensor_scalar(lnwr[:, :], lrows[:, 1, :], st[:, 5:6], None, ALU.mult))
                step(dve.tensor_tensor(v3(Hn), v3(Hn), rowbc(lnwr[:, :], NJ), ALU.mult))
                step(dve.tensor_tensor(v3(Hn), v3(Hn), rowbc(lrows[:, 2, :], NJ), ALU.add))
                step(dve.tensor_scalar(Hn[:, :], Hn[:, :], 0.0, None, ALU.max))
                dve.sem_inc(sem("h_ready"), 1)
            then(dve.tensor_tensor(X[:, :], X[:, :], Hn[:, :], ALU.add))

            norm(4)
            project(QD, lambda g, s: dve.tensor_scalar(z3(s, D), group(Hn, g), 1.0, None, ALU.mult),
                    lambda g: dve.tensor_scalar(group(AG, g), zo, 0.0, None, ALU.max))

            def make_e(g, s):
                z = z3(s, D + 2)
                j = g * GT
                dve.tensor_scalar(z[:, :, 0:1], vpos[:, bass.ds(j, GT)].unsqueeze(2), 1.0, None, ALU.mult)
                dve.tensor_scalar(z[:, :, 1:2], vneg[:, bass.ds(j, GT)].unsqueeze(2), 1.0, None, ALU.mult)
                return dve.tensor_scalar(z[:, :, 2:D + 2], group(AG, g), 1.0, None, ALU.mult)
            project(QE, make_e, lambda g: dve.tensor_scalar(group(T, g), zo, 1.0, None, ALU.mult))
            dve.sem_inc(sem("t_ready"), 1)
            then(dve.tensor_tensor(v3(Hn), bc(vin[:, :], [P, NJ, D]), rowbc(w1row[:, :], NJ), ALU.mult))
            then(dve.scalar_tensor_tensor(Hn[:, :], Hn[:, :], 0.0, AG[:, :], ALU.max, ALU.add))
            dve.wait_ge(sem("table_out"), 16 * (LAYERS + 2))
            then(dve.tensor_tensor(v3(T), bc(wsum[:, :, 0], [P, NJ, D]), rowbc(rcd[:, 0, :], NJ), ALU.mult))
            then(dve.tensor_tensor(v3(AG), bc(wsum[:, :, 1], [P, NJ, D]), rowbc(rcd[:, 1, :], NJ), ALU.mult))
            then(dve.tensor_tensor(T[:, :], T[:, :], AG[:, :], ALU.add))
            dve.sem_inc(sem("he_ready"), 1)
            gather_pass(N8, 6 * NIT)
            dve.wait_ge(sem("carry"), 16 * (LAYERS + 4))

            def rest2(g, ga, step):
                step(dve.tensor_tensor(ga, ga, group(T, g), ALU.add))
                step(dve.scalar_tensor_tensor(ga, ga, 0.0, group(Hn, g), ALU.max, ALU.add))
                step(dve.scalar_tensor_tensor(ga, ga, 0.0, group(X, g), ALU.max, ALU.add))
                step(dve.tensor_tensor(group(X, g), ga, group(L3O, g), ALU.add))
            base = LAYERS * NG * 8
            with dve.Fori(0, NG // 2) as g:
                per = g * (16 * GT) + 16 * GT * (3 * NG + 1)
                ends_sum(g * 2, 0, per, 1, g * 14 + base, rest2)
                ends_sum(g * 2 + 1, 1, per, 1, g * 14 + (base + 7), rest2)
            dve.sem_inc(sem("x_ready"), 1)


def ends_layer(pool, l, sem, dst, rows, idx, NG, GT):
    for g in range(NG):
        s = g % 2
        pool.wait_ge(sem(f"ends{s}"), (l * (NG // 2) + (NG + g // 2)) * (16 * GT))
        pool.sem_inc(sem("pool_turns"), 1)
        for k in range(GT):
            j = g * GT + k
            pool.indirect_dma_start(dst[:, j * D:(j + 1) * D], None, rows,
                                    bass.IndirectOffsetOnAxis(ap=idx[:, j:j + 1], axis=0)).then_inc(sem(f"ends{s}"), 16)


def kernel(**inputs):
    import numpy as np
    import concourse.bacc as bacc
    from concourse.bass_utils import run_bass_kernel_spmd as run

    i = {k: np.asarray(v) for k, v in inputs.items()}
    n, e = i["x"].shape[0], i["src"].shape[0]
    NJ, TILES = sizes(n, e)
    NP, EP = NJ * P, TILES * P

    def pad(x, rows, value=0):
        return np.concatenate([x, np.full((rows - x.shape[0],) + x.shape[1:], value, x.dtype)])

    def chunked(x):
        return np.ascontiguousarray(x.reshape(2, TILES // (2 * KC), KC, P).transpose(3, 1, 2, 0).reshape(P, TILES))

    src, dst = pad(i["src"], EP, NP - 1), pad(i["dst"], EP, NP - 1)
    w4_t = i["L2_gnn_W4"].T
    arrays = {
        "x": pad(i["x"], NP), "src_q": chunked(src), "dst_q": chunked(dst),
        "dst_ext": np.concatenate([np.full(1, -1, dst.dtype), dst])[None],
        "ew_q": chunked(pad(i["edge_weight"], EP)), "attr": pad(i["edge_attr_32"], EP),
        "v": pad(i["node_vec1"], NP), "poolw_t": i["L0_gnn_pool_w"].T, "pool_b": i["L0_gnn_pool_b"][:, None],
        "finalw_t": i["L0_gnn_final_w"].T, "final_b": i["L0_gnn_final_b"][None],
        "coef": i["L0_gnn_coef"].reshape(1, 1), "ws": i["L1_gnn_Ws"].reshape(-1, D),
        "bs": i["L1_gnn_bs"], "lnw": i["L1_gnn_ln_w"], "lnb": i["L1_gnn_ln_b"],
        "w1": i["L2_gnn_W1"], "w2": i["L2_gnn_W2"], "w3_t": i["L2_gnn_W3"].T, "w4_t": w4_t,
        "u": i["L3_gnn_u"][0:1], "l3w1": i["L3_gnn_W1"], "l3b1": i["L3_gnn_b1"][:, None],
        "l3w2": i["L3_gnn_W2"], "l3b2": i["L3_gnn_b2"][None],
    }
    arrays = {k: np.ascontiguousarray(v) for k, v in arrays.items()}
    nc = bacc.Bacc("TRN2", target_bir_lowering=False, num_devices=1)
    aps = {k: nc.dram_tensor(f"in_{k}", v.shape, mybir.dt.from_np(v.dtype), kind="ExternalInput").ap()
           for k, v in arrays.items()}
    out = nc.dram_tensor("out_x", (NP, D), F32, kind="ExternalOutput").ap()
    gnn_kernel(nc, n, e, aps, out)
    r = run(nc, [{f"in_{k}": v for k, v in arrays.items()}], core_ids=[0])
    return r.results[0]["out_x"][:n]
```

```python
import concourse.bass as bass
from concourse import mybir
from contextlib import ExitStack

F32 = mybir.dt.float32
BF16 = mybir.dt.bfloat16
I32 = mybir.dt.int32
ALU = mybir.AluOpType
ACT = mybir.ActivationFunctionType
AX = mybir.AxisListType
D = 64
AD = 32
P = 128
GT = 7
KC = 4
CE = KC * P
RW = D + AD + 4
C_DST, C_WP, C_WN, C_SRC = 96, 97, 98, 99
D0 = RW - D
A0 = D - AD - 4
NS = AD + 4
EW = NS + AD
BIG = 3.4028234e38
SELF = 1e33
EPS = 1e-5
LAYERS = 4


def sizes(n_nodes, n_edges):
    nj = -(-n_nodes // (P * GT * 2)) * GT * 2
    tiles = -(-n_edges // (P * KC * 8)) * KC * 8
    return nj, tiles


def positive(value):
    return not isinstance(value, int) or value > 0


def gnn_kernel(nc, n_nodes, n_edges, a, out):
    NJ, TILES = sizes(n_nodes, n_edges)
    NP = NJ * P
    EP = TILES * P
    H = EP // 2
    NCH = TILES // (2 * KC)
    NIT = NCH // 4
    NG = NJ // GT
    GW = GT * D
    assert NP > n_nodes or EP == n_edges
    assert NJ <= P and NIT >= 3 and LAYERS * NIT == NCH

    def dram(name, shape, dt):
        return nc.dram_tensor(name, shape, dt, kind="Internal").ap()

    table = dram("node_table", (NP, D), F32)
    fill = dram("fill_rows", (H, 2 * D), F32)
    rec = dram("records", (EP, RW), F32)
    runs = dram("runs", (H, 2 * D), F32)
    runs_l0 = dram("runs_l0", (H, 2 * D), F32)
    runs_e = dram("runs_e", (H, 2 * EW), F32)
    same_dst = dram("same_dst", (2, H), BF16)
    same_src = dram("same_src", (2, H), BF16)
    dst_by_src = dram("dst_by_src", (P, TILES), I32)
    counts = dram("counts", (2, NP), F32)
    starts = dram("starts", (2, NP), F32)

    ctx = ExitStack()
    with ctx:
        def sb(name, shape, dt=F32):
            return ctx.enter_context(nc.sbuf_tensor(name, shape, dt))

        sems = {}

        def sem(name):
            if name not in sems:
                sems[name] = ctx.enter_context(nc.semaphore(name))
            return sems[name]

        X = sb("X", [P, NJ * D])
        Hn = sb("Hn", [P, NJ * D])
        T = sb("T", [P, NJ * D])
        AGB = sb("AG", [P, max(NJ * D, 3 * TILES + 8)])
        AG = AGB[:, 0:NJ * D]
        EA = sb("EA", [P, max(4 * TILES, NJ * EW, 3 * CE + 8)])

        def v3(t, j0=0, n=NJ):
            return t[:, j0 * D:(j0 + n) * D].rearrange("p (j d) -> p j d", d=D)

        def group(t, g):
            return t[:, bass.ds(g * GW, GW)].rearrange("p (j d) -> p j d", d=D)

        s_q = EA[:, 0:TILES]
        pen_q = EA[:, TILES:2 * TILES]
        w_q = EA[:, 2 * TILES:3 * TILES]
        srcf_q = EA[:, 3 * TILES:4 * TILES]
        KEYS = AGB[:, 0:2 * (TILES + KC)].bitcast(BF16).rearrange("p (i t) -> p i t", i=4)
        dstf_q = AGB[:, 2 * (TILES + KC):2 * (TILES + KC) + TILES]
        SI = T[:, 0:TILES].bitcast(I32)
        DI = T[:, TILES:2 * TILES].bitcast(I32)
        tmp_i = dstf_q.bitcast(I32)

        G = sb("G", [P, 4, KC * P])
        M = sb("M", [P, 2, 2 * CE], BF16)
        L = sb("L", [P, 2, CE])
        S = sb("S", [P, 2, CE])
        R = sb("R", [P, 4, CE])
        RT = sb("RT", [P, 4, 8, RW])
        RTf = RT[:, :, :, :].rearrange("p s q r -> p (s q r)")
        Gs = RTf[:, 0:2 * CE].rearrange("p (s e) -> p s e", s=2)
        RD = RT[:, :, :, :].rearrange("p s q r -> p s (q r)")[:, :, 0:CE]
        IDX = sb("IDX", [P, 4, 8], I32)
        OH = sb("OH", [P, 2, 4, KC, P], BF16)
        OHTs = R[:, 0:2, :]
        Cs = R[:, 2, 0:2 * P].rearrange("p (s l) -> p s l", s=2)
        Lf = L[:, :, :].rearrange("p s e -> p (s e)")
        junk_rank = Lf.rearrange("p (x k e) -> p x k e", x=2, k=KC)
        Gf = G[:, :, :].rearrange("p s e -> p (s e)")
        Rf = R[:, :, :].rearrange("p s e -> p (s e)")
        DX = Gf[:, 0:TILES + 1].bitcast(I32)
        MD = Rf[:, 0:TILES // 2].bitcast(BF16)
        assert TILES < 4 * CE
        inr = sb("inr", [P, 2, 2, KC])
        lku = sb("lku", [P, 2, KC])
        off = [0]

        def ea(cols):
            o = off[0]
            off[0] += cols
            return EA[:, o:o + cols]
        KS = [ea(CE + 4) for _ in range(2)]
        MK = [ea(CE // 2).bitcast(BF16) for _ in range(2)]
        ends_e = EA[:, 0:NJ * EW].rearrange("p (j d) -> p j d", d=EW)
        rt_off = [0]

        def rtf(cols):
            o = rt_off[0]
            rt_off[0] += cols
            return RTf[:, o:o + cols]
        E_WIN = rtf(CE)
        E_MASK = rtf(CE // 2).bitcast(BF16)
        E_PEN = rtf(CE)
        E_SUM, E_MAX = rtf(CE), rtf(CE)
        E_OUT = rtf(2 * KC * EW)
        assert rt_off[0] <= 4 * 8 * RW
        E_KEEP = sb("E_KEEP", [P, 2])
        Z = sb("Z", [P, 2, GT * P])
        junk_look = Z[:, :, :].rearrange("p a b -> p (a b)")[:, 0:8 * P].rearrange("p (x k e) -> p x k e", x=2, k=KC)
        ZTs = Gf[:, 0:GT * P]
        rt_off[0] = 0
        Z3Ts, HS = rtf(GT * P), rtf(GT * P)
        t1, t2, t3 = rtf(GT * NS), rtf(GT * NS), rtf(GT * AD)
        CARG = L[:, 0, 0:GW]
        CR = sb("CR", [P, D])
        CR2 = sb("CR2", [P, D])
        CRE = sb("CRE", [P, EW])

        def node(name, dt=F32):
            return sb(name, [P, NJ], dt)

        cnt = [node("cnt_dst"), node("cnt_src")]
        beg = [node("beg_dst"), node("beg_src")]
        has = [node("has_dst"), node("has_src")]
        span = [node("span_dst"), node("span_src")]
        endrow = [node("endrow_dst", I32), node("endrow_src", I32)]
        begrow = node("begrow", I32)
        dinv = node("dinv")
        rcnt = node("rcnt")
        pen2 = node("pen2")
        valid = node("valid")
        vpos = node("vpos")
        vneg = node("vneg")
        vin = node("vin")
        wsum = sb("wsum", [P, NJ, 2])
        na = node("na")
        nb = node("nb")
        nd = node("nd")
        gsum = sb("gsum", [P, NG])
        st = sb("st", [P, 8])
        iota_i = sb("iota_i", [P, P], I32)
        pidx_i = sb("pidx_i", [P, 1], I32)
        iota_f = sb("iota_f", [P, P])
        iota_b = sb("iota_b", [P, P], BF16)
        pidx = sb("pidx", [P, 1])
        ident = sb("ident", [P, P])
        ident_b = sb("ident_b", [P, P], BF16)
        earlier = sb("earlier", [P, P])
        below = sb("below", [P, P])
        ones = sb("ones", [P, P])
        zero_rows = Z[:, :, :].rearrange("p a b -> p (a b)")
        HC = sb("HC", [P, 4, P])
        hoff = sb("hoff", [P, 2])
        dh = sb("dh", [1, 1], I32)
        poolw = sb("poolw", [D, D])
        finalw = sb("finalw", [2 * D, D])
        w3 = sb("w3", [D, D])
        w4 = sb("w4", [D, 3, D])
        w4c = sb("w4c", [D + 2, D])
        l3w1 = sb("l3w1", [3 * AD + 1, P])
        l3w2 = sb("l3w2", [P, D])
        l3b1 = sb("l3b1", [P, 1])
        wl = sb("wl", [D, D])
        lrows = sb("lrows", [P, 3, D])
        lnwr = sb("lnwr", [P, D])
        poolb = sb("poolb", [P, 1])
        fb = sb("fb", [P, D])
        b2 = sb("b2", [P, D])
        w1row = sb("w1row", [P, D])
        w12c = sb("w12c", [D, 2])
        w12r = sb("w12r", [D, 4])
        rcd = sb("rcd", [P, 2, D])
        coef = sb("coef", [P, 1])
        ucol = sb("ucol", [P, 1])

        PS = ctx.enter_context(nc.psum_tensor("PS", [P, 8 * 512], F32))

        def bank(i, n=1):
            return PS[:, i * 512:(i + n) * 512]

        def bc(ap, shape):
            while len(ap.shape) < len(shape):
                ap = ap.unsqueeze(len(ap.shape))
            return ap.broadcast_to(shape)

        def rowbc(row, mid):
            return row.unsqueeze(1).broadcast_to([P, mid, row.shape[1]])

        def dbc(ap, n):
            return bass.AP(tensor=ap.tensor, offset=ap.offset, ap=[[0, n], [1, ap.shape[-1]]])

        runs64 = runs.rearrange("r (h d) -> (r h) d", d=D)
        runs_l064 = runs_l0.rearrange("r (h d) -> (r h) d", d=D)
        runs_e_rows = runs_e.rearrange("r (h d) -> (r h) d", d=EW)
        fill64 = fill.rearrange("r (h d) -> (r h) d", d=D)

        block = ctx.enter_context(nc.Block())
        W = {"params": 0}
        N1, N2, N3, N4, N8 = 0, NCH, 2 * NCH, 3 * NCH, 7 * NCH
        QA, QB, QC, QD, QE = 0, NG, 2 * NG, 6 * NG, 7 * NG
        ZF = 2 * GT * P
        FW = H * 2 * D // P
        NZ = -(-FW // ZF)

        @block.sync
        def _(sp):
            def load(dst, src):
                sp.dma_start(dst, src).then_inc(sem("params"), 16)
                W["params"] += 16

            load(X[:, :], a["x"].rearrange("(p j) d -> p (j d)", p=P))
            load(SI, a["src_q"])
            load(DI, a["dst_q"])
            load(DX, bass.AP(tensor=a["dst_ext"].tensor, offset=0, ap=[[TILES, P], [1, TILES + 1]]))
            load(w_q, a["ew_q"])
            load(poolw[:, :], a["poolw_t"])
            load(finalw[:, :], a["finalw_t"])
            load(w3[:, :], a["w3_t"])
            for i in range(3):
                load(w4[:, i, :], a["w4_t"][i * D:(i + 1) * D, :])
            load(w4c[2:D + 2, :], a["w4_t"][2 * D:3 * D, :])
            load(l3w1[:, :], a["l3w1"])
            load(l3w2[:, :], a["l3w2"])
            load(l3b1[:, :], a["l3b1"])
            load(poolb[0:D, :], a["pool_b"])
            load(poolb[D:P, :], a["pool_b"])
            load(fb[:, :], dbc(a["final_b"], P))
            load(b2[:, :], dbc(a["l3b2"], P))
            load(w1row[:, :], dbc(a["w1"].rearrange("d o -> o d"), P))
            load(w12c[:, 0:1], a["w1"])
            load(w12c[:, 1:2], a["w2"])
            load(coef[:, :], dbc(a["coef"], P))
            load(ucol[:, :], dbc(a["u"], P))
            load(vin[:, :], a["v"].rearrange("(p j) o -> p (j o)", p=P))

            def table_out(n):
                sp.wait_ge(sem("t_ready"), n)
                sp.sem_inc(sem("sp_turns"), 1)
                sp.dma_start(table.rearrange("(p j) d -> p (j d)", p=P), T[:, :]).then_inc(sem("table_out"), 16)

            sp.wait_ge(sem("md_ready"), 1)
            sp.dma_start(same_dst.rearrange("h (q t) -> (h q) t", t=TILES), MD).then_inc(sem("same_dst"), 16)
            table_out(1)
            def masks_in(masks, c, slot, lo):
                if positive(lo):
                    sp.wait_ge(sem("scanned"), lo)
                sp.sem_inc(sem("sp_turns"), 1)
                for h in range(2):
                    src = masks[h:h + 1, bass.ds(c * CE, 2 * CE)]
                    sp.dma_start(M[h * D:(h + 1) * D, slot, :],
                                 src.broadcast_to([D, 2 * CE])).then_inc(sem(f"masks_in{slot}"), 16)

            def runs_out(dst, c, i, n):
                sp.wait_ge(sem("r_ready"), n + 1)
                sp.sem_inc(sem("sp_turns"), 1)
                rows = dst[bass.ds(c * CE, CE), :].rearrange("(k p) d -> p k d", p=P)
                sp.dma_start(rows, R[:, i, :].rearrange("p (k d) -> p k d", k=KC)).then_inc(sem(f"runs_out{i}"), 16)

            def attr_out(d):
                sp.wait_ge(sem("e_ready"), d + 1)
                sp.sem_inc(sem("sp_turns"), 1)
                rows = runs_e[bass.ds(d * CE, CE), :].rearrange("(k p) d -> p k d", p=P)
                sp.dma_start(rows, E_OUT.rearrange("p (k d) -> p k d", k=KC)).then_inc(sem("e_out"), 16)
                sp.wait_ge(sem("e_out"), d * 16 + 16)
                sp.sem_inc(sem("sp_turns"), 1)

            def attr_in(d):
                for h in range(2):
                    rows = rec[bass.ds(d * CE + h * H, CE), :].rearrange("(k p) d -> p k d", p=P)
                    sp.dma_start(E_WIN.rearrange("p (k h d) -> p k h d", k=KC, h=2)[:, :, h, :],
                                 rows[:, :, D0:RW]).then_inc(sem("e_in"), 16)
                    sp.dma_start(E_MASK[h * D:(h + 1) * D, :],
                                 same_src[h:h + 1, bass.ds(d * CE, CE)].broadcast_to([D, CE])).then_inc(sem("e_in"), 16)

            def gather_pass(masks, idx, dst, n0, g0, first_of_sem, attr=None):
                r0 = n0 if isinstance(n0, int) and n0 == 0 else n0 - NCH
                """Indices and masks in, running rows out, of a pass that gathers."""
                def step(it, i, lead):
                    c = it * 4 + i
                    if lead != "last":
                        if lead != "first":
                            sp.wait_ge(sem(f"{g0}{i}"), (it + first_of_sem) * 128)
                            sp.sem_inc(sem("sp_turns"), 1)
                        sp.dma_start(IDX[:, i, :], idx[:, bass.ds(c * 8, 8)]).then_inc(sem(f"idx_in{i}"), 16)
                        if i % 2 == 0:
                            masks_in(masks, c, i // 2, c + n0 - 2)
                    if lead != "first":
                        runs_out(dst, c - 4, i, c - 4 + r0)
                    if attr is not None and i == 3:
                        if lead != "first":
                            attr_out(attr + (it - 1))
                        if lead != "last":
                            attr_in(attr + it)
                for i in range(4):
                    step(0, i, "first")
                with sp.Fori(1, NIT) as it:
                    for i in range(4):
                        step(it, i, "mid")
                for i in range(4):
                    step(NIT, i, "last")

            gather_pass(same_dst, a["src_q"], runs_l0, N1, "gath_a", 0)

            for i in range(2):
                sp.wait_ge(sem("starts_ready"), i + 1)
                sp.dma_start(counts[i:i + 1, :].rearrange("o (h l) -> (o h) l", l=P), HC[0:NJ, i, :]).then_inc(sem("starts_out"), 16)
                sp.dma_start(starts[i:i + 1, :].rearrange("o (h l) -> (o h) l", l=P), HC[0:NJ, 2 + i, :]).then_inc(sem("starts_out"), 16)
            sp.wait_ge(sem("starts_out"), 64)
            for i in range(2):
                sp.dma_start(cnt[i][:, :], counts[i:i + 1, :].rearrange("o (p j) -> (o p) j", p=P)).then_inc(sem("starts_in"), 16)
                sp.dma_start(beg[i][:, :], starts[i:i + 1, :].rearrange("o (p j) -> (o p) j", p=P)).then_inc(sem("starts_in"), 16)
            sp.dma_start(dh[0:1, 0:1], a["dst_ext"][:, H + 1:H + 2]).then_inc(sem("dh_in"), 16)
            sp.wait_ge(sem("dh_in"), 16)
            node_h = sp.value_load(dh[0:1, 0:1], min_val=0, max_val=NP - 1)
            sp.wait_ge(sem("filled"), 16 * NJ)
            sp.dma_start(fill64[1:2, :], table[bass.ds(node_h, 1), :]).then_inc(sem("fill_b"), 16)
            sp.wait_ge(sem("fill_b"), 16)

            def step2(it, i, first):
                c = it * 4 + i
                sp.wait_ge(sem("fwd"), c + N2 - 3)
                sp.sem_inc(sem("sp_turns"), 1)
                rows = fill[bass.ds(c * CE, CE), :].rearrange("(k p) d -> p k d", p=P)
                sp.dma_start(G[:, i, :].rearrange("p (k d) -> p k d", k=KC), rows).then_inc(sem(f"fill_in{i}"), 16)
                if i % 2 == 0:
                    masks_in(same_dst, c, i // 2, c + N2 - 2)
                if not first:
                    sp.wait_ge(sem(f"scattered{i}"), it * 128)
                    sp.sem_inc(sem("sp_turns"), 1)
                rt = RT[:, i, :, :].rearrange("p (k h) r -> p k h r", h=2)
                for h in range(2):
                    rows = a["attr"][bass.ds(c * CE + h * H, CE), :].rearrange("(k p) d -> p k d", p=P)
                    sp.dma_start(rt[:, :, h, D:D + AD], rows).then_inc(sem(f"attr_in{i}"), 16)
            for i in range(4):
                step2(0, i, True)
            with sp.Fori(1, NIT) as it:
                for i in range(4):
                    step2(it, i, False)

            for i in range(4):
                sp.wait_ge(sem(f"scattered{i}"), NIT * 128)

            def step3(it, i, first):
                c = it * 4 + i
                if not first:
                    sp.wait_ge(sem("fwd3"), c - 3)
                    sp.sem_inc(sem("sp_turns"), 1)
                    sp.wait_ge(sem("dst_ready"), c - 3)
                    sp.sem_inc(sem("sp_turns"), 1)
                rt = RT[:, i, :, :].rearrange("p (k h) r -> p k h r", h=2)
                for h in range(2):
                    rows = rec[bass.ds(c * CE + h * H, CE), :].rearrange("(k p) d -> p k d", p=P)
                    sp.dma_start(G[:, i, :].rearrange("p (k h d) -> p k h d", k=KC, h=2)[:, :, h, :],
                                 rows[:, :, 0:D]).then_inc(sem(f"rec_in{i}"), 16)
                    sp.dma_start(rt[:, :, h, D + AD:RW], rows[:, :, D + AD:RW]).then_inc(sem(f"rec_in{i}"), 16)
            for i in range(4):
                step3(0, i, True)
            with sp.Fori(1, NIT) as it:
                for i in range(4):
                    step3(it, i, False)

            def carry_in(dst, src, n):
                sp.dma_start(dst, src).then_inc(sem("carry"), 16)

            for i in range(4):
                sp.wait_ge(sem(f"runs_out{i}"), 16 * NIT * 2)
            carry_in(CR[:, :], dbc(runs_l0[H - 1:H, 0:D], P), 0)
            carry_in(CR2[:, :], dbc(runs[H - 1:H, 0:D], P), 0)
            for i in range(2):
                sp.wait_ge(sem(f"same_src{i}"), 8 * NCH)
                sp.wait_ge(sem(f"dst_out{i}"), 8 * NCH)

            with sp.Fori(0, LAYERS) as l:
                sp.wait_ge(sem("h_ready"), l + 1)
                sp.sem_inc(sem("sp_turns"), 1)
                sp.dma_start(wl[:, :], a["ws"][bass.ds(l * D, D), :]).then_inc(sem("layer_in"), 16)
                for i, nm in enumerate(("bs", "lnw", "lnb")):
                    sp.dma_start(lrows[:, i, :], a[nm][bass.ds(l, 1), :].broadcast_to([P, D])).then_inc(sem("layer_in"), 16)
                table_out(l + 2)
                gather_pass(same_dst, a["src_q"], runs, N4 + l * NCH, "gath_b", l * NIT, l * NIT)
                for i in range(4):
                    sp.wait_ge(sem(f"runs_out{i}"), 16 * NIT * (l + 3))
                    sp.sem_inc(sem("sp_turns"), 1)
                sp.wait_ge(sem("carry_used"), l + 1)
                sp.sem_inc(sem("sp_turns"), 1)
                carry_in(CR[:, :], dbc(runs[H - 1:H, 0:D], P), 0)

            sp.dma_start(CRE[:, :], dbc(runs_e[H - 1:H, 0:EW], P)).then_inc(sem("carry_e"), 16)
            table_out(LAYERS + 2)
            gather_pass(same_src, dst_by_src, runs, N8, "gath_c", 0)
            for i in range(4):
                sp.wait_ge(sem(f"runs_out{i}"), 16 * NIT * 7)
            sp.wait_ge(sem("carry_used"), LAYERS + 1)
            carry_in(CR[:, :], dbc(runs[H - 1:H, 0:D], P), 0)

            sp.wait_ge(sem("x_ready"), 1)
            sp.dma_start(out.rearrange("(p j) d -> p (j d)", p=P), X[:, :]).then_inc(sem("out"), 16)
            sp.wait_ge(sem("out"), 16)

        @block.gpsimd
        def _(pool):
            pool.iota(iota_i[:, :], [[1, P]], base=0, channel_multiplier=0).then_inc(sem("iota"), 1)
            pool.iota(pidx_i[:, :], [[0, 1]], base=0, channel_multiplier=1).then_inc(sem("iota"), 1)
            pool.iota(na[:, :].bitcast(I32), [[1, NJ]], base=0, channel_multiplier=NJ).then_inc(sem("iota"), 1)

            def gather_pass(used, n0, name, done, tables):
                pool.wait_ge(sem("table_out"), tables)
                pool.sem_inc(sem("pool_turns"), 1)

                def step(it, i):
                    c = it * 4 + i
                    pool.wait_ge(sem(f"idx_in{i}"), (it + done) * 16 + 16)
                    pool.sem_inc(sem("pool_turns"), 1)
                    if positive(c + n0 - 3):
                        pool.wait_ge(sem(used), c + n0 - 3)
                    pool.sem_inc(sem("pool_turns"), 1)
                    for q in range(8):
                        pool.indirect_dma_start(
                            G[:, i, q * D:(q + 1) * D], None, table,
                            bass.IndirectOffsetOnAxis(ap=IDX[:, i, q:q + 1], axis=0)).then_inc(sem(f"{name}{i}"), 16)
                for i in range(4):
                    step(0, i)
                with pool.Fori(1, NIT) as it:
                    for i in range(4):
                        step(it, i)

            gather_pass("g_used", 0, "gath_a", 0, 16)

            pool.wait_ge(sem("fill_zero"), 16 * NZ)
            pool.wait_ge(sem("rows_ready"), 1)
            for j in range(NJ):
                pool.indirect_dma_start(
                    fill64, bass.IndirectOffsetOnAxis(ap=begrow[:, j:j + 1], axis=0),
                    T[:, j * D:(j + 1) * D], None, bounds_check=EP - 1, oob_is_err=False).then_inc(sem("filled"), 16)

            def scatter(it, i):
                pool.wait_ge(sem(f"attr_in{i}"), it * 32 + 32)
                pool.sem_inc(sem("pool_turns"), 1)
                pool.wait_ge(sem("pay_ready"), it * 4 + i + 1)
                pool.sem_inc(sem("pool_turns"), 1)
                pool.wait_ge(sem("msg_ready"), it * 4 + i + 1)
                pool.sem_inc(sem("pool_turns"), 1)
                pool.wait_ge(sem("pos_ready"), it * 4 + i + 1)
                pool.sem_inc(sem("pool_turns"), 1)
                for q in range(8):
                    pool.indirect_dma_start(
                        rec, bass.IndirectOffsetOnAxis(ap=IDX[:, i, q:q + 1], axis=0),
                        RT[:, i, q, :], None).then_inc(sem(f"scattered{i}"), 16)
            with pool.Fori(0, NIT) as it:
                for i in range(4):
                    scatter(it, i)

            def ends(dst, rows, idx, n):
                for g in range(NG):
                    s = g % 2
                    done = (n + g) // 2 * 16 * GT
                    if positive(done):
                        pool.wait_ge(sem(f"ends{s}"), done)
                    pool.sem_inc(sem("pool_turns"), 1)
                    for k in range(GT):
                        j = g * GT + k
                        pool.indirect_dma_start(dst[:, j * D:(j + 1) * D], None, rows,
                                                bass.IndirectOffsetOnAxis(ap=idx[:, j:j + 1], axis=0)).then_inc(sem(f"ends{s}"), 16)

            def runs_done(n):
                for i in range(4):
                    pool.wait_ge(sem(f"runs_out{i}"), 16 * NIT * n)
                    pool.sem_inc(sem("pool_turns"), 1)

            runs_done(1)
            for i in range(4):
                pool.wait_ge(sem(f"scattered{i}"), NIT * 128)
                pool.sem_inc(sem("pool_turns"), 1)
            ends(T, runs_l064, endrow[0], 0)

            runs_done(2)
            ends(AG, runs64, endrow[1], NG)

            with pool.Fori(0, LAYERS) as l:
                gather_pass("fwd", N4 - NCH + l * NCH, "gath_b", (l + 1) * NIT, l * 16 + 32)
                runs_done(l + 3)
                pool.wait_ge(sem("h_ready"), l + 1)
                pool.sem_inc(sem("pool_turns"), 1)
                ends_layer(pool, l, sem, AG, runs64, endrow[0], NG, GT)
            pool.wait_ge(sem("e_out"), 16 * NCH)
            for g in range(NG):
                s = g % 2
                if g >= 2:
                    pool.wait_ge(sem(f"ends_e{s}"), g // 2 * 16 * GT)
                pool.sem_inc(sem("pool_turns"), 1)
                for k in range(GT):
                    j = g * GT + k
                    pool.indirect_dma_start(EA[:, j * EW:(j + 1) * EW], None, runs_e_rows,
                                            bass.IndirectOffsetOnAxis(ap=endrow[1][:, j:j + 1], axis=0)).then_inc(sem(f"ends_e{s}"), 16)
            gather_pass("fwd", N8 - NCH, "gath_c", 5 * NIT, 16 * (LAYERS + 2))
            runs_done(7)
            pool.wait_ge(sem("he_ready"), 1)
            ends(AG, runs64, endrow[1], 6 * NG)

        @block.tensor
        def _(pe):
            def fwd(i, src, n, arrived, value):
                pe.wait_ge(arrived, value)
                if positive(n - 1):
                    pe.wait_ge(sem("pt_free"), n - 1)
                for k in range(KC):
                    t = pe.transpose(bank(i % 2)[:, k * P:(k + 1) * P], src[:, k * P:(k + 1) * P], ident[:, :])
                return t.then_inc(sem("fwd"), 1)

            def back(i, n, r):
                pe.wait_ge(sem("scanned"), n + 1)
                if positive(r - 1):
                    pe.wait_ge(sem("r_ready"), r - 1)
                for k in range(KC):
                    t = pe.transpose(bank(2 + i % 2)[:, k * P:(k + 1) * P], S[:, i % 2, k * P:(k + 1) * P], ident[:, :])
                t.then_inc(sem("back"), 1)

            def project(K, rhs, n0):
                def step(n, s):
                    pe.wait_ge(sem("z_ready"), n + 1)
                    if positive(n):
                        pe.wait_ge(sem("zts_ready"), n)
                    pe.sem_inc(sem("pe_turns"), 1)
                    for k in range(GT):
                        t = pe.transpose(PS[0:K, k * P:(k + 1) * P], Z[:, s, k * K:(k + 1) * K], ident[:, :])
                    t.then_inc(sem("zt"), 1)
                    pe.wait_ge(sem("zts_ready"), n + 1)
                    if positive(n):
                        pe.wait_ge(sem("zo_used"), n)
                    for k in range(GT):
                        t = pe.matmul(bank(2)[:, k * D:(k + 1) * D], ZTs[0:K, k * P:(k + 1) * P], rhs, start=True, stop=True)
                    t.then_inc(sem("zo"), 1)
                if isinstance(n0, int) and n0 == 0:
                    step(0, 0)
                    step(1, 1)
                    with pe.Fori(1, NG // 2) as g:
                        step(g * 2, 0)
                        step(g * 2 + 1, 1)
                else:
                    with pe.Fori(0, NG // 2) as g:
                        step(g * 2 + n0, 0)
                        step(g * 2 + n0 + 1, 1)

            def attr_fwd(d):
                pe.wait_ge(sem("e_in"), d * 64 + 64)
                for k in range(KC):
                    t = pe.transpose(bank(5)[:, k * P:(k + 1) * P], E_WIN[:, k * P:(k + 1) * P], ident[:, :])
                t.then_inc(sem("e_fwd"), 1)

            def attr_back(d):
                pe.wait_ge(sem("e_scanned"), d * 2 + 2)
                for m, src in enumerate((E_SUM, E_MAX)):
                    for k in range(KC):
                        t = pe.transpose(bank(6 + m)[:, k * P:(k + 1) * P], src[:, k * P:(k + 1) * P], ident[:, :])
                t.then_inc(sem("e_back"), 1)

            def gather_pass(n0, name, done, attr=None):
                def step(it, i, first):
                    c = it * 4 + i
                    fwd(i, G[:, i, :], c + n0 - NCH, sem(f"{name}{i}"), (it + done) * 128 + 128)
                    if not (first and i == 0):
                        back((i - 1) % 4, c + n0 - 1, c + n0 - 1 - NCH)
                    if attr is not None and i == 1:
                        attr_fwd(attr + it)
                    if attr is not None and i == 3:
                        attr_back(attr + it)
                for i in range(4):
                    step(0, i, True)
                with pe.Fori(1, NIT) as it:
                    for i in range(4):
                        step(it, i, False)
                back(3, n0 + (NCH - 1), n0 - 1)

            pe.wait_ge(sem("consts"), 1)
            pe.wait_ge(sem("params"), W["params"])
            pe.wait_ge(sem("w12_ready"), 1)
            pe.matmul(bank(4)[0:2, 0:D], w12r[:, 0:2], w4[:, 0, :], start=True, stop=True).then_inc(sem("w4_small"), 1)
            for i in range(2):
                pe.matmul(bank(5 + i)[:, 0:D], w12r[:, 2 + i:3 + i].broadcast_to([D, P]), w4[:, 1, :],
                          start=True, stop=True).then_inc(sem("w4_small"), 1)
            pe.wait_ge(sem("w4_copied"), 1)
            project(D, poolw[:, :], QA)

            pe.wait_ge(sem("hist_zero"), 1)
            for b in range(2):
                pe.matmul(bank(4 + b)[0:NJ, 0:P], ident[:, 0:NJ], HC[:, 0, :], start=True, stop=False, skip_group_check=True)

            def hist(n, s):
                pe.wait_ge(sem("oh_ready"), n + 1)
                for b in range(2):
                    for k in range(KC):
                        t = pe.matmul(bank(4 + b)[0:NJ, 0:P], OH[:, s, 2 * b, k, 0:NJ], OH[:, s, 2 * b + 1, k, :],
                                      start=False, stop=False, skip_group_check=True)
                t.then_inc(sem("hist_done"), 1)

            def step1(it, i, first):
                c = it * 4 + i
                fwd(i, Gs[:, i % 2, :], c, sem("gs_ready"), c + 1)
                hist(c * 2, 0)
                if not (first and i == 0):
                    back((i - 1) % 4, c - 1, c - 1)
                hist(c * 2 + 1, 1)
            for i in range(4):
                step1(0, i, True)
            with pe.Fori(1, NIT) as it:
                for i in range(4):
                    step1(it, i, False)
            back(3, NCH - 1, NCH - 1)
            for b in range(2):
                pe.matmul(bank(4 + b)[0:NJ, 0:P], ident[:, 0:NJ], HC[:, 0, :], start=False, stop=True,
                          skip_group_check=True).then_inc(sem("hist_sum"), 1)

            pe.wait_ge(sem("row_sums"), 1)
            pe.matmul(bank(6)[0:NJ, 0:2], below[0:NJ, 0:NJ], hoff[0:NJ, :], start=True, stop=True).then_inc(sem("row_offs"), 1)

            pe.wait_ge(sem("starts_ready"), 2)
            pe.wait_ge(sem("r_ready"), NCH)
            pe.matmul(bank(3)[0:NJ, 0:P], ident[0:NJ, 0:NJ], HC[0:NJ, 3, :], start=True, stop=False,
                      skip_group_check=True).then_inc(sem("counted"), 1)
            HB = 2 * NCH

            def digit(h, s, d, k):
                return OH[:, s // 2, 2 * (s % 2) + d, k, :]

            def key_col(i, q):
                return RT[:, i, q, C_SRC:C_SRC + 1].broadcast_to([P, P])

            def turn(h, s):
                pe.wait_ge(sem("oh_ready"), h + HB + 1)
                if positive(h):
                    pe.wait_ge(sem("oht_copied"), h)
                ohb = bank(5).bitcast(BF16)
                for k in range(KC):
                    t = pe.transpose(ohb[0:NJ, k * P:(k + 1) * P], digit(h, s, 0, k)[:, 0:NJ], ident_b[:, :])
                t.then_inc(sem("oht"), 1)

            def src_row(h, s, k):
                t = pe.matmul(bank(4 - 2 * (s % 2))[:, k * P:(k + 1) * P], key_col(s // 2, s % 2 * KC + k), ident[:, :],
                              start=True, stop=True)
                if k == KC - 1:
                    t.then_inc(sem("src_rows"), 1)

            def rows_free(h, c):
                pe.wait_ge(sem("pay_ready"), c + 1)
                if positive(h - 1):
                    pe.wait_ge(sem("ranked"), h - 1)

            def chain(c, i, x, last):
                h, s = c * 2 + x, i % 2 * 2 + x
                h_slot, n_slot = (i * 2 + x) % 4, (i * 2 + x + 1) % 4
                if positive(h - 1):
                    pe.wait_ge(sem("looked"), h - 1)
                for k in range(KC):
                    pe.wait_ge(sem("c_copied"), h * KC + k + 1)
                    pe.matmul(bank(3)[0:NJ, 0:P], digit(h, h_slot, 0, k)[:, 0:NJ], digit(h, h_slot, 1, k),
                              start=False, stop=False, skip_group_check=True).then_inc(sem("counted"), 1)
                    if k == 0:
                        pe.wait_ge(sem("oht_copied"), h + 1)
                    t = pe.matmul(bank(6 + x)[:, k * P:(k + 1) * P], OHTs[0:NJ, x, k * P:(k + 1) * P], Cs[0:NJ, k % 2, :],
                                  start=True, stop=True)
                    if k == KC - 1:
                        t.then_inc(sem("lookups"), 1)
                    if not last:
                        if k == 0:
                            turn(h + 1, n_slot)
                            rows_free(h + 1, c + x)
                        n = i * 2 + x + 1
                        src_row(h + 1, n % 8, k)

            def fwd2(it, i):
                pe.wait_ge(sem(f"fill_in{i}"), it * 16 + 16)
                pe.wait_ge(sem("pt_free"), it * 4 + i + N2)
                for k in range(KC):
                    t = pe.transpose(bank(0)[:, k * P:(k + 1) * P], G[:, i, k * P:(k + 1) * P], ident[:, :])
                t.then_inc(sem("fwd"), 1)

            def back2(n, i):
                pe.wait_ge(sem("scanned"), n + N2 + 1)
                if positive(n):
                    pe.wait_ge(sem("msg_ready"), n)
                for k in range(KC):
                    t = pe.transpose(bank(1)[:, k * P:(k + 1) * P], S[:, i % 2, k * P:(k + 1) * P], ident[:, :])
                t.then_inc(sem("back2"), 1)

            def step2(it, i, last):
                c = it * 4 + i
                end = last and i == 3
                chain(c, i, 0, False)
                back2(c, i)
                if not end:
                    fwd2(it + (i + 1) // 4, (i + 1) % 4)
                chain(c, i, 1, end)
            fwd2(0, 0)
            turn(0, 0)
            rows_free(0, 0)
            for k in range(KC):
                src_row(0, 0, k)
            for i in range(4):
                step2(0, i, False)
            with pe.Fori(1, NIT - 1) as it:
                for i in range(4):
                    step2(it, i, False)
            for i in range(4):
                step2(NIT - 1, i, True)

            def fwd3(it, i, first):
                c = it * 4 + i
                pe.wait_ge(sem(f"rec_in{i}"), it * 64 + 64)
                if positive(c - 1):
                    pe.wait_ge(sem("ks_ready"), c - 1)
                for k in range(KC):
                    for h in range(2):
                        t = pe.matmul(bank(2 * (i % 2))[h * D:(h + 1) * D, k * P:(k + 1) * P],
                                      RT[:, i, k * 2 + h, C_SRC:C_SRC + 1].broadcast_to([P, D]), ident[:, :],
                                      start=True, stop=True)
                t.then_inc(sem("kr"), 1)
                if positive(c - 1):
                    pe.wait_ge(sem("l3r"), c - 1)
                for k in range(KC):
                    t = pe.transpose(bank(1 + 5 * (i % 2))[:, k * P:(k + 1) * P], G[:, i, k * P:(k + 1) * P], ident[:, :])
                t.then_inc(sem("fwd3"), 1)

            def back3(i, c):
                pe.wait_ge(sem("scanned"), c + N3 + 1)
                pe.wait_ge(sem("r_ready"), c + N3 - NCH - 1)
                for k in range(KC):
                    t = pe.transpose(bank(3 + i % 2)[:, k * P:(k + 1) * P], S[:, i % 2, k * P:(k + 1) * P], ident[:, :])
                t.then_inc(sem("back"), 1)

            def step3(it, i, first):
                fwd3(it, i, first)
                if not (first and i == 0):
                    back3((i - 1) % 4, it * 4 + i - 1)
            for i in range(4):
                step3(0, i, True)
            with pe.Fori(1, NIT) as it:
                for i in range(4):
                    step3(it, i, False)
            back3(3, NCH - 1)

            project(2 * D, finalw[:, :], QB)

            def total(col, n):
                pe.wait_ge(sem("part_sum"), n)
                pe.matmul(bank(4)[:, 0:1], ones[:, :], st[:, col:col + 1], start=True, stop=True).then_inc(sem("total"), 1)
            with pe.Fori(0, LAYERS) as l:
                pe.wait_ge(sem("layer_in"), l * 64 + 64)
                pe.sem_inc(sem("pe_turns"), 1)
                project(D, wl[:, :], QC + l * NG)
                gather_pass(N4 + l * NCH, "gath_b", l * NIT, l * NIT)
                total(0, l * 2 + 1)
                total(1, l * 2 + 2)
            project(D, w3[:, :], QD)
            project(D + 2, w4c[:, :], QE)

            K3 = 3 * AD + 1

            def mlp(g, s):
                pe.wait_ge(sem("z3_ready"), g + 1)
                if positive(g):
                    pe.wait_ge(sem("z3ts_ready"), g)
                for k in range(GT):
                    t = pe.transpose(PS[0:K3, k * P:(k + 1) * P], Z[:, s, k * K3:(k + 1) * K3], ident[:, :])
                t.then_inc(sem("z3t"), 1)
                pe.wait_ge(sem("z3ts_ready"), g + 1)
                if positive(g):
                    pe.wait_ge(sem("hs_ready"), g)
                for m in range(2):
                    t = pe.matmul(bank(4 + m)[:, 0:GW], l3w1[:, :], Z3Ts[0:K3, m * GW:(m + 1) * GW], start=True, stop=True)
                t.then_inc(sem("h3"), 1)
                pe.wait_ge(sem("hs_ready"), g + 1)
                if positive(g):
                    pe.wait_ge(sem("l3_done"), g)
                for k in range(GT):
                    t = pe.matmul(bank(2)[:, k * D:(k + 1) * D], HS[:, k * P:(k + 1) * P], l3w2[:, :], start=True, stop=True)
                t.then_inc(sem("o3"), 1)
            mlp(0, 0)
            mlp(1, 1)
            with pe.Fori(1, NG // 2) as g:
                mlp(g * 2, 0)
                mlp(g * 2 + 1, 1)

            gather_pass(N8, "gath_c", 0)

        @block.scalar
        def _(act):
            def rcopy(it, i, n, outs):
                act.wait_ge(sem("back"), n + 1)
                if positive(outs):
                    act.wait_ge(sem(f"runs_out{i}"), outs)
                act.copy(R[:, i, :], bank(2 + i % 2)).then_inc(sem("r_ready"), 1)

            def project(K, n0):
                def step(n):
                    act.wait_ge(sem("zt"), n + 1)
                    if positive(n):
                        act.wait_ge(sem("zo"), n)
                    act.copy(ZTs[0:K, :], PS[0:K, 0:GT * P]).then_inc(sem("zts_ready"), 1)
                if isinstance(n0, int) and n0 == 0:
                    step(0)
                    with act.Fori(1, NG) as g:
                        step(g)
                else:
                    with act.Fori(0, NG) as g:
                        step(g + n0)

            def attr_pen(d):
                act.wait_ge(sem("e_in"), d * 64 + 64)
                act.activation(E_PEN, E_MASK, ACT.Copy, scale=BIG, bias=-BIG).then_inc(sem("e_pen"), 1)

            def attr_copy(d):
                e = E_OUT.rearrange("p (k h d) -> p k h d", k=KC, h=2)
                act.wait_ge(sem("e_back"), d + 1)
                act.copy(e[:, :, :, 0:NS], bank(6).rearrange("p (k h d) -> p k h d", k=KC, h=2)[:, :, :, A0:D])
                act.copy(e[:, :, :, NS:EW], bank(7).rearrange("p (k h d) -> p k h d", k=KC, h=2)[:, :, :, A0:A0 + AD])\
                   .then_inc(sem("e_ready"), 1)

            def gather_pass(n0, outs, attr=None):
                def step(it, i):
                    rcopy(it, i, it * 4 + (n0 + i), (it + outs) * 16)
                    if attr is not None and i == 1:
                        attr_pen(attr + it)
                    if attr is not None and i == 3:
                        attr_copy(attr + it)
                for i in range(4):
                    step(0, i)
                with act.Fori(1, NIT) as it:
                    for i in range(4):
                        step(it, i)

            def root(n):
                act.wait_ge(sem("root_in"), n)
                act.activation(na[:, :], nb[:, :], ACT.Sqrt).then_inc(sem("root_out"), 1)

            act.wait_ge(sem("w4_small"), 3)
            act.copy(w4c[0:2, :], bank(4)[0:2, 0:D]).then_inc(sem("w4_act"), 1)
            act.copy(rcd[:, 0, :], bank(5)[:, 0:D]).then_inc(sem("w4_act"), 1)
            act.copy(rcd[:, 1, :], bank(6)[:, 0:D]).then_inc(sem("w4_act"), 1)
            act.wait_ge(sem("w4_act"), 3)
            act.sem_inc(sem("w4_copied"), 1)
            root(1)
            project(D, QA)
            act.wait_ge(sem("zeroed"), 1)
            fv = fill.rearrange("(p r) d -> p (r d)", p=P)
            for z0 in range(0, FW, ZF):
                w = min(ZF, FW - z0)
                act.dma_start(fv[:, z0:z0 + w], zero_rows[:, 0:w]).then_inc(sem("fill_zero"), 16)

            def relu1(i, n):
                act.wait_ge(sem("fwd"), n + 1)
                if positive(n - 1):
                    act.wait_ge(sem("scanned"), n - 1)
                act.activation(L[:, i % 2, :], bank(i % 2), ACT.Relu, bias=poolb[:, 0:1]).then_inc(sem("pt_free"), 1)

            def step1(it, i, first):
                relu1(i, it * 4 + i)
                if not (first and i == 0):
                    rcopy(it, (i - 1) % 4, it * 4 + i - 1, (it if i else it - 1) * 16 if not first else 0)
            for i in range(4):
                step1(0, i, True)
            relu1(0, 4)
            rcopy(0, 3, 3, 0)
            for i in range(1, 4):
                step1(1, i, False)
            with act.Fori(2, NIT) as it:
                for i in range(4):
                    step1(it, i, False)
            rcopy(NIT - 1, 3, NCH - 1, (NIT - 1) * 16)
            root(2)

            def payload(it, i, first):
                if not first:
                    act.wait_ge(sem(f"scattered{i}"), it * 128)
                    act.sem_inc(sem("act_turns"), 1)
                q = it * 32 + i * 8
                for k, (col, t) in enumerate(((C_DST, dstf_q[:, bass.ds(q, 8)]), (C_SRC, srcf_q[:, bass.ds(q, 8)]))):
                    act.activation(RT[:, i, :, col], t, ACT.Copy)
                act.activation(RT[:, i, :, C_WP], w_q[:, bass.ds(q, 8)], ACT.Relu)
                act.activation(RT[:, i, :, C_WN], w_q[:, bass.ds(q, 8)], ACT.Relu, scale=-1.0).then_inc(sem("pay_ready"), 1)

            def oht_copy(h, s):
                act.wait_ge(sem("oht"), h + 1)
                if positive(h - 1):
                    act.wait_ge(sem("lookups"), h - 1)
                act.copy(OHTs[0:NJ, s, :], bank(5).bitcast(BF16)[0:NJ, 0:KC * P]).then_inc(sem("oht_copied"), 1)

            def c_copy(h, k):
                n = h * KC + k
                act.wait_ge(sem("counted"), n + 1)
                act.copy(Cs[0:NJ, k % 2, :], bank(3)[0:NJ, 0:P]).then_inc(sem("c_copied"), 1)

            def messages(c, i, q0):
                for q in (q0, q0 + 1):
                    t = act.activation(RT[:, i, q, 0:D], bank(1)[:, q * D:(q + 1) * D], ACT.Identity,
                                       scale=s_q[:, bass.ds(c * 8 + q, 1)], bias=pen_q[:, bass.ds(c * 8 + q, 1)])
                if q0 == 6:
                    t.then_inc(sem("msg_ready"), 1)

            def half(c, i, x, mc, mi, last):
                h = c * 2 + x
                c_copy(h, 0)
                c_copy(h, 1)
                if not last:
                    oht_copy(h + 1, 1 - x)
                c_copy(h, 2)
                if mc is not None:
                    if x == 1:
                        act.wait_ge(sem("back2"), mc + 1)
                        act.sem_inc(sem("act_turns"), 1)
                    messages(mc, mi, 4 - 4 * x)
                c_copy(h, 3)
                if mc is not None:
                    messages(mc, mi, 6 - 4 * x)

            def step2(it, i, first, last):
                c = it * 4 + i
                half(c, i, 0, None if first and i == 0 else c - 1, (i - 1) % 4, False)
                if not (last and i == 3):
                    payload(it + (i + 1) // 4, (i + 1) % 4, first and i < 3)
                half(c, i, 1, c, i, last and i == 3)
            act.wait_ge(sem("starts_ready"), 2)
            for i in range(3):
                act.wait_ge(sem(f"runs_out{i}"), NIT * 16)
            payload(0, 0, True)
            oht_copy(0, 0)
            for i in range(4):
                step2(0, i, True, False)
            with act.Fori(1, NIT - 1) as it:
                for i in range(4):
                    step2(it, i, False, False)
            for i in range(4):
                step2(NIT - 1, i, False, True)
            messages(NCH - 1, 3, 4)
            messages(NCH - 1, 3, 6)

            def step3(it, i, first):
                c = it * 4 + i
                s = i % 2
                act.wait_ge(sem("kr"), c + 1)
                if positive(c - 1):
                    act.wait_ge(sem("mk_ready"), c - 1)
                if positive(c - 1):
                    act.wait_ge(sem("ks_carry"), c - 1)
                act.copy(KS[s][:, 1:CE + 1], bank(2 * s)).then_inc(sem("ks_ready"), 1)
                if not (first and i == 0):
                    act.wait_ge(sem("ks_ready"), c)
                    act.copy(KS[s][:, 0:1], KS[1 - s][:, CE:CE + 1]).then_inc(sem("ks_carry"), 1)
                act.wait_ge(sem("fwd3"), c + 1)
                act.wait_ge(sem("scanned"), c + N3 - 1)
                act.activation(L[:, s, :], bank(1 + 5 * s), ACT.Relu, bias=poolb[:, 0:1]).then_inc(sem("l3r"), 1)
                if not (first and i == 0):
                    out3(it, (i - 1) % 4, c - 1, first, it if i else it - 1)

            def out3(it, i, c, first, uses):
                s = i % 2
                act.wait_ge(sem("back"), c + N3 - NCH + 1)
                if first:
                    act.wait_ge(sem(f"runs_out{i}"), NIT * 16)
                else:
                    act.wait_ge(sem(f"runs_out{i}"), (uses + NIT) * 16)
                act.copy(R[:, i, :], bank(3 + s)).then_inc(sem("r_ready"), 1)
                act.wait_ge(sem("mk_ready"), c + 1)
                act.sem_inc(sem("act_turns"), 1)
                act.dma_start(same_src[:, bass.ds(c * CE, CE)], MK[s][0:P:D, :]).then_inc(sem(f"same_src{s}"), 16)
                act.wait_ge(sem("dst_ready"), c + 1)
                act.sem_inc(sem("act_turns"), 1)
                act.dma_start(dst_by_src[:, bass.ds(c * 8, 8)], IDX[:, s, :]).then_inc(sem(f"dst_out{s}"), 16)
                act.wait_ge(sem("r_ready"), c + N3 - NCH + 1)
                act.sem_inc(sem("act_turns"), 1)
                rows = runs[bass.ds(c * CE, CE), :].rearrange("(k p) d -> p k d", p=P)
                act.dma_start(rows, R[:, i, :].rearrange("p (k d) -> p k d", k=KC)).then_inc(sem(f"runs_out{i}"), 16)

            for i in range(4):
                step3(0, i, True)
            with act.Fori(1, NIT) as it:
                for i in range(4):
                    step3(it, i, False)
            out3(NIT - 1, 3, NCH - 1, False, NIT - 1)

            project(2 * D, QB)
            root(3)
            with act.Fori(0, LAYERS) as l:
                project(D, QC + l * NG)
                gather_pass(N4 + l * NCH - NCH, (l + 2) * NIT, l * NIT)
                act.wait_ge(sem("dev_ready"), l + 1)
                act.activation(AG[:, :], Hn[:, :], ACT.Square, accum_out=st[:, 1:2]).then_inc(sem("sq_done"), 1)
                act.wait_ge(sem("var_ready"), l + 1)
                act.activation(st[:, 4:5], st[:, 3:4], ACT.Sqrt).then_inc(sem("std_ready"), 1)
            root(4)
            project(D, QD)
            project(D + 2, QE)

            K3 = 3 * AD + 1

            def mlp(g):
                act.wait_ge(sem("z3t"), g + 1)
                if positive(g):
                    act.wait_ge(sem("h3"), g)
                act.copy(Z3Ts[0:K3, :], PS[0:K3, 0:GT * P]).then_inc(sem("z3ts_ready"), 1)
                act.wait_ge(sem("h3"), g + 1)
                if positive(g):
                    act.wait_ge(sem("o3"), g)
                act.activation(HS[:, 0:GW], bank(4)[:, 0:GW], ACT.Relu, bias=l3b1[:, 0:1])
                act.activation(HS[:, GW:2 * GW], bank(5)[:, 0:GW], ACT.Relu, bias=l3b1[:, 0:1]).then_inc(sem("hs_ready"), 1)
            mlp(0)
            with act.Fori(1, NG) as g:
                mlp(g)
            gather_pass(N8 - NCH, 6 * NIT)

        @block.vector
        def _(dve):
            order = [0]

            def then(ins):
                order[0] += 1
                ins.then_inc(sem("dve_order"), 1)
                dve.wait_ge(sem("dve_order"), order[0])

            class Steps:
                def __init__(self, name, base):
                    self.sem, self.base, self.k = sem(name), base, 0

                def __call__(self, ins):
                    self.k += 1
                    ins.then_inc(self.sem, 1)
                    dve.wait_ge(self.sem, self.base + self.k)

            def f3(t):
                return t.rearrange("p (j d) -> p j d", d=D)

            dve.wait_ge(sem("iota"), 3)
            then(dve.tensor_copy(iota_f[:, :], iota_i[:, :]))
            then(dve.tensor_copy(iota_b[:, :], iota_f[:, :]))
            then(dve.tensor_copy(pidx[:, :], pidx_i[:, :]))
            then(dve.tensor_copy(nb[:, :], na[:, :].bitcast(I32)))
            then(dve.tensor_scalar(valid[:, :], nb[:, :], float(n_nodes), None, ALU.is_lt))
            dve.tensor_scalar(ident[:, :], iota_f[:, :], pidx[:, 0:1], None, ALU.is_equal)
            dve.tensor_scalar(ident_b[:, :], iota_f[:, :], pidx[:, 0:1], None, ALU.is_equal)
            dve.tensor_scalar(earlier[:, :], iota_f[:, :], pidx[:, 0:1], None, ALU.is_lt)
            dve.tensor_scalar(below[:, :], iota_f[:, :], pidx[:, 0:1], None, ALU.is_gt)
            dve.memset(ones[:, :], 1.0)
            then(dve.memset(HC[:, :, :], 0.0))
            dve.sem_inc(sem("consts"), 1)
            dve.sem_inc(sem("hist_zero"), 1)
            dve.wait_ge(sem("params"), W["params"])
            for i in range(2):
                dve.tensor_scalar(w12r[:, 2 * i:2 * i + 1], w12c[:, i:i + 1], 0.0, None, ALU.max)
                then(dve.tensor_scalar(w12r[:, 2 * i + 1:2 * i + 2], w12c[:, i:i + 1], -1.0, 0.0, ALU.mult, ALU.max))
            dve.sem_inc(sem("w12_ready"), 1)
            dve.tensor_tensor(MD, DX[:, 1:TILES + 1], DX[:, 0:TILES], ALU.is_equal).then_inc(sem("md_ready"), 1)

            def norm(n):
                then(dve.tensor_reduce(nd[:, :], v3(X), AX.X, ALU.add))
                then(dve.tensor_scalar(nd[:, :], nd[:, :], 1.0 / D, None, ALU.mult))
                then(dve.tensor_tensor(v3(Hn), v3(X), bc(nd[:, :], [P, NJ, D]), ALU.subtract))
                then(dve.tensor_tensor(AG[:, :], Hn[:, :], Hn[:, :], ALU.mult))
                then(dve.tensor_reduce(nb[:, :], v3(AG), AX.X, ALU.add))
                dve.tensor_scalar(nb[:, :], nb[:, :], 1.0 / D, EPS, ALU.mult, ALU.add).then_inc(sem("root_in"), 1)
                dve.wait_ge(sem("root_out"), n)
                then(dve.reciprocal(nd[:, :], na[:, :]))
                then(dve.scalar_tensor_tensor(v3(Hn), v3(Hn), 0.0, bc(nd[:, :], [P, NJ, D]), ALU.max, ALU.mult))
            norm(1)
            then(dve.memset(KEYS, 0.0))
            for i, t in enumerate((SI, DI)):
                then(dve.tensor_scalar(tmp_i, t, 7, None, ALU.logical_shift_right))
                then(dve.tensor_copy(KEYS[:, 2 * i, 0:TILES], tmp_i))
                then(dve.tensor_scalar(tmp_i, t, 127, None, ALU.bitwise_and))
                then(dve.tensor_copy(KEYS[:, 2 * i + 1, 0:TILES], tmp_i))
            dve.tensor_copy(srcf_q, SI)
            then(dve.tensor_copy(dstf_q, DI))
            dve.tensor_scalar(s_q, w_q, coef[:, 0:1], 1.0, ALU.mult, ALU.add)
            then(dve.tensor_tensor(pen_q, SI, DI, ALU.is_equal))
            then(dve.tensor_scalar(pen_q, pen_q, -SELF, None, ALU.mult))
            dve.tensor_scalar(vpos[:, :], vin[:, :], 0.0, None, ALU.max)
            then(dve.tensor_scalar(vneg[:, :], vin[:, :], -1.0, 0.0, ALU.mult, ALU.max))
            dve.wait_ge(sem("same_dst"), 16)

            def project(n0, make, post):
                def produce(g, s):
                    n = g + n0
                    if positive(n - 1):
                        dve.wait_ge(sem("zt"), n - 1)
                    make(g, s).then_inc(sem("z_ready"), 1)

                def consume(g):
                    n = g + n0
                    dve.wait_ge(sem("zo"), n + 1)
                    post(g).then_inc(sem("zo_used"), 1)
                produce(0, 0)
                produce(1, 1)
                consume(0)
                produce(2, 0)
                consume(1)
                produce(3, 1)
                with dve.Fori(2, NG // 2) as g:
                    consume(g * 2 - 2)
                    produce(g * 2, 0)
                    consume(g * 2 - 1)
                    produce(g * 2 + 1, 1)
                consume(NG - 2)
                consume(NG - 1)
                dve.wait_ge(sem("zo_used"), n0 + NG)
                dve.sem_inc(sem("dve_turns"), 1)

            def z3(s, K):
                return Z[:, s, 0:GT * K].rearrange("p (j d) -> p j d", d=K)

            zo = f3(bank(2)[:, 0:GW])
            project(QA, lambda g, s: dve.tensor_scalar(z3(s, D), group(Hn, g), 1.0, None, ALU.mult),
                    lambda g: dve.tensor_scalar(group(T, g), zo, 1.0, None, ALU.mult))
            dve.sem_inc(sem("t_ready"), 1)
            dve.memset(Z[:, :, :], 0.0).then_inc(sem("zeroed"), 1)

            def onehots(q, s, h, digits):
                if positive(h - 1):
                    dve.wait_ge(sem("hist_done"), h - 1)
                for d in range(digits):
                    t = dve.tensor_tensor(OH[:, s, d, :, :], rowbc(iota_b[:, :], KC),
                                          bc(KEYS[:, d, bass.ds(q, KC)], [P, KC, P]), ALU.is_equal)
                t.then_inc(sem("oh_ready"), 1)

            def scan(i, n, data, op0, op1, first=False, name="scanned"):
                mask = M[:, i // 2, (i % 2) * CE:(i % 2 + 1) * CE]
                init = 0.0 if first else S[:, 1 - i % 2, CE - 1:CE]
                return dve.tensor_tensor_scan(S[:, i % 2, :], mask, data, init, op0, op1)

            def masks_there(it, i, done):
                if i % 2 == 0:
                    dve.wait_ge(sem(f"masks_in{i // 2}"), (it + done) * 32 + 32)

            def pre1(it, i):
                c = it * 4 + i
                q = c * 8
                dve.wait_ge(sem(f"gath_a{i}"), it * 128 + 128)
                if positive(c - 1):
                    dve.wait_ge(sem("fwd"), c - 1)
                g = G[:, i, :].rearrange("p (q d) -> p q d", d=D)
                o = Gs[:, i % 2, :].rearrange("p (q d) -> p q d", d=D)
                dve.tensor_tensor(o, g, bc(s_q[:, bass.ds(q, 8)], [P, 8, D]), ALU.mult).then_inc(sem("g_used"), 1)
                dve.wait_ge(sem("g_used"), c + 1)
                dve.tensor_tensor(o, o, bc(pen_q[:, bass.ds(q, 8)], [P, 8, D]), ALU.add).then_inc(sem("gs_ready"), 1)

            def scan1(it, i, first):
                n = it * 4 + i
                dve.wait_ge(sem("pt_free"), n + 1)
                masks_there(it, i, 0)
                if positive(n - 1):
                    dve.wait_ge(sem("back"), n - 1)
                if positive(n):
                    dve.wait_ge(sem("scanned"), n)
                scan(i, n, L[:, i % 2, :], ALU.mult, ALU.max, first).then_inc(sem("scanned"), 1)

            def step1(it, i, first):
                c = it * 4 + i
                pre1(it, i)
                onehots(c * 8, 0, c * 2, 4)
                if not (first and i == 0):
                    scan1(it if i else it - 1, (i - 1) % 4, first and i == 1)
                onehots(c * 8 + 4, 1, c * 2 + 1, 4)
            for i in range(4):
                step1(0, i, True)
            with dve.Fori(1, NIT) as it:
                for i in range(4):
                    step1(it, i, False)
            scan1(NIT - 1, 3, False)

            dve.wait_ge(sem("hist_sum"), 2)
            then(dve.tensor_copy(HC[0:NJ, 0, :], bank(5)[0:NJ, 0:P]))
            then(dve.tensor_copy(HC[0:NJ, 1, :], bank(4)[0:NJ, 0:P]))
            for i in range(2):
                then(dve.tensor_tensor_scan(HC[0:NJ, 2 + i, :], ones[0:NJ, :], HC[0:NJ, i, :], 0.0, ALU.mult, ALU.add))
                then(dve.tensor_copy(hoff[0:NJ, i:i + 1], HC[0:NJ, 2 + i, P - 1:P]))
            dve.sem_inc(sem("row_sums"), 1)
            dve.wait_ge(sem("row_offs"), 1)
            then(dve.tensor_copy(hoff[0:NJ, :], bank(6)[0:NJ, 0:2]))
            for i in range(2):
                then(dve.tensor_tensor(HC[0:NJ, 2 + i, :], HC[0:NJ, 2 + i, :], HC[0:NJ, i, :], ALU.subtract))
                dve.tensor_scalar(HC[0:NJ, 2 + i, :], HC[0:NJ, 2 + i, :], hoff[0:NJ, i:i + 1], None, ALU.add)\
                   .then_inc(sem("starts_ready"), 1)
            dve.wait_ge(sem("starts_in"), 64)

            def row_of(dst, e, w):
                then(dve.tensor_scalar(w, e, float(H), float(-(2 * H - 1)), ALU.is_ge, ALU.mult))
                then(dve.scalar_tensor_tensor(w, e, 2.0, w, ALU.mult, ALU.add))
                return w

            for i in range(2):
                then(dve.tensor_scalar(has[i][:, :], cnt[i][:, :], 1.0, None, ALU.min))
                then(dve.tensor_tensor(na[:, :], beg[i][:, :], cnt[i][:, :], ALU.add))
                then(dve.tensor_scalar(nb[:, :], na[:, :], float(H), None, ALU.is_gt))
                then(dve.scalar_tensor_tensor(span[i][:, :], beg[i][:, :], float(H), nb[:, :], ALU.is_lt, ALU.mult))
                then(dve.tensor_scalar(na[:, :], na[:, :], -1.0, 0.0, ALU.add, ALU.max))
                row_of(None, na[:, :], nb[:, :])
                then(dve.tensor_copy(endrow[i][:, :], nb[:, :]))
            row_of(None, beg[0][:, :], nb[:, :])
            then(dve.tensor_scalar(na[:, :], has[0][:, :], float(-(1 << 22)), float(1 << 22), ALU.mult, ALU.add))
            then(dve.tensor_tensor(nb[:, :], nb[:, :], na[:, :], ALU.add))
            then(dve.tensor_copy(begrow[:, :], nb[:, :]))
            dve.sem_inc(sem("rows_ready"), 1)
            then(dve.tensor_scalar(nb[:, :], cnt[1][:, :], 1.0, None, ALU.max))
            then(dve.reciprocal(rcnt[:, :], nb[:, :]))
            then(dve.tensor_scalar(pen2[:, :], span[1][:, :], BIG, -BIG, ALU.mult, ALU.add))
            dve.tensor_scalar(nb[:, :], cnt[0][:, :], 1.0, None, ALU.add).then_inc(sem("root_in"), 1)
            dve.wait_ge(sem("root_out"), 2)
            then(dve.reciprocal(dinv[:, :], na[:, :]))

            def onehots2(h, s):
                if positive(h - 3):
                    dve.wait_ge(sem("lookups"), h - 3)
                    dve.wait_ge(sem("looked"), h - 3)
                for d in range(2):
                    t = dve.tensor_tensor(OH[:, s // 2, 2 * (s % 2) + d, :, :], rowbc(iota_b[:, :], KC),
                                          bc(KEYS[:, d, bass.ds(h * KC, KC)], [P, KC, P]), ALU.is_equal)
                t.then_inc(sem("oh_ready"), 1)

            def ranks(h, c, i, x):
                dve.wait_ge(sem("src_rows"), h + 1)
                if positive(c - 1):
                    dve.wait_ge(sem("pos_ready"), c - 1)
                for k in range(KC):
                    t = dve.scalar_tensor_tensor(junk_rank[:, x, k, :], bank(4 - 2 * x)[:, k * P:(k + 1) * P],
                                                 RT[:, i, x * KC + k, C_SRC:C_SRC + 1], earlier[:, :],
                                                 ALU.is_equal, ALU.mult, accum_out=inr[:, i % 2, x, k:k + 1])
                t.then_inc(sem("ranked"), 1)

            def look(h, c, i, x):
                dve.wait_ge(sem("lookups"), h + 1)
                if positive(c):
                    dve.wait_ge(sem("pos_ready"), c)
                for k in range(KC):
                    t = dve.scalar_tensor_tensor(junk_look[:, x, k, :], bank(6 + x)[:, k * P:(k + 1) * P],
                                                 1.0, OH[:, i % 2, 2 * x + 1, k, :],
                                                 ALU.mult, ALU.mult, accum_out=lku[:, x, k:k + 1])
                t.then_inc(sem("looked"), 1)

            def pos(it, i):
                c = it * 4 + i
                dve.wait_ge(sem("looked"), c * 2 + 2)
                dve.wait_ge(sem("ranked"), c * 2 + 2)
                if positive(it):
                    dve.wait_ge(sem(f"scattered{i}"), it * 128)
                dve.tensor_tensor(IDX[:, i, :], inr[:, i % 2, :, :].rearrange("p x k -> p (x k)"),
                                  lku[:, :, :].rearrange("p x k -> p (x k)"), ALU.add).then_inc(sem("pos_ready"), 1)

            def scan2(it, i, first):
                n = it * 4 + i + N2
                dve.wait_ge(sem("fwd"), n + 1)
                masks_there(it, i, NIT)
                if positive(it * 4 + i - 1):
                    dve.wait_ge(sem("back2"), it * 4 + i - 1)
                dve.wait_ge(sem("scanned"), n)
                scan(i, n, bank(0), ALU.mult, ALU.add, first).then_inc(sem("scanned"), 1)
                dve.wait_ge(sem("scanned"), n + 1)
                dve.sem_inc(sem("pt_free"), 1)

            def step2(it, i, first, last):
                c = it * 4 + i
                h = c * 2
                end = last and i == 3
                scan2(it, i, first and i == 0)
                if not (first and i == 0):
                    look(h - 1, c - 1, (i - 1) % 4, 1)
                    pos(it if i else it - 1, (i - 1) % 4)
                if not end:
                    onehots2(h + 2, (i * 2 + 2) % 4)
                ranks(h + 1, c, i, 1)
                look(h, c, i, 0)
                if not end:
                    onehots2(h + 3, (i * 2 + 3) % 4)
                    ranks(h + 2, c + 1, (i + 1) % 4, 0)
            dve.wait_ge(sem("fill_zero"), 16 * NZ)
            onehots2(0, 0)
            onehots2(1, 1)
            ranks(0, 0, 0, 0)
            for i in range(4):
                step2(0, i, True, False)
            for i in range(4):
                step2(1, i, False, False)
            with dve.Fori(2, NIT - 1) as it:
                for i in range(4):
                    step2(it, i, False, False)
            for i in range(4):
                step2(NIT - 1, i, False, True)
            look(2 * NCH - 1, NCH - 1, 3, 1)
            pos(NIT - 1, 3)

            for i in range(4):
                dve.wait_ge(sem(f"scattered{i}"), NIT * 128)
            then(dve.memset(KS[0][:, 0:1], -1.0))

            def step3(it, i, first):
                c = it * 4 + i
                s = i % 2
                start = first and i == 0
                dve.wait_ge(sem("ks_ready"), c + 1)
                if positive(c):
                    dve.wait_ge(sem("ks_carry"), c)
                if not first or i >= 2:
                    dve.wait_ge(sem(f"same_src{s}"), (c - i + i // 2 * 2) * 8)
                dve.wait_ge(sem("scanned"), c + N3 - 1)
                dve.tensor_tensor(MK[s], KS[s][:, 1:CE + 1], KS[s][:, 0:CE], ALU.is_equal).then_inc(sem("mk_ready"), 1)
                dve.wait_ge(sem(f"rec_in{i}"), it * 64 + 64)
                if not first or i >= 2:
                    dve.wait_ge(sem(f"dst_out{s}"), (c - i + i // 2 * 2) * 8)
                dve.tensor_copy(IDX[:, s, :], RT[:, i, :, C_DST]).then_inc(sem("dst_ready"), 1)
                dve.wait_ge(sem("mk_ready"), c + 1)
                dve.wait_ge(sem("l3r"), c + 1)
                dve.wait_ge(sem("back"), c + N3 - NCH - 1)
                dve.wait_ge(sem("scanned"), c + N3)
                dve.tensor_tensor_scan(S[:, s, :], MK[s], L[:, s, :], 0.0 if start else S[:, 1 - s, CE - 1:CE],
                                       ALU.mult, ALU.max).then_inc(sem("scanned"), 1)
            for i in range(4):
                step3(0, i, True)
            with dve.Fori(1, NIT) as it:
                for i in range(4):
                    step3(it, i, False)

            def make_b(g, s):
                j = g * GT
                ga, gb = group(AG, g), group(T, g)
                step = Steps("l0_order", g * 6)
                cc = f3(CARG)
                dve.wait_ge(sem("zo_used"), g + (QB - 1))
                for t, i, row in ((gb, 0, CR[:, :]), (ga, 1, CR2[:, :])):
                    step(dve.tensor_tensor(cc, rowbc(row, GT), bc(span[i][:, bass.ds(j, GT)], [P, GT, D]), ALU.mult))
                    step(dve.tensor_tensor(t, t, bc(has[i][:, bass.ds(j, GT)], [P, GT, D]), ALU.mult))
                    step(dve.tensor_tensor(t, t, cc, ALU.max))
                z = z3(s, 2 * D)
                dve.tensor_scalar(z[:, :, 0:D], group(Hn, g), 1.0, None, ALU.mult)
                return dve.tensor_tensor(z[:, :, D:2 * D], ga, gb, ALU.max)

            dve.wait_ge(sem("carry"), 32)
            for s in range(2):
                dve.wait_ge(sem(f"ends{s}"), 16 * GT * NG)

            def post_b(g):
                cc = f3(CARG)
                step = Steps("l0_post", g * 2)
                step(dve.tensor_tensor(cc, zo, rowbc(fb[:, :], GT), ALU.add))
                step(dve.tensor_scalar(cc, cc, 0.0, None, ALU.max))
                return dve.tensor_tensor(group(X, g), group(X, g), cc, ALU.add)
            project(QB, make_b, post_b)
            dve.sem_inc(sem("carry_used"), 1)
            norm(3)
            dve.sem_inc(sem("h_ready"), 1)

            def attr_scans(d):
                dve.wait_ge(sem("e_fwd"), d + 1)
                dve.wait_ge(sem("e_kept"), d + 1)
                dve.tensor_tensor_scan(E_SUM, E_MASK, bank(5), E_KEEP[:, 0:1], ALU.mult, ALU.add).then_inc(sem("e_scanned"), 1)
                dve.wait_ge(sem("e_pen"), d + 1)
                dve.tensor_tensor_scan(E_MAX, E_PEN, bank(5), E_KEEP[:, 1:2], ALU.add, ALU.max).then_inc(sem("e_scanned"), 1)
                dve.wait_ge(sem("e_scanned"), d * 2 + 2)
                dve.tensor_copy(E_KEEP[:, 0:1], E_SUM[:, CE - 1:CE])
                dve.tensor_copy(E_KEEP[:, 1:2], E_MAX[:, CE - 1:CE]).then_inc(sem("e_kept"), 1)

            def gather_pass(n0, done, attr=None):
                def step(it, i, first):
                    n = it * 4 + i + n0
                    dve.wait_ge(sem("fwd"), n + 1 - NCH)
                    masks_there(it, i, done)
                    dve.wait_ge(sem("back"), n - 1 - NCH)
                    dve.wait_ge(sem("scanned"), n)
                    scan(i, n, bank(i % 2), ALU.mult, ALU.add, first and i == 0).then_inc(sem("scanned"), 1)
                    dve.wait_ge(sem("scanned"), n + 1)
                    dve.sem_inc(sem("pt_free"), 1)
                    if attr is not None and i == 2:
                        attr_scans(attr + it)
                for i in range(4):
                    step(0, i, True)
                with dve.Fori(1, NIT) as it:
                    for i in range(4):
                        step(it, i, False)

            def ends_sum(g, s, per, i, base, rest):
                j = g * GT
                ga, cc = group(AG, g), f3(CARG)
                step = Steps("ends_order", base)
                dve.wait_ge(sem(f"ends{s}"), per)
                step(dve.tensor_tensor(cc, rowbc(CR[:, :], GT), bc(span[i][:, bass.ds(j, GT)], [P, GT, D]), ALU.mult))
                step(dve.tensor_tensor(ga, ga, bc(has[i][:, bass.ds(j, GT)], [P, GT, D]), ALU.mult))
                step(dve.tensor_tensor(ga, ga, cc, ALU.add))
                rest(g, ga, step)
                return step.k

            dve.memset(E_KEEP[:, :], 0.0).then_inc(sem("e_kept"), 1)
            with dve.Fori(0, LAYERS) as l:
                dve.wait_ge(sem("layer_in"), l * 64 + 64)
                dve.sem_inc(sem("dve_turns"), 1)
                project(QC + l * NG,
                        lambda g, s: dve.tensor_scalar(z3(s, D), group(Hn, g), 1.0, None, ALU.mult),
                        lambda g: dve.tensor_tensor(group(T, g), zo, bc(dinv[:, bass.ds(g * GT, GT)], [P, GT, D]), ALU.mult))
                dve.sem_inc(sem("t_ready"), 1)
                gather_pass(N4 + l * NCH, (l + 2) * NIT, l * NIT)
                dve.wait_ge(sem("carry"), l * 16 + 48)
                dve.sem_inc(sem("dve_turns"), 1)

                def rest(g, ga, step):
                    j = g * GT
                    step(dve.tensor_tensor(ga, ga, group(T, g), ALU.add))
                    step(dve.tensor_tensor(ga, ga, bc(dinv[:, bass.ds(j, GT)], [P, GT, D]), ALU.mult))
                    step(dve.tensor_tensor(ga, ga, rowbc(lrows[:, 0, :], GT), ALU.add))
                    step(dve.tensor_tensor(ga, ga, bc(valid[:, bass.ds(j, GT)], [P, GT, D]), ALU.mult))
                    step(dve.tensor_reduce(gsum[:, bass.ds(g, 1)], ga, AX.XY, ALU.add))
                with dve.Fori(0, NG // 2) as g:
                    per = (g + l * (NG // 2)) * (16 * GT) + 16 * GT * (NG + 1)
                    k = ends_sum(g * 2, 0, per, 0, (g + l * (NG // 2)) * 16, rest)
                    k = ends_sum(g * 2 + 1, 1, per, 0, (g + l * (NG // 2)) * 16 + 8, rest)
                    assert k == 8
                dve.sem_inc(sem("carry_used"), 1)
                step = Steps("layer_order", l * 6)
                scale = 1.0 / (n_nodes * D)
                dve.tensor_reduce(st[:, 0:1], gsum[:, :], AX.X, ALU.add).then_inc(sem("part_sum"), 1)
                dve.wait_ge(sem("total"), l * 2 + 1)
                step(dve.tensor_scalar(st[:, 2:3], bank(4)[:, 0:1], scale, None, ALU.mult))
                dve.scalar_tensor_tensor(v3(Hn), v3(AG), st[:, 2:3], bc(valid[:, :], [P, NJ, D]),
                                         ALU.subtract, ALU.mult).then_inc(sem("dev_ready"), 1)
                dve.wait_ge(sem("sq_done"), l + 1)
                dve.sem_inc(sem("part_sum"), 1)
                dve.wait_ge(sem("total"), l * 2 + 2)
                dve.tensor_scalar(st[:, 3:4], bank(4)[:, 0:1], scale, EPS, ALU.mult, ALU.add).then_inc(sem("var_ready"), 1)
                dve.wait_ge(sem("std_ready"), l + 1)
                step(dve.reciprocal(st[:, 5:6], st[:, 4:5]))
                step(dve.tensor_scalar(lnwr[:, :], lrows[:, 1, :], st[:, 5:6], None, ALU.mult))
                step(dve.tensor_tensor(v3(Hn), v3(Hn), rowbc(lnwr[:, :], NJ), ALU.mult))
                step(dve.tensor_tensor(v3(Hn), v3(Hn), rowbc(lrows[:, 2, :], NJ), ALU.add))
                step(dve.tensor_scalar(Hn[:, :], Hn[:, :], 0.0, None, ALU.max))
                dve.sem_inc(sem("h_ready"), 1)
            then(dve.tensor_tensor(X[:, :], X[:, :], Hn[:, :], ALU.add))

            norm(4)
            project(QD, lambda g, s: dve.tensor_scalar(z3(s, D), group(Hn, g), 1.0, None, ALU.mult),
                    lambda g: dve.tensor_scalar(group(AG, g), zo, 0.0, None, ALU.max))

            def make_e(g, s):
                z = z3(s, D + 2)
                j = g * GT
                dve.tensor_scalar(z[:, :, 0:1], vpos[:, bass.ds(j, GT)].unsqueeze(2), 1.0, None, ALU.mult)
                dve.tensor_scalar(z[:, :, 1:2], vneg[:, bass.ds(j, GT)].unsqueeze(2), 1.0, None, ALU.mult)
                return dve.tensor_scalar(z[:, :, 2:D + 2], group(AG, g), 1.0, None, ALU.mult)
            project(QE, make_e, lambda g: dve.tensor_scalar(group(T, g), zo, 1.0, None, ALU.mult))
            dve.sem_inc(sem("t_ready"), 1)
            then(dve.tensor_tensor(v3(Hn), bc(vin[:, :], [P, NJ, D]), rowbc(w1row[:, :], NJ), ALU.mult))
            then(dve.scalar_tensor_tensor(Hn[:, :], Hn[:, :], 0.0, AG[:, :], ALU.max, ALU.add))
            dve.wait_ge(sem("carry_e"), 16)
            for s in range(2):
                dve.wait_ge(sem(f"ends_e{s}"), 16 * GT * NG // 2)
            K3 = 3 * AD + 1
            W0 = AD + 1
            carried = t1.rearrange("p (j d) -> p j d", d=NS)
            sums = t2.rearrange("p (j d) -> p j d", d=NS)
            maxima = t3.rearrange("p (j d) -> p j d", d=AD)

            def gather3(g, s, base):
                j = g * GT
                e = ends_e[:, bass.ds(j, GT), :]
                z = Z[:, s, 0:GT * K3].rearrange("p (j d) -> p j d", d=K3)
                hs = has[1][:, bass.ds(j, GT)]
                sp_ = span[1][:, bass.ds(j, GT)]
                step = Steps("l3_order", base)
                step(dve.tensor_tensor(carried, rowbc(CRE[:, 0:NS], GT), bc(sp_, [P, GT, NS]), ALU.mult))
                step(dve.tensor_tensor(sums, e[:, :, 0:NS], bc(hs, [P, GT, NS]), ALU.mult))
                step(dve.tensor_tensor(sums, sums, carried, ALU.add))
                if positive(g - 1):
                    dve.wait_ge(sem("z3t"), g - 1)
                dve.tensor_tensor(wsum[:, bass.ds(j, GT), :], sums[:, :, W0:W0 + 2], bc(hs, [P, GT, 2]), ALU.mult)
                dve.tensor_tensor(z[:, :, 0:AD], sums[:, :, 0:AD], bc(hs, [P, GT, AD]), ALU.mult)
                dve.tensor_tensor(z[:, :, 2 * AD:3 * AD], sums[:, :, 0:AD], bc(rcnt[:, bass.ds(j, GT)], [P, GT, AD]), ALU.mult)
                dve.tensor_scalar(z[:, :, 3 * AD:K3], bc(ucol[:, 0:1], [P, GT, 1]), 1.0, None, ALU.mult)
                step(dve.tensor_tensor(maxima, rowbc(CRE[:, NS:EW], GT), bc(pen2[:, bass.ds(j, GT)], [P, GT, AD]), ALU.add))
                step(dve.tensor_tensor(maxima, maxima, e[:, :, NS:EW], ALU.max))
                step(dve.tensor_tensor(z[:, :, AD:2 * AD], maxima, bc(hs, [P, GT, AD]), ALU.mult))
                assert step.k == 6
                dve.sem_inc(sem("z3_ready"), 1)

            def store3(g):
                dve.wait_ge(sem("o3"), g + 1)
                dve.tensor_tensor(ends_e[:, bass.ds(g * GT, GT), 0:D], zo, rowbc(b2[:, :], GT), ALU.add).then_inc(sem("l3_done"), 1)
            gather3(0, 0, 0)
            gather3(1, 1, 6)
            store3(0)
            with dve.Fori(1, NG // 2) as g:
                gather3(g * 2, 0, g * 12)
                store3(g * 2 - 1)
                gather3(g * 2 + 1, 1, g * 12 + 6)
                store3(g * 2)
            store3(NG - 1)
            dve.wait_ge(sem("l3_done"), NG)

            dve.wait_ge(sem("table_out"), 16 * (LAYERS + 2))
            then(dve.tensor_tensor(v3(T), bc(wsum[:, :, 0], [P, NJ, D]), rowbc(rcd[:, 0, :], NJ), ALU.mult))
            then(dve.tensor_tensor(v3(AG), bc(wsum[:, :, 1], [P, NJ, D]), rowbc(rcd[:, 1, :], NJ), ALU.mult))
            then(dve.tensor_tensor(T[:, :], T[:, :], AG[:, :], ALU.add))
            dve.sem_inc(sem("he_ready"), 1)
            gather_pass(N8, 6 * NIT)
            dve.wait_ge(sem("carry"), 16 * (LAYERS + 3))

            def rest2(g, ga, step):
                step(dve.tensor_tensor(ga, ga, group(T, g), ALU.add))
                step(dve.scalar_tensor_tensor(ga, ga, 0.0, group(Hn, g), ALU.max, ALU.add))
                step(dve.scalar_tensor_tensor(ga, ga, 0.0, group(X, g), ALU.max, ALU.add))
                step(dve.tensor_tensor(group(X, g), ga, ends_e[:, bass.ds(g * GT, GT), 0:D], ALU.add))
            base = LAYERS * NG * 8
            with dve.Fori(0, NG // 2) as g:
                per = g * (16 * GT) + 16 * GT * (3 * NG + 1)
                ends_sum(g * 2, 0, per, 1, g * 14 + base, rest2)
                ends_sum(g * 2 + 1, 1, per, 1, g * 14 + (base + 7), rest2)
            dve.sem_inc(sem("x_ready"), 1)


def ends_layer(pool, l, sem, dst, rows, idx, NG, GT):
    for g in range(NG):
        s = g % 2
        pool.wait_ge(sem(f"ends{s}"), (l * (NG // 2) + (NG + g // 2)) * (16 * GT))
        pool.sem_inc(sem("pool_turns"), 1)
        for k in range(GT):
            j = g * GT + k
            pool.indirect_dma_start(dst[:, j * D:(j + 1) * D], None, rows,
                                    bass.IndirectOffsetOnAxis(ap=idx[:, j:j + 1], axis=0)).then_inc(sem(f"ends{s}"), 16)


def kernel(**inputs):
    import numpy as np
    import concourse.bacc as bacc
    from concourse.bass_utils import run_bass_kernel_spmd as run

    i = {k: np.asarray(v) for k, v in inputs.items()}
    n, e = i["x"].shape[0], i["src"].shape[0]
    NJ, TILES = sizes(n, e)
    NP, EP = NJ * P, TILES * P

    def pad(x, rows, value=0):
        return np.concatenate([x, np.full((rows - x.shape[0],) + x.shape[1:], value, x.dtype)])

    def chunked(x):
        return np.ascontiguousarray(x.reshape(2, TILES // (2 * KC), KC, P).transpose(3, 1, 2, 0).reshape(P, TILES))

    src, dst = pad(i["src"], EP, NP - 1), pad(i["dst"], EP, NP - 1)
    w4_t = i["L2_gnn_W4"].T
    arrays = {
        "x": pad(i["x"], NP), "src_q": chunked(src), "dst_q": chunked(dst),
        "dst_ext": np.concatenate([np.full(1, -1, dst.dtype), dst])[None],
        "ew_q": chunked(pad(i["edge_weight"], EP)), "attr": pad(i["edge_attr_32"], EP),
        "v": pad(i["node_vec1"], NP), "poolw_t": i["L0_gnn_pool_w"].T, "pool_b": i["L0_gnn_pool_b"][:, None],
        "finalw_t": i["L0_gnn_final_w"].T, "final_b": i["L0_gnn_final_b"][None],
        "coef": i["L0_gnn_coef"].reshape(1, 1), "ws": i["L1_gnn_Ws"].reshape(-1, D),
        "bs": i["L1_gnn_bs"], "lnw": i["L1_gnn_ln_w"], "lnb": i["L1_gnn_ln_b"],
        "w1": i["L2_gnn_W1"], "w2": i["L2_gnn_W2"], "w3_t": i["L2_gnn_W3"].T, "w4_t": w4_t,
        "u": i["L3_gnn_u"][0:1], "l3w1": i["L3_gnn_W1"], "l3b1": i["L3_gnn_b1"][:, None],
        "l3w2": i["L3_gnn_W2"], "l3b2": i["L3_gnn_b2"][None],
    }
    arrays = {k: np.ascontiguousarray(v) for k, v in arrays.items()}
    nc = bacc.Bacc("TRN2", target_bir_lowering=False, num_devices=1)
    aps = {k: nc.dram_tensor(f"in_{k}", v.shape, mybir.dt.from_np(v.dtype), kind="ExternalInput").ap()
           for k, v in arrays.items()}
    out = nc.dram_tensor("out_x", (NP, D), F32, kind="ExternalOutput").ap()
    gnn_kernel(nc, n, e, aps, out)
    r = run(nc, [{f"in_{k}": v for k, v in arrays.items()}], core_ids=[0])
    return r.results[0]["out_x"][:n]
```

```python
import concourse.bass as bass
from concourse import mybir
from contextlib import ExitStack

F32 = mybir.dt.float32
BF16 = mybir.dt.bfloat16
I32 = mybir.dt.int32
ALU = mybir.AluOpType
ACT = mybir.ActivationFunctionType
AX = mybir.AxisListType
D = 64
AD = 32
P = 128
GT = 7
KC = 4
CE = KC * P
RW = D + AD + 4
C_DST, C_WP, C_WN, C_SRC = 96, 97, 98, 99
D0 = RW - D
A0 = D - AD - 4
NS = AD + 4
EW = NS + AD
BIG = 3.4028234e38
SELF = 1e33
EPS = 1e-5
LAYERS = 4


def sizes(n_nodes, n_edges):
    nj = -(-n_nodes // (P * GT * 2)) * GT * 2
    tiles = -(-n_edges // (P * KC * 8)) * KC * 8
    return nj, tiles


def positive(value):
    return not isinstance(value, int) or value > 0


def gnn_kernel(nc, n_nodes, n_edges, a, out):
    NJ, TILES = sizes(n_nodes, n_edges)
    NP = NJ * P
    EP = TILES * P
    H = EP // 2
    NCH = TILES // (2 * KC)
    NIT = NCH // 4
    NG = NJ // GT
    GW = GT * D
    assert NP > n_nodes or EP == n_edges
    assert NJ <= P and NIT > NG + 1 and LAYERS * NIT == NCH

    def dram(name, shape, dt):
        return nc.dram_tensor(name, shape, dt, kind="Internal").ap()

    table = dram("node_table", (NP, D), F32)
    fill = dram("fill_rows", (H, 2 * D), F32)
    rec = dram("records", (EP, RW), F32)
    runs = dram("runs", (H, 2 * D), F32)
    runs_l0 = dram("runs_l0", (H, 2 * D), F32)
    runs_e = dram("runs_e", (H, 2 * EW), F32)
    same_dst = dram("same_dst", (2, H), BF16)
    same_src = dram("same_src", (2, H), BF16)
    dst_by_src = dram("dst_by_src", (P, TILES), I32)
    counts = dram("counts", (2, NP), F32)
    starts = dram("starts", (2, NP), F32)

    ctx = ExitStack()
    with ctx:
        def sb(name, shape, dt=F32):
            return ctx.enter_context(nc.sbuf_tensor(name, shape, dt))

        sems = {}

        def sem(name):
            if name not in sems:
                sems[name] = ctx.enter_context(nc.semaphore(name))
            return sems[name]

        X = sb("X", [P, NJ * D])
        Hn = sb("Hn", [P, NJ * D])
        T = sb("T", [P, NJ * D])
        AGB = sb("AG", [P, max(NJ * D, 3 * TILES + 8)])
        AG = AGB[:, 0:NJ * D]
        EA = sb("EA", [P, max(4 * TILES, NJ * EW, 3 * CE + 8)])

        def v3(t, j0=0, n=NJ):
            return t[:, j0 * D:(j0 + n) * D].rearrange("p (j d) -> p j d", d=D)

        def group(t, g):
            return t[:, bass.ds(g * GW, GW)].rearrange("p (j d) -> p j d", d=D)

        s_q = EA[:, 0:TILES]
        pen_q = EA[:, TILES:2 * TILES]
        w_q = EA[:, 2 * TILES:3 * TILES]
        srcf_q = EA[:, 3 * TILES:4 * TILES]
        KEYS = AGB[:, 0:2 * (TILES + KC)].bitcast(BF16).rearrange("p (i t) -> p i t", i=4)
        dstf_q = AGB[:, 2 * (TILES + KC):2 * (TILES + KC) + TILES]
        SI = srcf_q.bitcast(I32)
        DI = pen_q.bitcast(I32)
        tmp_i = dstf_q.bitcast(I32)

        G = sb("G", [P, 4, KC * P])
        M = sb("M", [P, 2, 2 * CE], BF16)
        L = sb("L", [P, 2, CE])
        S = sb("S", [P, 2, CE])
        R = sb("R", [P, 4, CE])
        RT = sb("RT", [P, 4, 8, RW])
        RTf = RT[:, :, :, :].rearrange("p s q r -> p (s q r)")
        Gs = RTf[:, 0:2 * CE].rearrange("p (s e) -> p s e", s=2)
        IDX = sb("IDX", [P, 4, 8], I32)
        OH = sb("OH", [P, 2, 4, KC, P], BF16)
        OHTs = R[:, 0:2, :]
        Cs = R[:, 2, 0:2 * P].rearrange("p (s l) -> p s l", s=2)
        Lf = L[:, :, :].rearrange("p s e -> p (s e)")
        junk_rank = Lf.rearrange("p (x k e) -> p x k e", x=2, k=KC)
        Gf = G[:, :, :].rearrange("p s e -> p (s e)")
        Rf = R[:, :, :].rearrange("p s e -> p (s e)")
        DX = Gf[:, 0:TILES + 1].bitcast(I32)
        MD = Rf[:, 0:TILES // 2].bitcast(BF16)
        assert TILES < 4 * CE
        inr = sb("inr", [P, 2, 2, KC])
        lku = sb("lku", [P, 2, KC])
        off = [0]

        def ea(cols):
            o = off[0]
            off[0] += cols
            return EA[:, o:o + cols]
        KS = [ea(CE + 4) for _ in range(2)]
        MK = [ea(CE // 2).bitcast(BF16) for _ in range(2)]
        ends_e = EA[:, 0:NJ * EW].rearrange("p (j d) -> p j d", d=EW)
        rt_off = [0]

        def rtf(cols):
            o = rt_off[0]
            rt_off[0] += cols
            return RTf[:, o:o + cols]
        E_WIN = rtf(CE)
        E_MASK = rtf(CE // 2).bitcast(BF16)
        E_PEN = rtf(CE)
        E_SUM, E_MAX = rtf(CE), rtf(CE)
        E_OUT = rtf(2 * KC * EW)
        assert rt_off[0] <= 4 * 8 * RW
        E_KEEP = sb("E_KEEP", [P, 2])
        Z = sb("Z", [P, 2, GT * P])
        junk_look = Z[:, :, :].rearrange("p a b -> p (a b)")[:, 0:8 * P].rearrange("p (x k e) -> p x k e", x=2, k=KC)
        ZTs = Gf[:, 0:GT * P]
        ZP = [Gf[:, i * GT * P:(i + 1) * GT * P] for i in range(2)]
        rt_off[0] = 0
        Z3Ts, HS = rtf(GT * P), rtf(GT * P)
        t1, t2, t3 = rtf(GT * NS), rtf(GT * NS), rtf(GT * AD)
        CARG = L[:, 0, 0:GW]
        LW = L[:, 1, 0:GW]
        CR = sb("CR", [P, D])
        CR2 = sb("CR2", [P, D])
        CRE = sb("CRE", [P, EW])

        def node(name, dt=F32):
            return sb(name, [P, NJ], dt)

        cnt = [node("cnt_dst"), node("cnt_src")]
        beg = [node("beg_dst"), node("beg_src")]
        has = [node("has_dst"), node("has_src")]
        span = [node("span_dst"), node("span_src")]
        endrow = [node("endrow_dst", I32), node("endrow_src", I32)]
        begrow = node("begrow", I32)
        dinv = node("dinv")
        rcnt = node("rcnt")
        pen2 = node("pen2")
        valid = node("valid")
        vpos = node("vpos")
        vneg = node("vneg")
        vin = node("vin")
        wsum = sb("wsum", [P, NJ, 2])
        na = node("na")
        nb = node("nb")
        nd = node("nd")
        gsum = sb("gsum", [P, NG])
        st = sb("st", [P, 8])
        iota_i = sb("iota_i", [P, P], I32)
        pidx_i = sb("pidx_i", [P, 1], I32)
        iota_f = sb("iota_f", [P, P])
        iota_b = sb("iota_b", [P, P], BF16)
        pidx = sb("pidx", [P, 1])
        ident = sb("ident", [P, P])
        ident_b = sb("ident_b", [P, P], BF16)
        earlier = sb("earlier", [P, P])
        below = sb("below", [P, P])
        ones = sb("ones", [P, P])
        zero_rows = Z[:, :, :].rearrange("p a b -> p (a b)")
        HC = sb("HC", [P, 4, P])
        hoff = sb("hoff", [P, 2])
        dh = sb("dh", [1, 1], I32)
        poolw = sb("poolw", [P, P])
        finalw = sb("finalw", [2 * D, D])
        w3 = sb("w3", [P, P])
        w4 = sb("w4", [D, 3, D])
        w4c = sb("w4c", [D + 2, D])
        l3w1 = sb("l3w1", [3 * AD + 1, P])
        l3w2 = sb("l3w2", [P, D])
        l3b1 = sb("l3b1", [P, 1])
        wl = sb("wl", [P, P])
        lcols = sb("lcols", [P, 2])
        pcols = sb("pcols", [P, 2])
        lrows = sb("lrows", [P, 3, D])
        lnwr = sb("lnwr", [P, D])
        poolb = sb("poolb", [P, 1])
        fb = sb("fb", [P, D])
        b2 = sb("b2", [P, D])
        w1row = sb("w1row", [P, D])
        w12c = sb("w12c", [D, 2])
        w12r = sb("w12r", [D, 4])
        rcd = sb("rcd", [P, 2, D])
        coef = sb("coef", [P, 1])
        ucol = sb("ucol", [P, 1])

        PS = ctx.enter_context(nc.psum_tensor("PS", [P, 8 * 512], F32))

        def bank(i, n=1):
            return PS[:, i * 512:(i + n) * 512]

        def bc(ap, shape):
            while len(ap.shape) < len(shape):
                ap = ap.unsqueeze(len(ap.shape))
            return ap.broadcast_to(shape)

        def rowbc(row, mid):
            return row.unsqueeze(1).broadcast_to([P, mid, row.shape[1]])

        def dbc(ap, n):
            return bass.AP(tensor=ap.tensor, offset=ap.offset, ap=[[0, n], [1, ap.shape[-1]]])

        runs64 = runs.rearrange("r (h d) -> (r h) d", d=D)
        runs_l064 = runs_l0.rearrange("r (h d) -> (r h) d", d=D)
        runs_e_rows = runs_e.rearrange("r (h d) -> (r h) d", d=EW)
        fill64 = fill.rearrange("r (h d) -> (r h) d", d=D)

        block = ctx.enter_context(nc.Block())
        W = {"params": 0}
        N1, N2, N3, N4, N8 = 0, NCH, 2 * NCH, 3 * NCH, 7 * NCH
        QB, QE = 0, NG
        NG2, GW2 = NG // 2, 2 * GW
        UA, UC, UD = 0, NG2, (LAYERS + 1) * NG2
        LIN = 7 * 16
        TP = NG2 * 16
        assert 2 * CE <= 2 * GT * P

        @block.sync
        def _(sp):
            def load(dst, src):
                sp.dma_start(dst, src).then_inc(sem("params"), 16)
                W["params"] += 16

            load(X[:, :], a["x"].rearrange("(p j) d -> p (j d)", p=P))
            load(SI, a["src_q"])
            load(DI, a["dst_q"])
            load(DX, bass.AP(tensor=a["dst_ext"].tensor, offset=0, ap=[[TILES, P], [1, TILES + 1]]))
            load(w_q, a["ew_q"])
            sp.wait_ge(sem("w_zero"), 1)
            for h in range(2):
                load(poolw[h * D:(h + 1) * D, h * D:(h + 1) * D], a["poolw_t"])
                load(w3[h * D:(h + 1) * D, h * D:(h + 1) * D], a["w3_t"])
            load(finalw[:, :], a["finalw_t"])
            for i in range(3):
                load(w4[:, i, :], a["w4_t"][i * D:(i + 1) * D, :])
            load(w4c[2:D + 2, :], a["w4_t"][2 * D:3 * D, :])
            load(l3w1[:, :], a["l3w1"])
            load(l3w2[:, :], a["l3w2"])
            load(l3b1[:, :], a["l3b1"])
            load(poolb[0:D, :], a["pool_b"])
            load(poolb[D:P, :], a["pool_b"])
            load(fb[:, :], dbc(a["final_b"], P))
            load(b2[:, :], dbc(a["l3b2"], P))
            load(w1row[:, :], dbc(a["w1"].rearrange("d o -> o d"), P))
            load(w12c[:, 0:1], a["w1"])
            load(w12c[:, 1:2], a["w2"])
            load(coef[:, :], dbc(a["coef"], P))
            load(ucol[:, :], dbc(a["u"], P))
            load(vin[:, :], a["v"].rearrange("(p j) o -> p (j o)", p=P))

            def table_out(n):
                sp.wait_ge(sem("t_ready"), n)
                sp.sem_inc(sem("sp_turns"), 1)
                sp.dma_start(table.rearrange("(p j) d -> p (j d)", p=P), T[:, :]).then_inc(sem("table_out"), 16)

            def table_parts(n0):
                rows = table.rearrange("(p j) d -> p (j d)", p=P)
                for s in range(NG2):
                    sp.wait_ge(sem("pair_used"), n0 + s + 1)
                    sp.sem_inc(sem("sp_turns"), 1)
                    sp.dma_start(rows[:, s * GW2:(s + 1) * GW2], T[:, s * GW2:(s + 1) * GW2]).then_inc(sem("table_out"), 16)

            sp.wait_ge(sem("md_ready"), 1)
            sp.dma_start(same_dst.rearrange("h (q t) -> (h q) t", t=TILES), MD).then_inc(sem("same_dst"), 16)
            table_parts(UA)
            def masks_in(masks, c, slot, lo):
                if positive(lo):
                    sp.wait_ge(sem("scanned"), lo)
                sp.sem_inc(sem("sp_turns"), 1)
                for h in range(2):
                    src = masks[h:h + 1, bass.ds(c * CE, 2 * CE)]
                    sp.dma_start(M[h * D:(h + 1) * D, slot, :],
                                 src.broadcast_to([D, 2 * CE])).then_inc(sem(f"masks_in{slot}"), 16)

            def runs_out(dst, c, i, n):
                sp.wait_ge(sem("r_ready"), n + 1)
                sp.sem_inc(sem("sp_turns"), 1)
                rows = dst[bass.ds(c * CE, CE), :].rearrange("(k p) d -> p k d", p=P)
                sp.dma_start(rows, R[:, i, :].rearrange("p (k d) -> p k d", k=KC)).then_inc(sem(f"runs_out{i}"), 16)

            def attr_out(d):
                sp.wait_ge(sem("e_ready"), d + 1)
                sp.sem_inc(sem("sp_turns"), 1)
                rows = runs_e[bass.ds(d * CE, CE), :].rearrange("(k p) d -> p k d", p=P)
                sp.dma_start(rows, E_OUT.rearrange("p (k d) -> p k d", k=KC)).then_inc(sem("e_out"), 16)
                sp.wait_ge(sem("e_out"), d * 16 + 16)
                sp.sem_inc(sem("sp_turns"), 1)

            def attr_in(d):
                for h in range(2):
                    rows = rec[bass.ds(d * CE + h * H, CE), :].rearrange("(k p) d -> p k d", p=P)
                    sp.dma_start(E_WIN.rearrange("p (k h d) -> p k h d", k=KC, h=2)[:, :, h, :],
                                 rows[:, :, D0:RW]).then_inc(sem("e_in"), 16)
                    sp.dma_start(E_MASK[h * D:(h + 1) * D, :],
                                 same_src[h:h + 1, bass.ds(d * CE, CE)].broadcast_to([D, CE])).then_inc(sem("e_in"), 16)

            def gather_pass(masks, idx, dst, n0, g0, first_of_sem, attr=None):
                r0 = n0 if isinstance(n0, int) and n0 == 0 else n0 - NCH
                def step(it, i, lead):
                    c = it * 4 + i
                    if lead != "last":
                        if lead != "first":
                            sp.wait_ge(sem(f"{g0}{i}"), (it + first_of_sem) * 128)
                            sp.sem_inc(sem("sp_turns"), 1)
                        sp.dma_start(IDX[:, i, :], idx[:, bass.ds(c * 8, 8)]).then_inc(sem(f"idx_in{i}"), 16)
                        if i % 2 == 0:
                            masks_in(masks, c, i // 2, c + n0 - 2)
                    if lead != "first":
                        runs_out(dst, c - 4, i, c - 4 + r0)
                    if attr is not None and i == 3:
                        if lead != "first":
                            attr_out(attr + (it - 1))
                        if lead != "last":
                            attr_in(attr + it)
                for i in range(4):
                    step(0, i, "first")
                with sp.Fori(1, NIT) as it:
                    for i in range(4):
                        step(it, i, "mid")
                for i in range(4):
                    step(NIT, i, "last")

            gather_pass(same_dst, a["src_q"], runs_l0, N1, "gath_a", 0)

            for i in range(2):
                sp.wait_ge(sem("starts_ready"), i + 1)
                sp.dma_start(counts[i:i + 1, :].rearrange("o (h l) -> (o h) l", l=P), HC[0:NJ, i, :]).then_inc(sem("starts_out"), 16)
                sp.dma_start(starts[i:i + 1, :].rearrange("o (h l) -> (o h) l", l=P), HC[0:NJ, 2 + i, :]).then_inc(sem("starts_out"), 16)
            sp.wait_ge(sem("starts_out"), 64)
            for i in range(2):
                sp.dma_start(cnt[i][:, :], counts[i:i + 1, :].rearrange("o (p j) -> (o p) j", p=P)).then_inc(sem("starts_in"), 16)
                sp.dma_start(beg[i][:, :], starts[i:i + 1, :].rearrange("o (p j) -> (o p) j", p=P)).then_inc(sem("starts_in"), 16)
            sp.dma_start(dh[0:1, 0:1], a["dst_ext"][:, H + 1:H + 2]).then_inc(sem("dh_in"), 16)
            sp.wait_ge(sem("dh_in"), 16)
            node_h = sp.value_load(dh[0:1, 0:1], min_val=0, max_val=NP - 1)
            sp.wait_ge(sem("filled"), 16 * NJ)
            sp.dma_start(fill64[1:2, :], table[bass.ds(node_h, 1), :]).then_inc(sem("fill_b"), 16)
            sp.wait_ge(sem("fill_b"), 16)

            def step2(it, i, first):
                c = it * 4 + i
                sp.wait_ge(sem("fwd"), c + N2 - 3)
                sp.sem_inc(sem("sp_turns"), 1)
                rows = fill[bass.ds(c * CE, CE), :].rearrange("(k p) d -> p k d", p=P)
                sp.dma_start(G[:, i, :].rearrange("p (k d) -> p k d", k=KC), rows).then_inc(sem(f"fill_in{i}"), 16)
                if i % 2 == 0:
                    masks_in(same_dst, c, i // 2, c + N2 - 2)
                if not first:
                    sp.wait_ge(sem(f"scattered{i}"), it * 128)
                    sp.sem_inc(sem("sp_turns"), 1)
                rt = RT[:, i, :, :].rearrange("p (k h) r -> p k h r", h=2)
                for h in range(2):
                    rows = a["attr"][bass.ds(c * CE + h * H, CE), :].rearrange("(k p) d -> p k d", p=P)
                    sp.dma_start(rt[:, :, h, D:D + AD], rows).then_inc(sem(f"attr_in{i}"), 16)
            for i in range(4):
                step2(0, i, True)
            with sp.Fori(1, NIT) as it:
                for i in range(4):
                    step2(it, i, False)

            for i in range(4):
                sp.wait_ge(sem(f"scattered{i}"), NIT * 128)

            def step3(it, i, first):
                c = it * 4 + i
                if not first:
                    sp.wait_ge(sem("fwd3"), c - 3)
                    sp.sem_inc(sem("sp_turns"), 1)
                    sp.wait_ge(sem("dst_ready"), c - 3)
                    sp.sem_inc(sem("sp_turns"), 1)
                rt = RT[:, i, :, :].rearrange("p (k h) r -> p k h r", h=2)
                for h in range(2):
                    rows = rec[bass.ds(c * CE + h * H, CE), :].rearrange("(k p) d -> p k d", p=P)
                    sp.dma_start(G[:, i, :].rearrange("p (k h d) -> p k h d", k=KC, h=2)[:, :, h, :],
                                 rows[:, :, 0:D]).then_inc(sem(f"rec_in{i}"), 16)
                    sp.dma_start(rt[:, :, h, D + AD:RW], rows[:, :, D + AD:RW]).then_inc(sem(f"rec_in{i}"), 16)
            for i in range(4):
                step3(0, i, True)
            with sp.Fori(1, NIT) as it:
                for i in range(4):
                    step3(it, i, False)

            def carry_in(dst, src, n):
                sp.dma_start(dst, src).then_inc(sem("carry"), 16)

            for i in range(4):
                sp.wait_ge(sem(f"runs_out{i}"), 16 * NIT * 2)
            carry_in(CR[:, :], dbc(runs_l0[H - 1:H, 0:D], P), 0)
            carry_in(CR2[:, :], dbc(runs[H - 1:H, 0:D], P), 0)
            for i in range(2):
                sp.wait_ge(sem(f"same_src{i}"), 8 * NCH)
                sp.wait_ge(sem(f"dst_out{i}"), 8 * NCH)

            def weights_in(l):
                for h in range(2):
                    sp.dma_start(wl[h * D:(h + 1) * D, h * D:(h + 1) * D], a["ws"][bass.ds(l * D, D), :]).then_inc(sem("wl_in"), 16)

            weights_in(0)
            with sp.Fori(0, LAYERS) as l:
                sp.wait_ge(sem("h_ready"), l + 1)
                sp.sem_inc(sem("sp_turns"), 1)
                for h in range(2):
                    for i, nm in enumerate(("lnw", "lnb")):
                        sp.dma_start(lcols[h * D:(h + 1) * D, i:i + 1],
                                     a[nm][bass.ds(l, 1), :].rearrange("o d -> d o")).then_inc(sem("layer_in"), 16)
                for i, nm in enumerate(("bs", "lnw", "lnb")):
                    sp.dma_start(lrows[:, i, :], a[nm][bass.ds(l, 1), :].broadcast_to([P, D])).then_inc(sem("layer_in"), 16)
                table_parts(UC + l * NG2)
                weights_in(l + 1)
                gather_pass(same_dst, a["src_q"], runs, N4 + l * NCH, "gath_b", l * NIT, l * NIT)
                for i in range(4):
                    sp.wait_ge(sem(f"runs_out{i}"), 16 * NIT * (l + 3))
                    sp.sem_inc(sem("sp_turns"), 1)
                sp.wait_ge(sem("carry_used"), l + 1)
                sp.sem_inc(sem("sp_turns"), 1)
                carry_in(CR[:, :], dbc(runs[H - 1:H, 0:D], P), 0)

            sp.dma_start(CRE[:, :], dbc(runs_e[H - 1:H, 0:EW], P)).then_inc(sem("carry_e"), 16)
            table_out(1)
            gather_pass(same_src, dst_by_src, runs, N8, "gath_c", 0)
            for i in range(4):
                sp.wait_ge(sem(f"runs_out{i}"), 16 * NIT * 7)
            sp.wait_ge(sem("carry_used"), LAYERS + 1)
            carry_in(CR[:, :], dbc(runs[H - 1:H, 0:D], P), 0)

            for s in range(NG2):
                sp.wait_ge(sem("x_ready"), s + 1)
                sp.dma_start(out.rearrange("(p j) d -> p (j d)", p=P)[:, s * GW2:(s + 1) * GW2],
                             X[:, s * GW2:(s + 1) * GW2]).then_inc(sem("out"), 16)
            sp.wait_ge(sem("out"), 16 * NG2)

        @block.gpsimd
        def _(pool):
            pool.iota(iota_i[:, :], [[1, P]], base=0, channel_multiplier=0).then_inc(sem("iota"), 1)
            pool.iota(pidx_i[:, :], [[0, 1]], base=0, channel_multiplier=1).then_inc(sem("iota"), 1)
            pool.iota(na[:, :].bitcast(I32), [[1, NJ]], base=0, channel_multiplier=NJ).then_inc(sem("iota"), 1)

            def gather_pass(used, n0, name, done, tables):
                pool.wait_ge(sem("table_out"), tables)
                pool.sem_inc(sem("pool_turns"), 1)

                def step(it, i):
                    c = it * 4 + i
                    pool.wait_ge(sem(f"idx_in{i}"), (it + done) * 16 + 16)
                    pool.sem_inc(sem("pool_turns"), 1)
                    if positive(c + n0 - 3):
                        pool.wait_ge(sem(used), c + n0 - 3)
                    pool.sem_inc(sem("pool_turns"), 1)
                    for q in range(8):
                        pool.indirect_dma_start(
                            G[:, i, q * D:(q + 1) * D], None, table,
                            bass.IndirectOffsetOnAxis(ap=IDX[:, i, q:q + 1], axis=0)).then_inc(sem(f"{name}{i}"), 16)
                for i in range(4):
                    step(0, i)
                with pool.Fori(1, NIT) as it:
                    for i in range(4):
                        step(it, i)

            gather_pass("g_used", 0, "gath_a", 0, TP)

            pool.wait_ge(sem("fill_zero"), 16 * NCH // 2)
            pool.wait_ge(sem("rows_ready"), 1)
            for j in range(NJ):
                pool.indirect_dma_start(
                    fill64, bass.IndirectOffsetOnAxis(ap=begrow[:, j:j + 1], axis=0),
                    T[:, j * D:(j + 1) * D], None, bounds_check=EP - 1, oob_is_err=False).then_inc(sem("filled"), 16)

            def scatter(it, i):
                pool.wait_ge(sem(f"attr_in{i}"), it * 32 + 32)
                pool.sem_inc(sem("pool_turns"), 1)
                pool.wait_ge(sem("pay_ready"), it * 4 + i + 1)
                pool.sem_inc(sem("pool_turns"), 1)
                pool.wait_ge(sem("msg_ready"), it * 4 + i + 1)
                pool.sem_inc(sem("pool_turns"), 1)
                pool.wait_ge(sem("pos_ready"), it * 4 + i + 1)
                pool.sem_inc(sem("pool_turns"), 1)
                for q in range(8):
                    pool.indirect_dma_start(
                        rec, bass.IndirectOffsetOnAxis(ap=IDX[:, i, q:q + 1], axis=0),
                        RT[:, i, q, :], None).then_inc(sem(f"scattered{i}"), 16)
            with pool.Fori(0, NIT) as it:
                for i in range(4):
                    scatter(it, i)

            def ends(dst, rows, idx, n):
                for g in range(NG):
                    s = g % 2
                    done = (n + g) // 2 * 16 * GT
                    if positive(done):
                        pool.wait_ge(sem(f"ends{s}"), done)
                    pool.sem_inc(sem("pool_turns"), 1)
                    for k in range(GT):
                        j = g * GT + k
                        pool.indirect_dma_start(dst[:, j * D:(j + 1) * D], None, rows,
                                                bass.IndirectOffsetOnAxis(ap=idx[:, j:j + 1], axis=0)).then_inc(sem(f"ends{s}"), 16)

            def runs_done(n):
                for i in range(4):
                    pool.wait_ge(sem(f"runs_out{i}"), 16 * NIT * n)
                    pool.sem_inc(sem("pool_turns"), 1)

            runs_done(1)
            for i in range(4):
                pool.wait_ge(sem(f"scattered{i}"), NIT * 128)
                pool.sem_inc(sem("pool_turns"), 1)
            ends(T, runs_l064, endrow[0], 0)

            runs_done(2)
            ends(AG, runs64, endrow[1], NG)

            with pool.Fori(0, LAYERS) as l:
                gather_pass("fwd", N4 - NCH + l * NCH, "gath_b", (l + 1) * NIT, l * TP + 2 * TP)
                runs_done(l + 3)
                pool.wait_ge(sem("h_ready"), l + 1)
                pool.sem_inc(sem("pool_turns"), 1)
                ends_layer(pool, l, sem, AG, runs64, endrow[0], NG, GT)
            pool.wait_ge(sem("e_out"), 16 * NCH)
            for g in range(NG):
                s = g % 2
                if g >= 2:
                    pool.wait_ge(sem(f"ends_e{s}"), g // 2 * 16 * GT)
                pool.sem_inc(sem("pool_turns"), 1)
                for k in range(GT):
                    j = g * GT + k
                    pool.indirect_dma_start(EA[:, j * EW:(j + 1) * EW], None, runs_e_rows,
                                            bass.IndirectOffsetOnAxis(ap=endrow[1][:, j:j + 1], axis=0)).then_inc(sem(f"ends_e{s}"), 16)
            gather_pass("fwd", N8 - NCH, "gath_c", 5 * NIT, (LAYERS + 1) * TP + 16)
            runs_done(7)
            pool.wait_ge(sem("he_ready"), 1)
            ends(AG, runs64, endrow[1], 6 * NG)

        @block.tensor
        def _(pe):
            def fwd(i, src, n, arrived, value):
                pe.wait_ge(arrived, value)
                if positive(n - 1):
                    pe.wait_ge(sem("pt_free"), n - 1)
                for k in range(KC):
                    t = pe.transpose(bank(i % 2)[:, k * P:(k + 1) * P], src[:, k * P:(k + 1) * P], ident[:, :])
                return t.then_inc(sem("fwd"), 1)

            def back(i, n, r):
                pe.wait_ge(sem("scanned"), n + 1)
                if positive(r - 1):
                    pe.wait_ge(sem("r_ready"), r - 1)
                for k in range(KC):
                    t = pe.transpose(bank(2 + i % 2)[:, k * P:(k + 1) * P], S[:, i % 2, k * P:(k + 1) * P], ident[:, :])
                t.then_inc(sem("back"), 1)

            def project(K, rhs, n0):
                def step(n, s):
                    pe.wait_ge(sem("z_ready"), n + 1)
                    if positive(n):
                        pe.wait_ge(sem("zts_ready"), n)
                    pe.sem_inc(sem("pe_turns"), 1)
                    for k in range(GT):
                        t = pe.transpose(PS[0:K, k * P:(k + 1) * P], Z[:, s, k * K:(k + 1) * K], ident[:, :])
                    t.then_inc(sem("zt"), 1)
                    pe.wait_ge(sem("zts_ready"), n + 1)
                    if positive(n):
                        pe.wait_ge(sem("zo_used"), n)
                    for k in range(GT):
                        t = pe.matmul(bank(2)[:, k * D:(k + 1) * D], ZTs[0:K, k * P:(k + 1) * P], rhs, start=True, stop=True)
                    t.then_inc(sem("zo"), 1)
                if isinstance(n0, int) and n0 == 0:
                    step(0, 0)
                    step(1, 1)
                    with pe.Fori(1, NG // 2) as g:
                        step(g * 2, 0)
                        step(g * 2 + 1, 1)
                else:
                    with pe.Fori(0, NG // 2) as g:
                        step(g * 2 + n0, 0)
                        step(g * 2 + n0 + 1, 1)

            def attr_fwd(d):
                pe.wait_ge(sem("e_in"), d * 64 + 64)
                for k in range(KC):
                    t = pe.transpose(bank(5)[:, k * P:(k + 1) * P], E_WIN[:, k * P:(k + 1) * P], ident[:, :])
                t.then_inc(sem("e_fwd"), 1)

            def attr_back(d):
                pe.wait_ge(sem("e_scanned"), d * 2 + 2)
                for m, src in enumerate((E_SUM, E_MAX)):
                    for k in range(KC):
                        t = pe.transpose(bank(6 + m)[:, k * P:(k + 1) * P], src[:, k * P:(k + 1) * P], ident[:, :])
                t.then_inc(sem("e_back"), 1)

            def pair_banks(s, base):
                return PS[:, (s % 2 * 4 + base) * 512:(s % 2 * 4 + base) * 512 + GT * P]

            def project_pairs(n0, w):
                def products(s):
                    pe.wait_ge(sem("pair_in"), n0 + s + 1)
                    if s >= 2:
                        pe.wait_ge(sem("pair_used"), n0 + s - 1)
                    for k in range(GT):
                        t = pe.matmul(pair_banks(s, 2)[:, k * P:(k + 1) * P], ZP[s % 2][:, k * P:(k + 1) * P], w[:, :],
                                      start=True, stop=True)
                    t.then_inc(sem("pair_out"), 1)
                for s in range(NG2):
                    if s >= 2:
                        pe.wait_ge(sem("pair_in"), n0 + s - 1)
                    for k in range(GT):
                        t = pe.transpose(pair_banks(s, 0)[:, k * P:(k + 1) * P],
                                         Hn[:, s * GW2 + k * P:s * GW2 + (k + 1) * P], ident[:, :])
                    t.then_inc(sem("pair_t"), 1)
                    if s:
                        products(s - 1)
                products(NG2 - 1)

            def gather_pass(n0, name, done, attr=None, beside=None):
                def step(it, i, first):
                    c = it * 4 + i
                    fwd(i, G[:, i, :], c + n0 - NCH, sem(f"{name}{i}"), (it + done) * 128 + 128)
                    if not (first and i == 0):
                        back((i - 1) % 4, c + n0 - 1, c + n0 - 1 - NCH)
                    if attr is not None and i == 1:
                        attr_fwd(attr + it)
                    if attr is not None and i == 3:
                        attr_back(attr + it)
                for i in range(4):
                    step(0, i, True)
                if beside is not None:
                    with pe.Fori(1, NG + 1) as it:
                        for i in range(4):
                            step(it, i, False)
                            beside(it - 1, i)
                with pe.Fori(1 if beside is None else NG + 1, NIT) as it:
                    for i in range(4):
                        step(it, i, False)
                back(3, n0 + (NCH - 1), n0 - 1)

            pe.wait_ge(sem("consts"), 1)
            pe.wait_ge(sem("params"), W["params"])
            pe.wait_ge(sem("w12_ready"), 1)
            pe.matmul(bank(4)[0:2, 0:D], w12r[:, 0:2], w4[:, 0, :], start=True, stop=True).then_inc(sem("w4_small"), 1)
            for i in range(2):
                pe.matmul(bank(5 + i)[:, 0:D], w12r[:, 2 + i:3 + i].broadcast_to([D, P]), w4[:, 1, :],
                          start=True, stop=True).then_inc(sem("w4_small"), 1)
            pe.wait_ge(sem("w4_copied"), 1)
            pe.wait_ge(sem("hn_ready"), 1)
            project_pairs(UA, poolw)

            pe.wait_ge(sem("hist_zero"), 1)
            for b in range(2):
                pe.matmul(bank(4 + b)[0:NJ, 0:P], ident[:, 0:NJ], HC[:, 0, :], start=True, stop=False, skip_group_check=True)

            def hist(n, s):
                pe.wait_ge(sem("oh_ready"), n + 1)
                for b in range(2):
                    for k in range(KC):
                        t = pe.matmul(bank(4 + b)[0:NJ, 0:P], OH[:, s, 2 * b, k, 0:NJ], OH[:, s, 2 * b + 1, k, :],
                                      start=False, stop=False, skip_group_check=True)
                t.then_inc(sem("hist_done"), 1)

            def step1(it, i, first):
                c = it * 4 + i
                fwd(i, Gs[:, i % 2, :], c, sem("gs_ready"), c + 1)
                hist(c * 2, 0)
                if not (first and i == 0):
                    back((i - 1) % 4, c - 1, c - 1)
                hist(c * 2 + 1, 1)
            for i in range(4):
                step1(0, i, True)
            with pe.Fori(1, NIT) as it:
                for i in range(4):
                    step1(it, i, False)
            back(3, NCH - 1, NCH - 1)
            for b in range(2):
                pe.matmul(bank(4 + b)[0:NJ, 0:P], ident[:, 0:NJ], HC[:, 0, :], start=False, stop=True,
                          skip_group_check=True).then_inc(sem("hist_sum"), 1)

            pe.wait_ge(sem("row_sums"), 1)
            pe.matmul(bank(6)[0:NJ, 0:2], below[0:NJ, 0:NJ], hoff[0:NJ, :], start=True, stop=True).then_inc(sem("row_offs"), 1)

            pe.wait_ge(sem("starts_ready"), 2)
            pe.wait_ge(sem("r_ready"), NCH)
            pe.matmul(bank(3)[0:NJ, 0:P], ident[0:NJ, 0:NJ], HC[0:NJ, 3, :], start=True, stop=False,
                      skip_group_check=True).then_inc(sem("counted"), 1)
            HB = 2 * NCH

            def digit(h, s, d, k):
                return OH[:, s // 2, 2 * (s % 2) + d, k, :]

            def key_col(i, q):
                return RT[:, i, q, C_SRC:C_SRC + 1].broadcast_to([P, P])

            def turn(h, s):
                pe.wait_ge(sem("oh_ready"), h + HB + 1)
                if positive(h):
                    pe.wait_ge(sem("oht_copied"), h)
                ohb = bank(5).bitcast(BF16)
                for k in range(KC):
                    t = pe.transpose(ohb[0:NJ, k * P:(k + 1) * P], digit(h, s, 0, k)[:, 0:NJ], ident_b[:, :])
                t.then_inc(sem("oht"), 1)

            def src_row(h, s, k):
                t = pe.matmul(bank(4 - 2 * (s % 2))[:, k * P:(k + 1) * P], key_col(s // 2, s % 2 * KC + k), ident[:, :],
                              start=True, stop=True)
                if k == KC - 1:
                    t.then_inc(sem("src_rows"), 1)

            def rows_free(h, c):
                pe.wait_ge(sem("pay_ready"), c + 1)
                if positive(h - 1):
                    pe.wait_ge(sem("ranked"), h - 1)

            def chain(c, i, x, last):
                h, s = c * 2 + x, i % 2 * 2 + x
                h_slot, n_slot = (i * 2 + x) % 4, (i * 2 + x + 1) % 4
                if positive(h - 1):
                    pe.wait_ge(sem("looked"), h - 1)
                for k in range(KC):
                    pe.wait_ge(sem("c_copied"), h * KC + k + 1)
                    pe.matmul(bank(3)[0:NJ, 0:P], digit(h, h_slot, 0, k)[:, 0:NJ], digit(h, h_slot, 1, k),
                              start=False, stop=False, skip_group_check=True).then_inc(sem("counted"), 1)
                    if k == 0:
                        pe.wait_ge(sem("oht_copied"), h + 1)
                    t = pe.matmul(bank(6 + x)[:, k * P:(k + 1) * P], OHTs[0:NJ, x, k * P:(k + 1) * P], Cs[0:NJ, k % 2, :],
                                  start=True, stop=True)
                    if k == KC - 1:
                        t.then_inc(sem("lookups"), 1)
                    if not last:
                        if k == 0:
                            turn(h + 1, n_slot)
                            rows_free(h + 1, c + x)
                        n = i * 2 + x + 1
                        src_row(h + 1, n % 8, k)

            def fwd2(it, i):
                pe.wait_ge(sem(f"fill_in{i}"), it * 16 + 16)
                pe.wait_ge(sem("pt_free"), it * 4 + i + N2)
                for k in range(KC):
                    t = pe.transpose(bank(0)[:, k * P:(k + 1) * P], G[:, i, k * P:(k + 1) * P], ident[:, :])
                t.then_inc(sem("fwd"), 1)

            def back2(n, i):
                pe.wait_ge(sem("scanned"), n + N2 + 1)
                if positive(n):
                    pe.wait_ge(sem("msg_ready"), n)
                for k in range(KC):
                    t = pe.transpose(bank(1)[:, k * P:(k + 1) * P], S[:, i % 2, k * P:(k + 1) * P], ident[:, :])
                t.then_inc(sem("back2"), 1)

            def step2(it, i, last):
                c = it * 4 + i
                end = last and i == 3
                chain(c, i, 0, False)
                back2(c, i)
                if not end:
                    fwd2(it + (i + 1) // 4, (i + 1) % 4)
                chain(c, i, 1, end)
            fwd2(0, 0)
            turn(0, 0)
            rows_free(0, 0)
            for k in range(KC):
                src_row(0, 0, k)
            for i in range(4):
                step2(0, i, False)
            with pe.Fori(1, NIT - 1) as it:
                for i in range(4):
                    step2(it, i, False)
            for i in range(4):
                step2(NIT - 1, i, True)

            def fwd3(it, i, first):
                c = it * 4 + i
                pe.wait_ge(sem(f"rec_in{i}"), it * 64 + 64)
                if positive(c - 1):
                    pe.wait_ge(sem("ks_ready"), c - 1)
                for k in range(KC):
                    for h in range(2):
                        t = pe.matmul(bank(2 * (i % 2))[h * D:(h + 1) * D, k * P:(k + 1) * P],
                                      RT[:, i, k * 2 + h, C_SRC:C_SRC + 1].broadcast_to([P, D]), ident[:, :],
                                      start=True, stop=True)
                t.then_inc(sem("kr"), 1)
                if positive(c - 1):
                    pe.wait_ge(sem("l3r"), c - 1)
                for k in range(KC):
                    t = pe.transpose(bank(1 + 5 * (i % 2))[:, k * P:(k + 1) * P], G[:, i, k * P:(k + 1) * P], ident[:, :])
                t.then_inc(sem("fwd3"), 1)

            def back3(i, c):
                pe.wait_ge(sem("scanned"), c + N3 + 1)
                pe.wait_ge(sem("r_ready"), c + N3 - NCH - 1)
                for k in range(KC):
                    t = pe.transpose(bank(3 + i % 2)[:, k * P:(k + 1) * P], S[:, i % 2, k * P:(k + 1) * P], ident[:, :])
                t.then_inc(sem("back"), 1)

            def step3(it, i, first):
                fwd3(it, i, first)
                if not (first and i == 0):
                    back3((i - 1) % 4, it * 4 + i - 1)
            for i in range(4):
                step3(0, i, True)
            with pe.Fori(1, NIT) as it:
                for i in range(4):
                    step3(it, i, False)
            back3(3, NCH - 1)

            project(2 * D, finalw[:, :], QB)

            def total(col, n):
                pe.wait_ge(sem("part_sum"), n)
                pe.matmul(bank(4)[:, 0:1], ones[:, :], st[:, col:col + 1], start=True, stop=True).then_inc(sem("total"), 1)
            with pe.Fori(0, LAYERS) as l:
                pe.wait_ge(sem("wl_in"), l * 32 + 32)
                pe.sem_inc(sem("pe_turns"), 1)
                pe.wait_ge(sem("h_ready"), l + 1)
                pe.sem_inc(sem("pe_turns"), 1)
                project_pairs(UC + l * NG2, wl)
                gather_pass(N4 + l * NCH, "gath_b", l * NIT, l * NIT)
                total(0, l * 2 + 1)
                total(1, l * 2 + 2)
            pe.wait_ge(sem("hn_ready"), 2)
            project_pairs(UD, w3)
            project(D + 2, w4c[:, :], QE)

            K3 = 3 * AD + 1

            def mlp(g, i):
                if i == 0:
                    pe.wait_ge(sem("z3_ready"), g + 1)
                    for k in range(GT):
                        t = pe.transpose(PS[0:K3, 4 * 512 + k * P:4 * 512 + (k + 1) * P], Z[:, 0, k * K3:(k + 1) * K3], ident[:, :])
                    t.then_inc(sem("z3t"), 1)
                if i == 1:
                    pe.wait_ge(sem("z3ts_ready"), g + 1)
                    for m in range(2):
                        t = pe.matmul(bank(6 + m)[:, 0:GW], l3w1[:, :], Z3Ts[0:K3, m * GW:(m + 1) * GW], start=True, stop=True)
                    t.then_inc(sem("h3"), 1)
                if i == 2:
                    pe.wait_ge(sem("hs_ready"), g + 1)
                    for k in range(GT):
                        t = pe.matmul(bank(4)[:, k * D:(k + 1) * D], HS[:, k * P:(k + 1) * P], l3w2[:, :], start=True, stop=True)
                    t.then_inc(sem("o3"), 1)

            gather_pass(N8, "gath_c", 0, beside=mlp)

        @block.scalar
        def _(act):
            def rcopy(it, i, n, outs):
                act.wait_ge(sem("back"), n + 1)
                if positive(outs):
                    act.wait_ge(sem(f"runs_out{i}"), outs)
                act.copy(R[:, i, :], bank(2 + i % 2)).then_inc(sem("r_ready"), 1)

            def project(K, n0):
                def step(n):
                    act.wait_ge(sem("zt"), n + 1)
                    if positive(n):
                        act.wait_ge(sem("zo"), n)
                    act.copy(ZTs[0:K, :], PS[0:K, 0:GT * P]).then_inc(sem("zts_ready"), 1)
                if isinstance(n0, int) and n0 == 0:
                    step(0)
                    with act.Fori(1, NG) as g:
                        step(g)
                else:
                    with act.Fori(0, NG) as g:
                        step(g + n0)

            def pairs_in(n0):
                for s in range(NG2):
                    act.wait_ge(sem("pair_t"), n0 + s + 1)
                    if s >= 2:
                        act.wait_ge(sem("pair_out"), n0 + s - 1)
                    b = s % 2 * 4 * 512
                    act.activation(ZP[s % 2], PS[:, b:b + GT * P], ACT.Relu, scale=pcols[:, 0:1], bias=pcols[:, 1:2])\
                       .then_inc(sem("pair_in"), 1)

            def attr_pen(d):
                act.wait_ge(sem("e_in"), d * 64 + 64)
                act.activation(E_PEN, E_MASK, ACT.Copy, scale=BIG, bias=-BIG).then_inc(sem("e_pen"), 1)

            def attr_copy(d):
                e = E_OUT.rearrange("p (k h d) -> p k h d", k=KC, h=2)
                act.wait_ge(sem("e_back"), d + 1)
                act.copy(e[:, :, :, 0:NS], bank(6).rearrange("p (k h d) -> p k h d", k=KC, h=2)[:, :, :, A0:D])
                act.copy(e[:, :, :, NS:EW], bank(7).rearrange("p (k h d) -> p k h d", k=KC, h=2)[:, :, :, A0:A0 + AD])\
                   .then_inc(sem("e_ready"), 1)

            def gather_pass(n0, outs, attr=None, beside=None):
                def step(it, i):
                    rcopy(it, i, it * 4 + (n0 + i), (it + outs) * 16)
                    if attr is not None and i == 1:
                        attr_pen(attr + it)
                    if attr is not None and i == 3:
                        attr_copy(attr + it)
                for i in range(4):
                    step(0, i)
                if beside is not None:
                    with act.Fori(1, NG + 1) as it:
                        for i in range(4):
                            step(it, i)
                            beside(it - 1, i)
                with act.Fori(1 if beside is None else NG + 1, NIT) as it:
                    for i in range(4):
                        step(it, i)

            def root(n):
                act.wait_ge(sem("root_in"), n)
                act.activation(na[:, :], nb[:, :], ACT.Sqrt).then_inc(sem("root_out"), 1)

            act.wait_ge(sem("w4_small"), 3)
            act.copy(w4c[0:2, :], bank(4)[0:2, 0:D]).then_inc(sem("w4_act"), 1)
            act.copy(rcd[:, 0, :], bank(5)[:, 0:D]).then_inc(sem("w4_act"), 1)
            act.copy(rcd[:, 1, :], bank(6)[:, 0:D]).then_inc(sem("w4_act"), 1)
            act.wait_ge(sem("w4_act"), 3)
            act.sem_inc(sem("w4_copied"), 1)
            root(1)
            pairs_in(UA)
            act.wait_ge(sem("zeroed"), 1)
            fv = fill.rearrange("(p r) d -> p (r d)", p=P)

            def zeroes(c):
                act.dma_start(fv[:, bass.ds(c * CE, 2 * CE)], zero_rows[:, 0:2 * CE]).then_inc(sem("fill_zero"), 16)

            def relu1(i, n):
                act.wait_ge(sem("fwd"), n + 1)
                if positive(n - 1):
                    act.wait_ge(sem("scanned"), n - 1)
                act.activation(L[:, i % 2, :], bank(i % 2), ACT.Relu, bias=poolb[:, 0:1]).then_inc(sem("pt_free"), 1)

            def step1(it, i, first):
                if i % 2 == 0:
                    zeroes(it * 4 + i)
                relu1(i, it * 4 + i)
                if not (first and i == 0):
                    rcopy(it, (i - 1) % 4, it * 4 + i - 1, (it if i else it - 1) * 16 if not first else 0)
            for i in range(4):
                step1(0, i, True)
            zeroes(4)
            relu1(0, 4)
            rcopy(0, 3, 3, 0)
            for i in range(1, 4):
                step1(1, i, False)
            with act.Fori(2, NIT) as it:
                for i in range(4):
                    step1(it, i, False)
            rcopy(NIT - 1, 3, NCH - 1, (NIT - 1) * 16)
            root(2)

            def payload(it, i, first):
                if not first:
                    act.wait_ge(sem(f"scattered{i}"), it * 128)
                    act.sem_inc(sem("act_turns"), 1)
                q = it * 32 + i * 8
                for k, (col, t) in enumerate(((C_DST, dstf_q[:, bass.ds(q, 8)]), (C_SRC, srcf_q[:, bass.ds(q, 8)]))):
                    act.activation(RT[:, i, :, col], t, ACT.Copy)
                act.activation(RT[:, i, :, C_WP], w_q[:, bass.ds(q, 8)], ACT.Relu)
                act.activation(RT[:, i, :, C_WN], w_q[:, bass.ds(q, 8)], ACT.Relu, scale=-1.0).then_inc(sem("pay_ready"), 1)

            def oht_copy(h, s):
                act.wait_ge(sem("oht"), h + 1)
                if positive(h - 1):
                    act.wait_ge(sem("lookups"), h - 1)
                act.copy(OHTs[0:NJ, s, :], bank(5).bitcast(BF16)[0:NJ, 0:KC * P]).then_inc(sem("oht_copied"), 1)

            def c_copy(h, k):
                n = h * KC + k
                act.wait_ge(sem("counted"), n + 1)
                act.copy(Cs[0:NJ, k % 2, :], bank(3)[0:NJ, 0:P]).then_inc(sem("c_copied"), 1)

            def messages(c, i, q0):
                for q in (q0, q0 + 1):
                    t = act.activation(RT[:, i, q, 0:D], bank(1)[:, q * D:(q + 1) * D], ACT.Identity,
                                       scale=s_q[:, bass.ds(c * 8 + q, 1)], bias=pen_q[:, bass.ds(c * 8 + q, 1)])
                if q0 == 6:
                    t.then_inc(sem("msg_ready"), 1)

            def half(c, i, x, mc, mi, last):
                h = c * 2 + x
                c_copy(h, 0)
                c_copy(h, 1)
                if not last:
                    oht_copy(h + 1, 1 - x)
                c_copy(h, 2)
                if mc is not None:
                    if x == 1:
                        act.wait_ge(sem("back2"), mc + 1)
                        act.sem_inc(sem("act_turns"), 1)
                    messages(mc, mi, 4 - 4 * x)
                c_copy(h, 3)
                if mc is not None:
                    messages(mc, mi, 6 - 4 * x)

            def step2(it, i, first, last):
                c = it * 4 + i
                half(c, i, 0, None if first and i == 0 else c - 1, (i - 1) % 4, False)
                if not (last and i == 3):
                    payload(it + (i + 1) // 4, (i + 1) % 4, first and i < 3)
                half(c, i, 1, c, i, last and i == 3)
            act.wait_ge(sem("starts_ready"), 2)
            for i in range(3):
                act.wait_ge(sem(f"runs_out{i}"), NIT * 16)
            payload(0, 0, True)
            oht_copy(0, 0)
            for i in range(4):
                step2(0, i, True, False)
            with act.Fori(1, NIT - 1) as it:
                for i in range(4):
                    step2(it, i, False, False)
            for i in range(4):
                step2(NIT - 1, i, False, True)
            messages(NCH - 1, 3, 4)
            messages(NCH - 1, 3, 6)

            def step3(it, i, first):
                c = it * 4 + i
                s = i % 2
                act.wait_ge(sem("kr"), c + 1)
                if positive(c - 1):
                    act.wait_ge(sem("mk_ready"), c - 1)
                if positive(c - 1):
                    act.wait_ge(sem("ks_carry"), c - 1)
                act.copy(KS[s][:, 1:CE + 1], bank(2 * s)).then_inc(sem("ks_ready"), 1)
                if not (first and i == 0):
                    act.wait_ge(sem("ks_ready"), c)
                    act.copy(KS[s][:, 0:1], KS[1 - s][:, CE:CE + 1]).then_inc(sem("ks_carry"), 1)
                act.wait_ge(sem("fwd3"), c + 1)
                act.wait_ge(sem("scanned"), c + N3 - 1)
                act.activation(L[:, s, :], bank(1 + 5 * s), ACT.Relu, bias=poolb[:, 0:1]).then_inc(sem("l3r"), 1)
                if not (first and i == 0):
                    out3(it, (i - 1) % 4, c - 1, first, it if i else it - 1)

            def out3(it, i, c, first, uses):
                s = i % 2
                act.wait_ge(sem("back"), c + N3 - NCH + 1)
                if first:
                    act.wait_ge(sem(f"runs_out{i}"), NIT * 16)
                else:
                    act.wait_ge(sem(f"runs_out{i}"), (uses + NIT) * 16)
                act.copy(R[:, i, :], bank(3 + s)).then_inc(sem("r_ready"), 1)
                act.wait_ge(sem("mk_ready"), c + 1)
                act.sem_inc(sem("act_turns"), 1)
                act.dma_start(same_src[:, bass.ds(c * CE, CE)], MK[s][0:P:D, :]).then_inc(sem(f"same_src{s}"), 16)
                act.wait_ge(sem("dst_ready"), c + 1)
                act.sem_inc(sem("act_turns"), 1)
                act.dma_start(dst_by_src[:, bass.ds(c * 8, 8)], IDX[:, s, :]).then_inc(sem(f"dst_out{s}"), 16)
                act.wait_ge(sem("r_ready"), c + N3 - NCH + 1)
                act.sem_inc(sem("act_turns"), 1)
                rows = runs[bass.ds(c * CE, CE), :].rearrange("(k p) d -> p k d", p=P)
                act.dma_start(rows, R[:, i, :].rearrange("p (k d) -> p k d", k=KC)).then_inc(sem(f"runs_out{i}"), 16)

            for i in range(4):
                step3(0, i, True)
            with act.Fori(1, NIT) as it:
                for i in range(4):
                    step3(it, i, False)
            out3(NIT - 1, 3, NCH - 1, False, NIT - 1)

            project(2 * D, QB)
            root(3)
            with act.Fori(0, LAYERS) as l:
                pairs_in(UC + l * NG2)
                gather_pass(N4 + l * NCH - NCH, (l + 2) * NIT, l * NIT)
                act.wait_ge(sem("dev_ready"), l + 1)
                act.activation(AG[:, :], Hn[:, :], ACT.Square, accum_out=st[:, 1:2]).then_inc(sem("sq_done"), 1)
                act.wait_ge(sem("var_ready"), l + 1)
                act.activation(st[:, 4:5], st[:, 3:4], ACT.Sqrt).then_inc(sem("std_ready"), 1)
            root(4)
            pairs_in(UD)
            project(D + 2, QE)

            K3 = 3 * AD + 1

            def mlp(g, i):
                if i == 0:
                    act.wait_ge(sem("z3t"), g + 1)
                    act.copy(Z3Ts[0:K3, :], PS[0:K3, 4 * 512:4 * 512 + GT * P]).then_inc(sem("z3ts_ready"), 1)
                if i == 1:
                    act.wait_ge(sem("h3"), g + 1)
                    act.activation(HS[:, 0:GW], bank(6)[:, 0:GW], ACT.Relu, bias=l3b1[:, 0:1])
                    act.activation(HS[:, GW:2 * GW], bank(7)[:, 0:GW], ACT.Relu, bias=l3b1[:, 0:1]).then_inc(sem("hs_ready"), 1)

            gather_pass(N8 - NCH, 6 * NIT, beside=mlp)

        @block.vector
        def _(dve):
            order = [0]

            def then(ins):
                order[0] += 1
                ins.then_inc(sem("dve_order"), 1)
                dve.wait_ge(sem("dve_order"), order[0])

            class Steps:
                def __init__(self, name, base):
                    self.sem, self.base, self.k = sem(name), base, 0

                def __call__(self, ins):
                    self.k += 1
                    ins.then_inc(self.sem, 1)
                    dve.wait_ge(self.sem, self.base + self.k)

            def f3(t):
                return t.rearrange("p (j d) -> p j d", d=D)

            for w in (poolw, w3, wl):
                dve.memset(w[:, :], 0.0)
            dve.memset(pcols[:, 1:2], 0.0)
            then(dve.memset(pcols[:, 0:1], 1.0))
            dve.sem_inc(sem("w_zero"), 1)
            dve.wait_ge(sem("iota"), 3)
            then(dve.tensor_copy(iota_f[:, :], iota_i[:, :]))
            then(dve.tensor_copy(iota_b[:, :], iota_f[:, :]))
            then(dve.tensor_copy(pidx[:, :], pidx_i[:, :]))
            then(dve.tensor_copy(nb[:, :], na[:, :].bitcast(I32)))
            then(dve.tensor_scalar(valid[:, :], nb[:, :], float(n_nodes), None, ALU.is_lt))
            dve.tensor_scalar(ident[:, :], iota_f[:, :], pidx[:, 0:1], None, ALU.is_equal)
            dve.tensor_scalar(ident_b[:, :], iota_f[:, :], pidx[:, 0:1], None, ALU.is_equal)
            dve.tensor_scalar(earlier[:, :], iota_f[:, :], pidx[:, 0:1], None, ALU.is_lt)
            dve.tensor_scalar(below[:, :], iota_f[:, :], pidx[:, 0:1], None, ALU.is_gt)
            dve.memset(ones[:, :], 1.0)
            then(dve.memset(HC[:, :, :], 0.0))
            dve.sem_inc(sem("consts"), 1)
            dve.sem_inc(sem("hist_zero"), 1)
            dve.wait_ge(sem("params"), W["params"])
            for i in range(2):
                dve.tensor_scalar(w12r[:, 2 * i:2 * i + 1], w12c[:, i:i + 1], 0.0, None, ALU.max)
                then(dve.tensor_scalar(w12r[:, 2 * i + 1:2 * i + 2], w12c[:, i:i + 1], -1.0, 0.0, ALU.mult, ALU.max))
            dve.sem_inc(sem("w12_ready"), 1)
            dve.tensor_tensor(MD, DX[:, 1:TILES + 1], DX[:, 0:TILES], ALU.is_equal).then_inc(sem("md_ready"), 1)

            def norm(n):
                then(dve.tensor_reduce(nd[:, :], v3(X), AX.X, ALU.add))
                then(dve.tensor_scalar(nd[:, :], nd[:, :], 1.0 / D, None, ALU.mult))
                then(dve.tensor_tensor(v3(Hn), v3(X), bc(nd[:, :], [P, NJ, D]), ALU.subtract))
                then(dve.tensor_tensor(AG[:, :], Hn[:, :], Hn[:, :], ALU.mult))
                then(dve.tensor_reduce(nb[:, :], v3(AG), AX.X, ALU.add))
                dve.tensor_scalar(nb[:, :], nb[:, :], 1.0 / D, EPS, ALU.mult, ALU.add).then_inc(sem("root_in"), 1)
                dve.wait_ge(sem("root_out"), n)
                then(dve.reciprocal(nd[:, :], na[:, :]))
                then(dve.scalar_tensor_tensor(v3(Hn), v3(Hn), 0.0, bc(nd[:, :], [P, NJ, D]), ALU.max, ALU.mult))
            norm(1)
            dve.sem_inc(sem("hn_ready"), 1)
            dve.tensor_scalar(vpos[:, :], vin[:, :], 0.0, None, ALU.max)
            then(dve.tensor_scalar(vneg[:, :], vin[:, :], -1.0, 0.0, ALU.mult, ALU.max))
            dve.wait_ge(sem("same_dst"), 16)

            def project(n0, make, post):
                def produce(g, s):
                    n = g + n0
                    if positive(n - 1):
                        dve.wait_ge(sem("zt"), n - 1)
                    make(g, s).then_inc(sem("z_ready"), 1)

                def consume(g):
                    n = g + n0
                    dve.wait_ge(sem("zo"), n + 1)
                    post(g).then_inc(sem("zo_used"), 1)
                produce(0, 0)
                produce(1, 1)
                consume(0)
                produce(2, 0)
                consume(1)
                produce(3, 1)
                with dve.Fori(2, NG // 2) as g:
                    consume(g * 2 - 2)
                    produce(g * 2, 0)
                    consume(g * 2 - 1)
                    produce(g * 2 + 1, 1)
                consume(NG - 2)
                consume(NG - 1)
                dve.wait_ge(sem("zo_used"), n0 + NG)
                dve.sem_inc(sem("dve_turns"), 1)

            def z3(s, K):
                return Z[:, s, 0:GT * K].rearrange("p (j d) -> p j d", d=K)

            zo = f3(bank(2)[:, 0:GW])
            def pairs_out(n0, post):
                for s in range(NG2):
                    dve.wait_ge(sem("pair_out"), n0 + s + 1)
                    b = (s % 2 * 4 + 2) * 512
                    post(s, slice(s * GW2, (s + 1) * GW2), PS[:, b:b + GT * P]).then_inc(sem("pair_used"), 1)
                dve.wait_ge(sem("pair_used"), n0 + NG2)
                dve.sem_inc(sem("dve_turns"), 1)
            pairs_out(UA, lambda s, cols, o: dve.tensor_scalar(T[:, cols], o, 1.0, None, ALU.mult))
            dve.memset(Z[:, :, :], 0.0).then_inc(sem("zeroed"), 1)
            then(dve.memset(KEYS, 0.0))
            for i, t in enumerate((SI, DI)):
                then(dve.tensor_scalar(tmp_i, t, 7, None, ALU.logical_shift_right))
                then(dve.tensor_copy(KEYS[:, 2 * i, 0:TILES], tmp_i))
                then(dve.tensor_scalar(tmp_i, t, 127, None, ALU.bitwise_and))
                then(dve.tensor_copy(KEYS[:, 2 * i + 1, 0:TILES], tmp_i))
            then(dve.tensor_copy(dstf_q, DI))
            dve.tensor_scalar(s_q, w_q, coef[:, 0:1], 1.0, ALU.mult, ALU.add)
            then(dve.tensor_tensor(pen_q, SI, DI, ALU.is_equal))
            then(dve.tensor_copy(srcf_q, SI))
            then(dve.tensor_scalar(pen_q, pen_q, -SELF, None, ALU.mult))

            def onehots(q, s, h, digits):
                if positive(h - 1):
                    dve.wait_ge(sem("hist_done"), h - 1)
                for d in range(digits):
                    w = P if d % 2 else NJ
                    t = dve.tensor_tensor(OH[:, s, d, :, 0:w], rowbc(iota_b[:, 0:w], KC),
                                          bc(KEYS[:, d, bass.ds(q, KC)], [P, KC, w]), ALU.is_equal)
                t.then_inc(sem("oh_ready"), 1)

            def scan(i, n, data, op0, op1, first=False, name="scanned"):
                mask = M[:, i // 2, (i % 2) * CE:(i % 2 + 1) * CE]
                init = 0.0 if first else S[:, 1 - i % 2, CE - 1:CE]
                return dve.tensor_tensor_scan(S[:, i % 2, :], mask, data, init, op0, op1)

            def masks_there(it, i, done):
                if i % 2 == 0:
                    dve.wait_ge(sem(f"masks_in{i // 2}"), (it + done) * 32 + 32)

            def pre1(it, i):
                c = it * 4 + i
                q = c * 8
                dve.wait_ge(sem(f"gath_a{i}"), it * 128 + 128)
                if positive(c - 1):
                    dve.wait_ge(sem("fwd"), c - 1)
                g = G[:, i, :].rearrange("p (q d) -> p q d", d=D)
                o = Gs[:, i % 2, :].rearrange("p (q d) -> p q d", d=D)
                dve.tensor_tensor(o, g, bc(s_q[:, bass.ds(q, 8)], [P, 8, D]), ALU.mult).then_inc(sem("g_used"), 1)
                dve.wait_ge(sem("g_used"), c + 1)
                dve.tensor_tensor(o, o, bc(pen_q[:, bass.ds(q, 8)], [P, 8, D]), ALU.add).then_inc(sem("gs_ready"), 1)

            def scan1(it, i, first):
                n = it * 4 + i
                dve.wait_ge(sem("pt_free"), n + 1)
                masks_there(it, i, 0)
                if positive(n - 1):
                    dve.wait_ge(sem("back"), n - 1)
                if positive(n):
                    dve.wait_ge(sem("scanned"), n)
                scan(i, n, L[:, i % 2, :], ALU.mult, ALU.max, first).then_inc(sem("scanned"), 1)

            def step1(it, i, first):
                c = it * 4 + i
                pre1(it, i)
                onehots(c * 8, 0, c * 2, 4)
                if not (first and i == 0):
                    scan1(it if i else it - 1, (i - 1) % 4, first and i == 1)
                onehots(c * 8 + 4, 1, c * 2 + 1, 4)
            for i in range(4):
                step1(0, i, True)
            with dve.Fori(1, NIT) as it:
                for i in range(4):
                    step1(it, i, False)
            scan1(NIT - 1, 3, False)

            dve.wait_ge(sem("hist_sum"), 2)
            then(dve.tensor_copy(HC[0:NJ, 0, :], bank(5)[0:NJ, 0:P]))
            then(dve.tensor_copy(HC[0:NJ, 1, :], bank(4)[0:NJ, 0:P]))
            for i in range(2):
                then(dve.tensor_tensor_scan(HC[0:NJ, 2 + i, :], ones[0:NJ, :], HC[0:NJ, i, :], 0.0, ALU.mult, ALU.add))
                then(dve.tensor_copy(hoff[0:NJ, i:i + 1], HC[0:NJ, 2 + i, P - 1:P]))
            dve.sem_inc(sem("row_sums"), 1)
            dve.wait_ge(sem("row_offs"), 1)
            then(dve.tensor_copy(hoff[0:NJ, :], bank(6)[0:NJ, 0:2]))
            for i in range(2):
                then(dve.tensor_tensor(HC[0:NJ, 2 + i, :], HC[0:NJ, 2 + i, :], HC[0:NJ, i, :], ALU.subtract))
                dve.tensor_scalar(HC[0:NJ, 2 + i, :], HC[0:NJ, 2 + i, :], hoff[0:NJ, i:i + 1], None, ALU.add)\
                   .then_inc(sem("starts_ready"), 1)
            dve.wait_ge(sem("starts_in"), 64)

            def row_of(dst, e, w):
                then(dve.tensor_scalar(w, e, float(H), float(-(2 * H - 1)), ALU.is_ge, ALU.mult))
                then(dve.scalar_tensor_tensor(w, e, 2.0, w, ALU.mult, ALU.add))
                return w

            for i in range(2):
                then(dve.tensor_scalar(has[i][:, :], cnt[i][:, :], 1.0, None, ALU.min))
                then(dve.tensor_tensor(na[:, :], beg[i][:, :], cnt[i][:, :], ALU.add))
                then(dve.tensor_scalar(nb[:, :], na[:, :], float(H), None, ALU.is_gt))
                then(dve.scalar_tensor_tensor(span[i][:, :], beg[i][:, :], float(H), nb[:, :], ALU.is_lt, ALU.mult))
                then(dve.tensor_scalar(na[:, :], na[:, :], -1.0, 0.0, ALU.add, ALU.max))
                row_of(None, na[:, :], nb[:, :])
                then(dve.tensor_copy(endrow[i][:, :], nb[:, :]))
            row_of(None, beg[0][:, :], nb[:, :])
            then(dve.tensor_scalar(na[:, :], has[0][:, :], float(-(1 << 22)), float(1 << 22), ALU.mult, ALU.add))
            then(dve.tensor_tensor(nb[:, :], nb[:, :], na[:, :], ALU.add))
            then(dve.tensor_copy(begrow[:, :], nb[:, :]))
            dve.sem_inc(sem("rows_ready"), 1)
            then(dve.tensor_scalar(nb[:, :], cnt[1][:, :], 1.0, None, ALU.max))
            then(dve.reciprocal(rcnt[:, :], nb[:, :]))
            then(dve.tensor_scalar(pen2[:, :], span[1][:, :], BIG, -BIG, ALU.mult, ALU.add))
            dve.tensor_scalar(nb[:, :], cnt[0][:, :], 1.0, None, ALU.add).then_inc(sem("root_in"), 1)
            dve.wait_ge(sem("root_out"), 2)
            then(dve.reciprocal(dinv[:, :], na[:, :]))

            def onehots2(h, s):
                if positive(h - 3):
                    dve.wait_ge(sem("lookups"), h - 3)
                    dve.wait_ge(sem("looked"), h - 3)
                for d in range(2):
                    w = P if d else NJ
                    t = dve.tensor_tensor(OH[:, s // 2, 2 * (s % 2) + d, :, 0:w], rowbc(iota_b[:, 0:w], KC),
                                          bc(KEYS[:, d, bass.ds(h * KC, KC)], [P, KC, w]), ALU.is_equal)
                t.then_inc(sem("oh_ready"), 1)

            def ranks(h, c, i, x):
                dve.wait_ge(sem("src_rows"), h + 1)
                if positive(c - 1):
                    dve.wait_ge(sem("pos_ready"), c - 1)
                for k in range(KC):
                    t = dve.scalar_tensor_tensor(junk_rank[:, x, k, :], bank(4 - 2 * x)[:, k * P:(k + 1) * P],
                                                 RT[:, i, x * KC + k, C_SRC:C_SRC + 1], earlier[:, :],
                                                 ALU.is_equal, ALU.mult, accum_out=inr[:, i % 2, x, k:k + 1])
                t.then_inc(sem("ranked"), 1)

            def look(h, c, i, x):
                dve.wait_ge(sem("lookups"), h + 1)
                if positive(c):
                    dve.wait_ge(sem("pos_ready"), c)
                for k in range(KC):
                    t = dve.scalar_tensor_tensor(junk_look[:, x, k, :], bank(6 + x)[:, k * P:(k + 1) * P],
                                                 1.0, OH[:, i % 2, 2 * x + 1, k, :],
                                                 ALU.mult, ALU.mult, accum_out=lku[:, x, k:k + 1])
                t.then_inc(sem("looked"), 1)

            def pos(it, i):
                c = it * 4 + i
                dve.wait_ge(sem("looked"), c * 2 + 2)
                dve.wait_ge(sem("ranked"), c * 2 + 2)
                if positive(it):
                    dve.wait_ge(sem(f"scattered{i}"), it * 128)
                dve.tensor_tensor(IDX[:, i, :], inr[:, i % 2, :, :].rearrange("p x k -> p (x k)"),
                                  lku[:, :, :].rearrange("p x k -> p (x k)"), ALU.add).then_inc(sem("pos_ready"), 1)

            def scan2(it, i, first):
                n = it * 4 + i + N2
                dve.wait_ge(sem("fwd"), n + 1)
                masks_there(it, i, NIT)
                if positive(it * 4 + i - 1):
                    dve.wait_ge(sem("back2"), it * 4 + i - 1)
                dve.wait_ge(sem("scanned"), n)
                scan(i, n, bank(0), ALU.mult, ALU.add, first).then_inc(sem("scanned"), 1)
                dve.wait_ge(sem("scanned"), n + 1)
                dve.sem_inc(sem("pt_free"), 1)

            def step2(it, i, first, last):
                c = it * 4 + i
                h = c * 2
                end = last and i == 3
                scan2(it, i, first and i == 0)
                if not (first and i == 0):
                    look(h - 1, c - 1, (i - 1) % 4, 1)
                    pos(it if i else it - 1, (i - 1) % 4)
                if not end:
                    onehots2(h + 2, (i * 2 + 2) % 4)
                ranks(h + 1, c, i, 1)
                look(h, c, i, 0)
                if not end:
                    onehots2(h + 3, (i * 2 + 3) % 4)
                    ranks(h + 2, c + 1, (i + 1) % 4, 0)
            dve.wait_ge(sem("fill_zero"), 16 * NCH // 2)
            onehots2(0, 0)
            onehots2(1, 1)
            ranks(0, 0, 0, 0)
            for i in range(4):
                step2(0, i, True, False)
            for i in range(4):
                step2(1, i, False, False)
            with dve.Fori(2, NIT - 1) as it:
                for i in range(4):
                    step2(it, i, False, False)
            for i in range(4):
                step2(NIT - 1, i, False, True)
            look(2 * NCH - 1, NCH - 1, 3, 1)
            pos(NIT - 1, 3)

            for i in range(4):
                dve.wait_ge(sem(f"scattered{i}"), NIT * 128)
            then(dve.memset(KS[0][:, 0:1], -1.0))

            def step3(it, i, first):
                c = it * 4 + i
                s = i % 2
                start = first and i == 0
                dve.wait_ge(sem("ks_ready"), c + 1)
                if positive(c):
                    dve.wait_ge(sem("ks_carry"), c)
                if not first or i >= 2:
                    dve.wait_ge(sem(f"same_src{s}"), (c - i + i // 2 * 2) * 8)
                dve.wait_ge(sem("scanned"), c + N3 - 1)
                dve.tensor_tensor(MK[s], KS[s][:, 1:CE + 1], KS[s][:, 0:CE], ALU.is_equal).then_inc(sem("mk_ready"), 1)
                dve.wait_ge(sem(f"rec_in{i}"), it * 64 + 64)
                if not first or i >= 2:
                    dve.wait_ge(sem(f"dst_out{s}"), (c - i + i // 2 * 2) * 8)
                dve.tensor_copy(IDX[:, s, :], RT[:, i, :, C_DST]).then_inc(sem("dst_ready"), 1)
                dve.wait_ge(sem("mk_ready"), c + 1)
                dve.wait_ge(sem("l3r"), c + 1)
                dve.wait_ge(sem("back"), c + N3 - NCH - 1)
                dve.wait_ge(sem("scanned"), c + N3)
                dve.tensor_tensor_scan(S[:, s, :], MK[s], L[:, s, :], 0.0 if start else S[:, 1 - s, CE - 1:CE],
                                       ALU.mult, ALU.max).then_inc(sem("scanned"), 1)
            for i in range(4):
                step3(0, i, True)
            with dve.Fori(1, NIT) as it:
                for i in range(4):
                    step3(it, i, False)

            def make_b(g, s):
                j = g * GT
                ga, gb = group(AG, g), group(T, g)
                step = Steps("l0_order", g * 6)
                cc = f3(CARG)
                if positive(g + (QB - 1)):
                    dve.wait_ge(sem("zo_used"), g + (QB - 1))
                dve.wait_ge(sem(f"ends{s}"), (g - s) * (8 * GT) + 16 * GT * (NG // 2 + 1))
                for t, i, row in ((gb, 0, CR[:, :]), (ga, 1, CR2[:, :])):
                    step(dve.tensor_tensor(cc, rowbc(row, GT), bc(span[i][:, bass.ds(j, GT)], [P, GT, D]), ALU.mult))
                    step(dve.tensor_tensor(t, t, bc(has[i][:, bass.ds(j, GT)], [P, GT, D]), ALU.mult))
                    step(dve.tensor_tensor(t, t, cc, ALU.max))
                z = z3(s, 2 * D)
                dve.tensor_scalar(z[:, :, 0:D], group(Hn, g), 1.0, None, ALU.mult)
                return dve.tensor_tensor(z[:, :, D:2 * D], ga, gb, ALU.max)

            dve.wait_ge(sem("carry"), 32)

            def post_b(g):
                cc = f3(CARG)
                step = Steps("l0_post", g * 2)
                step(dve.tensor_tensor(cc, zo, rowbc(fb[:, :], GT), ALU.add))
                step(dve.tensor_scalar(cc, cc, 0.0, None, ALU.max))
                return dve.tensor_tensor(group(X, g), group(X, g), cc, ALU.add)
            project(QB, make_b, post_b)
            dve.sem_inc(sem("carry_used"), 1)
            norm(3)
            dve.sem_inc(sem("h_ready"), 1)

            def attr_scans(d):
                dve.wait_ge(sem("e_fwd"), d + 1)
                dve.wait_ge(sem("e_kept"), d + 1)
                dve.tensor_tensor_scan(E_SUM, E_MASK, bank(5), E_KEEP[:, 0:1], ALU.mult, ALU.add).then_inc(sem("e_scanned"), 1)
                dve.wait_ge(sem("e_pen"), d + 1)
                dve.tensor_tensor_scan(E_MAX, E_PEN, bank(5), E_KEEP[:, 1:2], ALU.add, ALU.max).then_inc(sem("e_scanned"), 1)
                dve.wait_ge(sem("e_scanned"), d * 2 + 2)
                dve.tensor_copy(E_KEEP[:, 0:1], E_SUM[:, CE - 1:CE])
                dve.tensor_copy(E_KEEP[:, 1:2], E_MAX[:, CE - 1:CE]).then_inc(sem("e_kept"), 1)

            def gather_pass(n0, done, attr=None, beside=None):
                def step(it, i, first):
                    n = it * 4 + i + n0
                    dve.wait_ge(sem("fwd"), n + 1 - NCH)
                    masks_there(it, i, done)
                    dve.wait_ge(sem("back"), n - 1 - NCH)
                    dve.wait_ge(sem("scanned"), n)
                    scan(i, n, bank(i % 2), ALU.mult, ALU.add, first and i == 0).then_inc(sem("scanned"), 1)
                    dve.wait_ge(sem("scanned"), n + 1)
                    dve.sem_inc(sem("pt_free"), 1)
                    if attr is not None and i == 2:
                        attr_scans(attr + it)
                for i in range(4):
                    step(0, i, True)
                if beside is not None:
                    with dve.Fori(1, NG + 1) as it:
                        for i in range(4):
                            step(it, i, False)
                            beside(it - 1, i)
                with dve.Fori(1 if beside is None else NG + 1, NIT) as it:
                    for i in range(4):
                        step(it, i, False)

            def ends_sum(g, s, per, i, base, rest):
                j = g * GT
                ga, cc = group(AG, g), f3(CARG)
                step = Steps("ends_order", base)
                dve.wait_ge(sem(f"ends{s}"), per)
                step(dve.tensor_tensor(cc, rowbc(CR[:, :], GT), bc(span[i][:, bass.ds(j, GT)], [P, GT, D]), ALU.mult))
                step(dve.tensor_tensor(ga, ga, bc(has[i][:, bass.ds(j, GT)], [P, GT, D]), ALU.mult))
                step(dve.tensor_tensor(ga, ga, cc, ALU.add))
                rest(g, ga, step)
                return step.k

            dve.memset(E_KEEP[:, :], 0.0).then_inc(sem("e_kept"), 1)
            with dve.Fori(0, LAYERS) as l:
                pairs_out(UC + l * NG2, lambda s, cols, o: dve.tensor_tensor(
                    f3(T[:, cols]), f3(o), bc(dinv[:, s * 2 * GT:(s + 1) * 2 * GT], [P, 2 * GT, D]), ALU.mult))
                gather_pass(N4 + l * NCH, (l + 2) * NIT, l * NIT)
                dve.wait_ge(sem("layer_in"), l * LIN + LIN)
                dve.sem_inc(sem("dve_turns"), 1)
                dve.wait_ge(sem("carry"), l * 16 + 48)
                dve.sem_inc(sem("dve_turns"), 1)

                def rest(g, ga, step):
                    j = g * GT
                    step(dve.tensor_tensor(ga, ga, group(T, g), ALU.add))
                    step(dve.tensor_tensor(ga, ga, bc(dinv[:, bass.ds(j, GT)], [P, GT, D]), ALU.mult))
                    step(dve.tensor_tensor(ga, ga, rowbc(lrows[:, 0, :], GT), ALU.add))
                    step(dve.tensor_tensor(ga, ga, bc(valid[:, bass.ds(j, GT)], [P, GT, D]), ALU.mult))
                    step(dve.tensor_reduce(gsum[:, bass.ds(g, 1)], ga, AX.XY, ALU.add))
                with dve.Fori(0, NG // 2) as g:
                    per = (g + l * (NG // 2)) * (16 * GT) + 16 * GT * (NG + 1)
                    k = ends_sum(g * 2, 0, per, 0, (g + l * (NG // 2)) * 16, rest)
                    k = ends_sum(g * 2 + 1, 1, per, 0, (g + l * (NG // 2)) * 16 + 8, rest)
                    assert k == 8
                dve.sem_inc(sem("carry_used"), 1)
                step = Steps("layer_order", l * 5)
                scale = 1.0 / (n_nodes * D)
                dve.tensor_reduce(st[:, 0:1], gsum[:, :], AX.X, ALU.add).then_inc(sem("part_sum"), 1)
                dve.wait_ge(sem("total"), l * 2 + 1)
                step(dve.tensor_scalar(st[:, 2:3], bank(4)[:, 0:1], scale, None, ALU.mult))
                dve.scalar_tensor_tensor(v3(Hn), v3(AG), st[:, 2:3], bc(valid[:, :], [P, NJ, D]),
                                         ALU.subtract, ALU.mult).then_inc(sem("dev_ready"), 1)
                dve.wait_ge(sem("sq_done"), l + 1)
                dve.sem_inc(sem("part_sum"), 1)
                dve.wait_ge(sem("total"), l * 2 + 2)
                dve.tensor_scalar(st[:, 3:4], bank(4)[:, 0:1], scale, EPS, ALU.mult, ALU.add).then_inc(sem("var_ready"), 1)
                dve.wait_ge(sem("std_ready"), l + 1)
                step(dve.reciprocal(st[:, 5:6], st[:, 4:5]))
                step(dve.tensor_scalar(pcols[:, 0:1], lcols[:, 0:1], st[:, 5:6], None, ALU.mult))
                step(dve.tensor_scalar(pcols[:, 1:2], lcols[:, 1:2], 1.0, None, ALU.mult))
                step(dve.tensor_scalar(lnwr[:, :], lrows[:, 1, :], st[:, 5:6], None, ALU.mult))
                assert step.k == 5
                dve.sem_inc(sem("h_ready"), 1)
            then(dve.tensor_tensor(v3(Hn), v3(Hn), rowbc(lnwr[:, :], NJ), ALU.mult))
            then(dve.tensor_tensor(v3(Hn), v3(Hn), rowbc(lrows[:, 2, :], NJ), ALU.add))
            then(dve.scalar_tensor_tensor(X[:, :], Hn[:, :], 0.0, X[:, :], ALU.max, ALU.add))
            dve.memset(pcols[:, 1:2], 0.0)
            then(dve.memset(pcols[:, 0:1], 1.0))

            norm(4)
            dve.sem_inc(sem("hn_ready"), 1)
            pairs_out(UD, lambda s, cols, o: dve.tensor_scalar(AG[:, cols], o, 0.0, None, ALU.max))

            def make_e(g, s):
                z = z3(s, D + 2)
                j = g * GT
                dve.tensor_scalar(z[:, :, 0:1], vpos[:, bass.ds(j, GT)].unsqueeze(2), 1.0, None, ALU.mult)
                dve.tensor_scalar(z[:, :, 1:2], vneg[:, bass.ds(j, GT)].unsqueeze(2), 1.0, None, ALU.mult)
                return dve.tensor_scalar(z[:, :, 2:D + 2], group(AG, g), 1.0, None, ALU.mult)
            project(QE, make_e, lambda g: dve.tensor_scalar(group(T, g), zo, 1.0, None, ALU.mult))
            dve.sem_inc(sem("t_ready"), 1)
            then(dve.tensor_tensor(v3(Hn), bc(vin[:, :], [P, NJ, D]), rowbc(w1row[:, :], NJ), ALU.mult))
            then(dve.scalar_tensor_tensor(Hn[:, :], Hn[:, :], 0.0, AG[:, :], ALU.max, ALU.add))
            dve.sem_inc(sem("he_ready"), 1)
            dve.wait_ge(sem("table_out"), (LAYERS + 1) * TP + 16)

            dve.wait_ge(sem("carry_e"), 16)
            for s in range(2):
                dve.wait_ge(sem(f"ends_e{s}"), 16 * GT * NG // 2)
            K3 = 3 * AD + 1
            W0 = AD + 1
            carried = t1.rearrange("p (j d) -> p j d", d=NS)
            sums = t2.rearrange("p (j d) -> p j d", d=NS)
            maxima = t3.rearrange("p (j d) -> p j d", d=AD)

            def gather3(g):
                j = g * GT
                e = ends_e[:, bass.ds(j, GT), :]
                z = Z[:, 0, 0:GT * K3].rearrange("p (j d) -> p j d", d=K3)
                hs = has[1][:, bass.ds(j, GT)]
                sp_ = span[1][:, bass.ds(j, GT)]
                step = Steps("l3_order", g * 9)
                step(dve.tensor_tensor(carried, rowbc(CRE[:, 0:NS], GT), bc(sp_, [P, GT, NS]), ALU.mult))
                step(dve.tensor_tensor(sums, e[:, :, 0:NS], bc(hs, [P, GT, NS]), ALU.mult))
                step(dve.tensor_tensor(sums, sums, carried, ALU.add))
                step(dve.tensor_tensor(wsum[:, bass.ds(j, GT), :], sums[:, :, W0:W0 + 2], bc(hs, [P, GT, 2]), ALU.mult))
                dve.tensor_tensor(z[:, :, 0:AD], sums[:, :, 0:AD], bc(hs, [P, GT, AD]), ALU.mult)
                dve.tensor_tensor(z[:, :, 2 * AD:3 * AD], sums[:, :, 0:AD], bc(rcnt[:, bass.ds(j, GT)], [P, GT, AD]), ALU.mult)
                dve.tensor_scalar(z[:, :, 3 * AD:K3], bc(ucol[:, 0:1], [P, GT, 1]), 1.0, None, ALU.mult)
                step(dve.tensor_tensor(maxima, rowbc(CRE[:, NS:EW], GT), bc(pen2[:, bass.ds(j, GT)], [P, GT, AD]), ALU.add))
                step(dve.tensor_tensor(maxima, maxima, e[:, :, NS:EW], ALU.max))
                step(dve.tensor_tensor(z[:, :, AD:2 * AD], maxima, bc(hs, [P, GT, AD]), ALU.mult))
                dve.sem_inc(sem("z3_ready"), 1)
                gt, other = group(T, g), f3(LW)
                dve.tensor_tensor(gt, bc(wsum[:, bass.ds(j, GT), 0], [P, GT, D]), rowbc(rcd[:, 0, :], GT), ALU.mult)
                step(dve.tensor_tensor(other, bc(wsum[:, bass.ds(j, GT), 1], [P, GT, D]), rowbc(rcd[:, 1, :], GT), ALU.mult))
                step(dve.tensor_tensor(gt, gt, other, ALU.add))
                assert step.k == 9

            def store3(g):
                dve.wait_ge(sem("o3"), g + 1)
                dve.tensor_tensor(ends_e[:, bass.ds(g * GT, GT), 0:D], f3(bank(4)[:, 0:GW]), rowbc(b2[:, :], GT), ALU.add)\
                   .then_inc(sem("l3_done"), 1)

            def beside(g, i):
                if i == 0:
                    gather3(g)
                if i == 3:
                    store3(g)
            gather_pass(N8, 6 * NIT, beside=beside)
            dve.wait_ge(sem("l3_done"), NG)
            dve.wait_ge(sem("carry"), 16 * (LAYERS + 3))

            def rest2(g, ga, step):
                step(dve.tensor_tensor(ga, ga, group(T, g), ALU.add))
                step(dve.scalar_tensor_tensor(ga, ga, 0.0, group(Hn, g), ALU.max, ALU.add))
                step(dve.scalar_tensor_tensor(ga, ga, 0.0, group(X, g), ALU.max, ALU.add))
                step(dve.tensor_tensor(group(X, g), ga, ends_e[:, bass.ds(g * GT, GT), 0:D], ALU.add))
            base = LAYERS * NG * 8
            with dve.Fori(0, NG // 2) as g:
                per = g * (16 * GT) + 16 * GT * (3 * NG + 1)
                ends_sum(g * 2, 0, per, 1, g * 14 + base, rest2)
                ends_sum(g * 2 + 1, 1, per, 1, g * 14 + (base + 7), rest2)
                dve.sem_inc(sem("x_ready"), 1)


def ends_layer(pool, l, sem, dst, rows, idx, NG, GT):
    for g in range(NG):
        s = g % 2
        pool.wait_ge(sem(f"ends{s}"), (l * (NG // 2) + (NG + g // 2)) * (16 * GT))
        pool.sem_inc(sem("pool_turns"), 1)
        for k in range(GT):
            j = g * GT + k
            pool.indirect_dma_start(dst[:, j * D:(j + 1) * D], None, rows,
                                    bass.IndirectOffsetOnAxis(ap=idx[:, j:j + 1], axis=0)).then_inc(sem(f"ends{s}"), 16)


def kernel(**inputs):
    import numpy as np
    import concourse.bacc as bacc
    from concourse.bass_utils import run_bass_kernel_spmd as run

    i = {k: np.asarray(v) for k, v in inputs.items()}
    n, e = i["x"].shape[0], i["src"].shape[0]
    NJ, TILES = sizes(n, e)
    NP, EP = NJ * P, TILES * P

    def pad(x, rows, value=0):
        return np.concatenate([x, np.full((rows - x.shape[0],) + x.shape[1:], value, x.dtype)])

    def chunked(x):
        return np.ascontiguousarray(x.reshape(2, TILES // (2 * KC), KC, P).transpose(3, 1, 2, 0).reshape(P, TILES))

    src, dst = pad(i["src"], EP, NP - 1), pad(i["dst"], EP, NP - 1)
    w4_t = i["L2_gnn_W4"].T
    arrays = {
        "x": pad(i["x"], NP), "src_q": chunked(src), "dst_q": chunked(dst),
        "dst_ext": np.concatenate([np.full(1, -1, dst.dtype), dst])[None],
        "ew_q": chunked(pad(i["edge_weight"], EP)), "attr": pad(i["edge_attr_32"], EP),
        "v": pad(i["node_vec1"], NP), "poolw_t": i["L0_gnn_pool_w"].T, "pool_b": i["L0_gnn_pool_b"][:, None],
        "finalw_t": i["L0_gnn_final_w"].T, "final_b": i["L0_gnn_final_b"][None],
        "coef": i["L0_gnn_coef"].reshape(1, 1), "ws": pad(i["L1_gnn_Ws"].reshape(-1, D), (LAYERS + 1) * D),
        "bs": i["L1_gnn_bs"], "lnw": i["L1_gnn_ln_w"], "lnb": i["L1_gnn_ln_b"],
        "w1": i["L2_gnn_W1"], "w2": i["L2_gnn_W2"], "w3_t": i["L2_gnn_W3"].T, "w4_t": w4_t,
        "u": i["L3_gnn_u"][0:1], "l3w1": i["L3_gnn_W1"], "l3b1": i["L3_gnn_b1"][:, None],
        "l3w2": i["L3_gnn_W2"], "l3b2": i["L3_gnn_b2"][None],
    }
    arrays = {k: np.ascontiguousarray(v) for k, v in arrays.items()}
    nc = bacc.Bacc("TRN2", target_bir_lowering=False, num_devices=1)
    aps = {k: nc.dram_tensor(f"in_{k}", v.shape, mybir.dt.from_np(v.dtype), kind="ExternalInput").ap()
           for k, v in arrays.items()}
    out = nc.dram_tensor("out_x", (NP, D), F32, kind="ExternalOutput").ap()
    gnn_kernel(nc, n, e, aps, out)
    r = run(nc, [{f"in_{k}": v for k, v in arrays.items()}], core_ids=[0])
    return r.results[0]["out_x"][:n]
```
